# Optimizing a Trainium2 kernel written in Bass

```python
import numpy as np
import jax
import jax.numpy as jnp

def _softmax(x, axis=-1):
    return jax.nn.softmax(x, axis=axis)

def _gelu(x):
    return jax.nn.gelu(x, approximate=True)

def _silu(x):
    return jax.nn.silu(x)

def _sigmoid(x):
    return jax.nn.sigmoid(x)

def _layernorm(x, axis=-1, eps=1e-05):
    m = jnp.mean(x, axis=axis, keepdims=True)
    v = jnp.var(x, axis=axis, keepdims=True)
    return (x - m) / jnp.sqrt(v + eps)

def _scatter_add(tgt, idx, src, axis=0):
    return tgt.at[idx].add(src)

def _segment_sum(src, seg, n):
    return jax.ops.segment_sum(src, seg, n)
kernel_name = 'mk_decoder_preln_d1_seqx_r4_e21386'

def setup_inputs(seed: int=0):
    np.random.seed(seed)
    _w = jnp.asarray

    def _rec_inputs():
        import jax
        import jax.numpy as jnp
        _rk = jax.random.key(seed)
        x = 7.22e-05 + 1 * jax.random.normal(jax.random.fold_in(_rk, 1), (16, 256, 512), jnp.float32)
        _lenS = 256 - jax.random.randint(jax.random.fold_in(_rk, 7), (16,), 0, max(1, 256 // 4) + 1, jnp.int32)
        _lenS2 = 256 - jax.random.randint(jax.random.fold_in(_rk, 8), (16,), 0, max(1, 256 // 4) + 1, jnp.int32)
        _ctx_2048P = jax.random.normal(jax.random.fold_in(_rk, 11), (16, 16, 512), jnp.float32)
        _ctx_2048c = jax.random.dirichlet(jax.random.fold_in(_rk, 511), 0.3 * jnp.ones((16,), jnp.float32), (16, 256))
        _ctx_2048t = jnp.einsum('bsk,bkd->bsd', _ctx_2048c, _ctx_2048P)
        _ctx_2048t = _ctx_2048t * jax.lax.rsqrt(jnp.mean(jnp.square(_ctx_2048t)) + 1e-12) * 0.953939
        ctx_2048 = 4.13588e-05 + 0.999923 * (_ctx_2048t + 0.3 * jax.random.normal(jax.random.fold_in(_rk, 611), (16, 256, 512), jnp.float32))
        return (x, ctx_2048)
    x, ctx_2048 = _rec_inputs()

    def _L0_attn_setup():
        import jax, jax.numpy as jnp
        import numpy as np
        HIDDEN = 512
        NUM_HEADS = 16
        HEAD_DIM = 128
        WINDOW = 256
        ROPE_THETA = 10000.0
        B, L = (1, 1024)

        def _apply_rotary(x, cos, sin):
            d2 = x.shape[-1] // 2
            x1, x2 = (x[..., :d2], x[..., d2:])
            return jnp.concatenate([x1 * cos - x2 * sin, x2 * cos + x1 * sin], axis=-1)
        key = jax.random.key(seed)
        k0, k1, k2, k3, k4 = jax.random.split(key, 5)
        s = 1.0 / np.sqrt(HIDDEN)
        return {'hidden_states': jax.random.normal(k0, (B, L, HIDDEN), dtype=jnp.float32), 'wq': jax.random.normal(k1, (HIDDEN, NUM_HEADS * HEAD_DIM), dtype=jnp.float32) * s, 'wk': jax.random.normal(k2, (HIDDEN, NUM_HEADS * HEAD_DIM), dtype=jnp.float32) * s, 'wv': jax.random.normal(k3, (HIDDEN, NUM_HEADS * HEAD_DIM), dtype=jnp.float32) * s, 'wo': jax.random.normal(k4, (NUM_HEADS * HEAD_DIM, HIDDEN), dtype=jnp.float32) * s}
    _L0_attn_all = _L0_attn_setup()
    _L0_attn_in = {k: v for k, v in _L0_attn_all.items() if k in ('wq', 'wk', 'wv', 'wo')}
    del _L0_attn_all

    def _L0_xattn_setup():
        import jax, jax.numpy as jnp
        import numpy as np
        N_HEAD = 8
        key = jax.random.key(seed)
        k1, k2, k3 = jax.random.split(key, 3)
        B, D, L = (4, 256, 512)
        q = jax.random.normal(k1, (B, D, L), dtype=jnp.float32)
        k = jax.random.normal(k2, (B, D, L), dtype=jnp.float32)
        v = jax.random.normal(k3, (B, D, L), dtype=jnp.float32)
        gamma = jnp.ones((), dtype=jnp.float32)
        return {'q': q, 'k': k, 'v': v, 'gamma': gamma}
    _L0_xattn_all = _L0_xattn_setup()
    _L0_xattn_in = {k: v for k, v in _L0_xattn_all.items() if k in ('gamma',)}
    del _L0_xattn_all

    def _L0_ffn_setup():
        import jax, jax.numpy as jnp
        import numpy as np
        NUM_EXPERTS = 16
        C = 1.0
        key = jax.random.key(seed)
        k1, k2, k3 = jax.random.split(key, 3)
        b, s, h = (4, 512, 512)
        return {'x': jax.random.normal(k1, (b, s, h), dtype=jnp.float32), 'router_w': jax.random.normal(k2, (h, NUM_EXPERTS), dtype=jnp.float32) * 0.02, 'router_b': jnp.zeros((NUM_EXPERTS,), dtype=jnp.float32), 'expert_w': jax.random.normal(k3, (h, h), dtype=jnp.float32) * 0.02, 'expert_b': jnp.zeros((h,), dtype=jnp.float32)}
    _L0_ffn_all = _L0_ffn_setup()
    _L0_ffn_in = {k: v for k, v in _L0_ffn_all.items() if k in ('router_w', 'router_b', 'expert_w', 'expert_b')}
    del _L0_ffn_all
    return {'x': x, 'ctx_2048': ctx_2048, 'L0_attn_wq': _L0_attn_in['wq'], 'L0_attn_wk': _L0_attn_in['wk'], 'L0_attn_wv': _L0_attn_in['wv'], 'L0_attn_wo': _L0_attn_in['wo'], 'L0_xattn_gamma': _L0_xattn_in['gamma'], 'L0_ffn_router_w': _L0_ffn_in['router_w'], 'L0_ffn_router_b': _L0_ffn_in['router_b'], 'L0_ffn_expert_w': _L0_ffn_in['expert_w'], 'L0_ffn_expert_b': _L0_ffn_in['expert_b']}

def reference(x, ctx_2048, L0_attn_wq, L0_attn_wk, L0_attn_wv, L0_attn_wo, L0_xattn_gamma, L0_ffn_router_w, L0_ffn_router_b, L0_ffn_expert_w, L0_ffn_expert_b):
    import jax
    import jax.numpy as jnp

    def _L0_attn_ref(hidden_states, wq, wk, wv, wo):
        import jax, jax.numpy as jnp
        import numpy as np
        HIDDEN = 512
        NUM_HEADS = 16
        HEAD_DIM = 128
        WINDOW = 256
        ROPE_THETA = 10000.0
        B, L = (1, 1024)

        def _apply_rotary(x, cos, sin):
            d2 = x.shape[-1] // 2
            x1, x2 = (x[..., :d2], x[..., d2:])
            return jnp.concatenate([x1 * cos - x2 * sin, x2 * cos + x1 * sin], axis=-1)
        Bsz, Ln, _ = hidden_states.shape
        dtype = hidden_states.dtype
        scale = HEAD_DIM ** (-0.5)

        def split_heads(x):
            return x.reshape(Bsz, Ln, NUM_HEADS, HEAD_DIM).transpose(0, 2, 1, 3)
        q = split_heads(hidden_states @ wq)
        k = split_heads(hidden_states @ wk)
        v = split_heads(hidden_states @ wv)
        inv_freq = 1.0 / ROPE_THETA ** (jnp.arange(0, HEAD_DIM, 2, dtype=jnp.float32) / HEAD_DIM)
        pos = jnp.arange(Ln, dtype=jnp.float32)
        freqs = pos[:, None] * inv_freq[None, :]
        cos = jnp.cos(freqs).astype(dtype)
        sin = jnp.sin(freqs).astype(dtype)
        q = _apply_rotary(q, cos, sin)
        k = _apply_rotary(k, cos, sin)
        q_pos = jnp.arange(Ln)[:, None]
        k_pos = jnp.arange(Ln)[None, :]
        valid = (k_pos > q_pos - WINDOW) & (k_pos <= q_pos)
        neg = jnp.finfo(dtype).min
        attn = jnp.einsum('bhqd,bhkd->bhqk', q, k) * scale
        attn = jnp.where(valid, attn, neg)
        attn = jax.nn.softmax(attn, axis=-1)
        out = jnp.einsum('bhqk,bhkd->bhqd', attn, v)
        out = out.transpose(0, 2, 1, 3).reshape(Bsz, Ln, NUM_HEADS * HEAD_DIM)
        return out @ wo

    def _L0_xattn_ref(q, k, v, gamma):
        import jax, jax.numpy as jnp
        import numpy as np
        N_HEAD = 8
        B, Dq, Lq = q.shape
        Dv, Lk = (v.shape[-2], v.shape[-1])
        h = N_HEAD
        dq = Dq // h
        dv = Dv // h
        qh = q.reshape(B, h, dq, Lq)
        kh = k.reshape(B, h, dq, Lk)
        vh = v.reshape(B, h, dv, Lk)
        scale = 1.0 / jnp.sqrt(jnp.asarray(dq, dtype=q.dtype))
        qk = jnp.einsum('bhdq,bhdl->bhql', qh, kh) * scale
        sm = jax.nn.softmax(qk, axis=-1)
        ret = jnp.einsum('bhql,bhdl->bhdq', sm, vh)
        ret = ret.reshape(B, Dv, Lq)
        return gamma * ret

    def _L0_ffn_ref(x, router_w, router_b, expert_w, expert_b):
        import jax, jax.numpy as jnp
        import numpy as np
        NUM_EXPERTS = 16
        C = 1.0
        b, s, h = x.shape
        bs = b * s
        k = min(int(bs * C / NUM_EXPERTS), bs)
        xf = x.reshape(bs, h)
        logits = xf @ router_w + router_b
        S = jax.nn.softmax(logits, axis=-1)
        G, idx = jax.lax.top_k(S.T, k)
        tokens = xf[idx]
        out = jnp.einsum('ekh,hd->ekd', tokens, expert_w) + expert_b
        weighted = G[..., None] * out
        y = jnp.zeros((bs, h), dtype=x.dtype).at[idx.reshape(-1)].add(weighted.reshape(-1, h))
        return y.reshape(b, s, h)
    x = x + _L0_attn_ref(_layernorm(x, axis=-1), L0_attn_wq, L0_attn_wk, L0_attn_wv, L0_attn_wo)
    x = x + _L0_xattn_ref(_layernorm(x, axis=-1), ctx_2048, ctx_2048, L0_xattn_gamma)
    x = x + _L0_ffn_ref(_layernorm(x, axis=-1), L0_ffn_router_w, L0_ffn_router_b, L0_ffn_expert_w, L0_ffn_expert_b)
    return x

_drawn_inputs = setup_inputs


def setup_inputs(seed=0):
    import zlib

    import numpy as np

    out = dict(_drawn_inputs(seed))
    spreads = {'L0_ffn_router_b': (0.0, 0.8), 'L0_ffn_expert_b': (0.0, 0.68)}
    factors = {}
    for name, (base, spread) in spreads.items():
        noise = np.random.default_rng([zlib.crc32(name.encode()), seed]).standard_normal(out[name].shape)
        drawn = base * np.exp(spread * noise) if base else spread * noise
        out[name] = jnp.asarray(drawn.astype(out[name].dtype))
    for name, factor in factors.items():
        out[name] = (out[name] * factor).astype(out[name].dtype)
    return out
```

```python
import concourse.bass as bass
from concourse import mybir
from contextlib import ExitStack
import numpy as np

F32 = mybir.dt.float32
F32R = mybir.dt.float32r
BF16 = mybir.dt.bfloat16
I32 = mybir.dt.int32
ALU = mybir.AluOpType
ACT = mybir.ActivationFunctionType
AX = mybir.AxisListType

P = 128
B, L, D = 16, 256, 512
TILES = B * L // P
TB = L // P
CB = D // P
H, HD = 16, 128
HG = 4
G = H // HG
GW = HG * HD
NCH = 3 * CB + HG
KBLK = 3
XH, XD = 8, 32
XPT = P // XD
E = 16
TOPK = B * L // E
EPS = 1e-5
MASKED = -3.0e38
SCALE = HD ** -0.5
XSCALE = XD ** -0.5
CH_Q, CH_K, CH_V, CH_O = 0, CB, 2 * CB, 3 * CB


def turns(eng, count, body):
    body(0)
    with eng.Fori(1, count) as i:
        body(i)


def rstd_of_all(nc, act, dve, mv, rstd, tmp, s_in, n_in, s_sqrt, s_step, final_scale):
    if act is not None:
        act.wait_ge(s_in, n_in)
        nc.scalar.activation(tmp[:, 1, :], tmp[:, 0, :], ACT.Sqrt).then_inc(s_sqrt, 1)
    if dve is not None:
        steps = [0]

        def step(ins):
            steps[0] += 1
            ins.then_inc(s_step, 1)
            dve.wait_ge(s_step, steps[0])

        dve.wait_ge(s_sqrt, 1)
        step(nc.vector.reciprocal(rstd, tmp[:, 1, :]))
        step(nc.vector.tensor_tensor(tmp[:, 1, :], rstd, rstd, ALU.mult))
        step(nc.vector.tensor_tensor(tmp[:, 1, :], tmp[:, 1, :], tmp[:, 0, :], ALU.mult))
        step(nc.vector.tensor_scalar(tmp[:, 1, :], tmp[:, 1, :], -0.5 * final_scale, 1.5 * final_scale,
                                     ALU.mult, ALU.add))
        step(nc.vector.tensor_tensor(rstd, rstd, tmp[:, 1, :], ALU.mult))


def layer_norm_1(nc, x, xt, cst):
    ident = cst["ident"]
    ctx = ExitStack()
    with ctx:
        def sb(name, shape, dt):
            return ctx.enter_context(nc.sbuf_tensor(name, shape, dt))

        def sem(name):
            return ctx.enter_context(nc.semaphore(name))

        x_all = sb("x_all", [P, TILES, D], F32)
        bn = sb("bn1", [P, TILES, 6], F32)
        mv = sb("mv1", [P, TILES, 2], F32)
        tmp = sb("rs_tmp1", [P, 2, TILES], F32)
        rstd = sb("rstd1", [P, TILES], F32)
        xn = sb("xn1", [P, 2, D], F32)
        parts = sb("parts1", [P, 2, 2, CB, P], F32R)
        ps = [ctx.enter_context(nc.psum_tensor(f"n1ps{i}", [P, CB * P], F32)) for i in range(2)]

        s_x = [sem(f"n1_x{i}") for i in range(4)]
        s_const = sem("n1_const")
        s_bn, s_mv, s_var = sem("n1_bn"), sem("n1_mv"), sem("n1_var")
        s_sqrt, s_step = sem("n1_sqrt"), sem("n1_step")
        s_xn, s_tr, s_hi, s_lo = sem("n1_xn"), sem("n1_tr"), sem("n1_hi"), sem("n1_lo")
        s_out = [sem(f"n1_out{i}") for i in range(2)]
        xv = x.rearrange("b (t p) d -> p (b t) d", p=P)
        block = ctx.enter_context(nc.Block())
        per = TILES // 4

        @block.sync
        def _(sp):
            for i in range(4):
                sp.dma_start(x_all[:, i * per:(i + 1) * per, :], xv[:, i * per:(i + 1) * per, :]).then_inc(s_x[i], 16)
            def turn(b):
                for t in range(TB):
                    sp.wait_ge(s_lo, 2 * b + t + 1)
                    sp.dma_start(xt[bass.ds(b, 1), :, :, :, t * P:(t + 1) * P].rearrange("o p h c n -> (o p) h c n"),
                                 parts[:, t, :, :, :].bitcast(F32)).then_inc(s_out[t], 16)

            turns(sp, B, turn)
            for t in range(TB):
                sp.wait_ge(s_out[t], 16 * B)

        @block.gpsimd
        def _(pool):
            nc.gpsimd.memset(ident[:, :], 0.0).then_inc(s_const, 1)
            nc.gpsimd.memset(cst["identb"][:, :], 0.0).then_inc(s_const, 1)
            nc.gpsimd.memset(cst["mask"][:, :], 0.0).then_inc(s_const, 1)
            nc.gpsimd.memset(cst["ones"][:, :], 1.0).then_inc(s_const, 1)
            nc.gpsimd.memset(cst["tri"][:, :], 1.0).then_inc(s_const, 1)
            pool.wait_ge(s_const, 5)
            for m in (ident, cst["identb"]):
                nc.gpsimd.affine_select(out=m[:, :], in_=m[:, :], compare_op=ALU.not_equal, fill=1.0, base=0,
                                        pattern=[[-1, P]], channel_multiplier=1).then_inc(s_const, 1)
            nc.gpsimd.affine_select(out=cst["mask"][:, :], in_=cst["mask"][:, :], compare_op=ALU.is_ge, fill=MASKED,
                                    base=0, pattern=[[-1, P]], channel_multiplier=1).then_inc(s_const, 1)
            nc.gpsimd.affine_select(out=cst["tri"][:, :], in_=cst["tri"][:, :], compare_op=ALU.is_ge, fill=0.0,
                                    base=0, pattern=[[1, P]], channel_multiplier=-1).then_inc(s_const, 1)

        @block.vector
        def _(dve):
            for i in range(4):
                dve.wait_ge(s_x[i], 16)
                for t in range(i * per, (i + 1) * per):
                    nc.vector.bn_stats(bn[:, t, :], x_all[:, t, :]).then_inc(s_bn, 1)
            dve.wait_ge(s_bn, TILES)
            for t in range(TILES):
                nc.vector.bn_aggr(mv[:, t, :], bn[:, t, :]).then_inc(s_mv, 1)
            dve.wait_ge(s_mv, TILES)
            nc.vector.tensor_scalar(tmp[:, 0, :], mv[:, :, 1], EPS, None, ALU.add).then_inc(s_var, 1)
            rstd_of_all(nc, None, dve, mv, rstd[:, :], tmp, s_var, 1, s_sqrt, s_step, 1.0)
            def turn(b):
                for t in range(TB):
                    n = 2 * b + t
                    dve.wait_ge(s_tr, 2 * b)
                    nc.vector.tensor_scalar(xn[:, t, :], x_all[:, bass.ds(n, 1), :].rearrange("p o d -> p (o d)"),
                                            mv[:, bass.ds(n, 1), 0], rstd[:, bass.ds(n, 1)],
                                            ALU.subtract, ALU.mult).then_inc(s_xn, 1)
                for t in range(TB):
                    n = 2 * b + t
                    dve.wait_ge(s_hi, n + 1)
                    nc.vector.tensor_tensor(parts[:, t, 1, :, :].rearrange("p c n -> p (c n)"), ps[t][:, :],
                                            parts[:, t, 0, :, :].rearrange("p c n -> p (c n)").bitcast(F32),
                                            ALU.subtract).then_inc(s_lo, 1)

            turns(dve, B, turn)

        @block.scalar
        def _(act):
            rstd_of_all(nc, act, None, mv, rstd, tmp, s_var, 1, s_sqrt, s_step, 1.0)
            def turn(b):
                for t in range(TB):
                    act.wait_ge(s_tr, 2 * b + t + 1)
                    act.wait_ge(s_out[t], 16 * b)
                    nc.scalar.activation(parts[:, t, 0, :, :].rearrange("p c n -> p (c n)"), ps[t][:, :],
                                         ACT.Copy).then_inc(s_hi, 1)

            turns(act, B, turn)

        @block.tensor
        def _(pe):
            pe.wait_ge(s_const, 9)
            def turn(b):
                for t in range(TB):
                    pe.wait_ge(s_xn, 2 * b + t + 1)
                    pe.wait_ge(s_lo, 2 * b)
                    for c in range(CB):
                        last = nc.tensor.transpose(ps[t][:, c * P:(c + 1) * P], xn[:, t, c * P:(c + 1) * P], ident[:, :])
                    last.then_inc(s_tr, 1)

            turns(pe, B, turn)


def self_attention(nc, x, w_all, rope, xt, x1, mv2, cst):
    ident, identb, mask = cst["ident"], cst["identb"], cst["mask"]
    ctx = ExitStack()
    with ctx:
        def sb(name, shape, dt):
            return ctx.enter_context(nc.sbuf_tensor(name, shape, dt))

        def pb(name):
            return ctx.enter_context(nc.psum_tensor(name, [P, 512], F32))

        def sem(name):
            return ctx.enter_context(nc.semaphore(name))

        whi = [sb(f"whi{i}", [P, NCH, 512], F32R) for i in range(2)]
        wlo = [sb(f"wlo{i}", [P, NCH, 512], F32R) for i in range(2)]
        raw = sb("wraw", [P, 2, 512], F32)
        xnt = [sb(f"xnt{i}", [P, 2, CB, L], F32R) for i in range(2)]
        rot = [sb(f"rot{i}", [P, TB, GW], F32) for i in range(2)]
        swp = sb("swp", [P, 2, GW], F32)
        v_sb = [sb(f"v{i}", [P, TB, GW], F32) for i in range(2)]
        qkt = [sb(f"qkt{i}", [P, HG, L], F32) for i in range(2)]
        pr = sb("pr", [P, HG, KBLK * P], F32)
        prt = sb("prt", [P, HG, KBLK * P], F32)
        ohi = sb("ohi", [P, HG, L], F32R)
        olo = sb("olo", [P, HG, L], F32R)
        xio = sb("xio", [P, 2, TB, D], F32)
        trig = sb("trig", [P, TB, 3, HD // 2], F32)
        mx = sb("mx", [P, HG, TB], F32)
        nmx = sb("nmx", [P, HG, TB], F32)
        rsum = sb("rsum", [P, HG, TB], F32)
        rinv = sb("rinv", [P, HG, TB], F32)
        bn = sb("bn2", [P, TB, 6], F32)
        agg = sb("agg2", [P, TB, 2], F32)
        hold = sb("hold2", [P, 1], F32)

        PJ = [pb("pj0"), pb("pj1")]
        TR = [pb("tr0"), pb("tr1")]
        SC = [pb("sc0"), pb("sc1")]
        OB = [pb("ob0"), pb("ob1")]

        s_trig = sem("a_trig")
        s_xn = [sem(f"a_xn{i}") for i in range(2)]
        s_raw = [sem(f"a_raw{i}") for i in range(2)]
        s_xi = [sem(f"a_xi{i}") for i in range(2)]
        s_xo = [sem(f"a_xo{i}") for i in range(2)]
        s_whi, s_wlo = sem("a_whi"), sem("a_wlo")
        s_proj = sem("a_proj")
        s_mul = sem("a_mul")
        s_swp = sem("a_swp")
        s_vev = sem("a_vev")
        s_qkt = sem("a_qkt")
        s_qke = sem("a_qke")
        s_sc = sem("a_sc")
        s_mx, s_nmx = sem("a_mx"), sem("a_nmx")
        s_exp = sem("a_exp")
        s_ri, s_pr = sem("a_ri"), sem("a_pr")
        s_pt = sem("a_pt")
        s_pte = sem("a_pte")
        s_pv = sem("a_pv")
        s_ohi, s_olo = sem("a_ohi"), sem("a_olo")
        s_wo = sem("a_wo")
        s_x1 = [sem(f"a_x1{i}") for i in range(TB)]
        s_bn, s_mv = sem("a_bn"), sem("a_mv")
        block = ctx.enter_context(nc.Block())

        xv = x.rearrange("b (t p) d -> b p t d", p=P)
        ITEMS = G * B

        def items(eng, item, ahead=True):
            for g in range(G):
                if g == 0:
                    item(0, 0, 0, 0, 0, True)
                    item(1, 0, 1, 1, 0, True)
                with eng.Fori(1 if g == 0 else 0, B // 2 - 1) as j:
                    for par in range(2):
                        item(2 * j + (g * B + par), g, 2 * j + par, par, g, True)
                item(g * B + B - 2, g, B - 2, 0, g, True)
                item(g * B + B - 1, g, B - 1, 1, g + 1, g + 1 < G)

        def one(ap, i):
            return ap[bass.ds(i, 1)].rearrange("o p a d -> (o p) a d") if not isinstance(i, int) else ap[i]

        @block.sync
        def _(sp):
            sp.dma_start(trig[:, :, :, :], rope).then_inc(s_trig, 16)
            for m in range(2):
                sp.dma_start(xnt[m][:, :, :, :].bitcast(F32), xt[m]).then_inc(s_xn[m], 16)
            for c in range(NCH):
                if c >= 2:
                    sp.wait_ge(s_wlo, c - 1)
                sp.dma_start(raw[:, c % 2, :], w_all[0, c]).then_inc(s_raw[c % 2], 16)

            def item(n, g, b, par, gn, more):
                half = (n - par) // 2 if isinstance(n, int) else None
                stored = 16 * half if half is not None else 8 * (n - par)
                sp.wait_ge(s_xo[par], stored)
                src = (xv if g == 0 else x1)
                src = src[b] if isinstance(b, int) else src[bass.ds(b, 1)].rearrange("o p t d -> (o p) t d")
                sp.dma_start(xio[:, par, :, :], src).then_inc(s_xi[par], 16)
                if g + 1 < G:
                    sp.wait_ge(s_wlo, n + (NCH - 1))
                    wsrc = w_all[g + 1, b] if isinstance(b, int) else w_all[g + 1, bass.ds(b, 1)].rearrange("o p d -> (o p) d")
                    sp.dma_start(raw[:, par, :], wsrc).then_inc(s_raw[par], 16)
                if isinstance(b, int):
                    b2, there = (b + 2) % B, g + (b + 2) // B < G
                else:
                    b2, there = b + 2, True
                if there:
                    sp.wait_ge(s_proj, 6 * n + 6)
                    xsrc = xt[b2] if isinstance(b2, int) else xt[bass.ds(b2, 1)].rearrange("o p h c n -> (o p) h c n")
                    sp.dma_start(xnt[par][:, :, :, :].bitcast(F32), xsrc).then_inc(s_xn[par], 16)
                for t in range(TB):
                    sp.wait_ge(s_x1[t], n + 1)
                dst = x1[b] if isinstance(b, int) else x1[bass.ds(b, 1)].rearrange("o p t d -> (o p) t d")
                sp.dma_start(dst, xio[:, par, :, :]).then_inc(s_xo[par], 16)

            items(sp, item)
            for par in range(2):
                sp.wait_ge(s_xo[par], 16 * ITEMS // 2)

        @block.gpsimd
        def _(pool):
            def rotate(m):
                for i in range(4):
                    pool.wait_ge(s_mul, 4 * m + i + 1)
                    r = rot[i // 2][:, i % 2, :]
                    nc.gpsimd.tensor_tensor(r, r, swp[:, i % 2, :], ALU.add).then_inc(s_swp, 1)

            rotate(0)
            items(pool, lambda n, g, b, par, gn, more: rotate(n + 1) if more else None)

        @block.tensor
        def _(pe):
            def project(bank, m, gn, par, kind, t):
                k = 0
                for c in range(CB):
                    tok = slice(t * P, (t + 1) * P)
                    for xpart, w in ((0, whi), (0, wlo), (1, whi)):
                        last = nc.tensor.matmul(bank[:, :], xnt[par][:, xpart, c, tok], w[gn % 2][:, kind + c, :],
                                                start=(k == 0), stop=(k == 3 * CB - 1))
                        k += 1
                last.then_inc(s_proj, 1)

            def xn_here(m, par):
                if isinstance(m, int):
                    pe.wait_ge(s_xn[par], 16 * (m // 2 + 1))
                else:
                    pe.wait_ge(s_xn[par], 8 * (m - par) + 16)

            pe.wait_ge(s_whi, 3 * CB)
            pe.wait_ge(s_wlo, 3 * CB)
            xn_here(0, 0)
            project(PJ[0], 0, 0, 0, CH_Q, 0)
            project(PJ[1], 0, 0, 0, CH_Q, 1)
            pe.wait_ge(s_mul, 1)
            project(PJ[0], 0, 0, 0, CH_K, 0)
            pe.wait_ge(s_mul, 2)
            project(PJ[1], 0, 0, 0, CH_K, 1)
            pe.wait_ge(s_mul, 3)
            project(PJ[0], 0, 0, 0, CH_V, 0)
            pe.wait_ge(s_mul, 4)
            project(PJ[1], 0, 0, 0, CH_V, 1)

            def item(n, g, b, par, gn, more):
                m, mp = n + 1, 1 - par

                def transposes(i):
                    src, h0 = rot[i % 2], 2 * (i // 2)
                    for h in range(2):
                        for t in range(TB):
                            last = nc.tensor.transpose(TR[i % 2][:, (h * TB + t) * P:(h * TB + t + 1) * P],
                                                       src[:, t, (h0 + h) * HD:(h0 + h + 1) * HD], ident[:, :])
                    last.then_inc(s_qkt, 1)

                def scores(h):
                    bank = SC[h % 2]
                    qT, kT = qkt[0][:, h, :], qkt[1][:, h, :]
                    nc.tensor.matmul(bank[:, 0:P], qT[:, 0:P], kT[:, 0:P], start=True, stop=False)
                    nc.tensor.matmul(bank[:, 0:P], identb[:, :], mask[:, :], start=False, stop=True)
                    nc.tensor.matmul(bank[:, P:3 * P], qT[:, P:2 * P], kT[:, 0:2 * P], start=True, stop=False)
                    nc.tensor.matmul(bank[:, 2 * P:3 * P], identb[:, :], mask[:, :], start=False,
                                     stop=True).then_inc(s_sc, 1)

                def prob_transposes(h):
                    for k in range(KBLK):
                        last = nc.tensor.transpose(TR[h % 2][:, k * P:(k + 1) * P], pr[:, h, k * P:(k + 1) * P],
                                                   ident[:, :])
                    last.then_inc(s_pt, 1)

                def weigh(h):
                    bank, o = OB[h // 2], (h % 2) * L
                    hd = slice(h * HD, (h + 1) * HD)
                    nc.tensor.matmul(bank[:, o:o + L], v_sb[par][:, 0, hd], prt[:, h, 0:2 * P], start=True, stop=False)
                    last = nc.tensor.matmul(bank[:, o + P:o + L], v_sb[par][:, 1, hd], prt[:, h, 2 * P:3 * P],
                                            start=False, stop=True)
                    if h % 2:
                        last.then_inc(s_pv, 1)

                pe.wait_ge(s_swp, 4 * n + 4)
                pe.wait_ge(s_pte, 4 * n)
                transposes(0)
                transposes(1)
                if more:
                    xn_here(m, mp)
                    pe.wait_ge(s_wlo, gn * NCH + 3 * CB)
                    pe.wait_ge(s_vev, 2 * n + 2)
                    pe.wait_ge(s_x1[0], n)
                    project(PJ[0], m, gn, mp, CH_Q, 0)
                pe.wait_ge(s_qke, 4 * n + 1)
                transposes(2)
                pe.wait_ge(s_qke, 4 * n + 2)
                transposes(3)
                pe.wait_ge(s_exp, 8 * n)
                scores(0)
                scores(1)
                if more:
                    pe.wait_ge(s_x1[1], n)
                    project(PJ[1], m, gn, mp, CH_Q, 1)
                    pe.wait_ge(s_mul, 4 * m + 1)
                    project(PJ[0], m, gn, mp, CH_K, 0)
                pe.wait_ge(s_qke, 4 * n + 4)
                pe.wait_ge(s_exp, 8 * n + 4)
                scores(2)
                scores(3)
                pe.wait_ge(s_pr, 8 * n + 4)
                prob_transposes(0)
                prob_transposes(1)
                if more:
                    pe.wait_ge(s_mul, 4 * m + 2)
                    project(PJ[1], m, gn, mp, CH_K, 1)
                    pe.wait_ge(s_mul, 4 * m + 3)
                    project(PJ[0], m, gn, mp, CH_V, 0)
                pe.wait_ge(s_pr, 8 * n + 8)
                pe.wait_ge(s_pte, 4 * n + 1)
                prob_transposes(2)
                pe.wait_ge(s_pte, 4 * n + 2)
                prob_transposes(3)
                pe.wait_ge(s_vev, 2 * n + 2)
                pe.wait_ge(s_olo, 2 * n)
                weigh(0)
                weigh(1)
                if more:
                    pe.wait_ge(s_mul, 4 * m + 4)
                    project(PJ[1], m, gn, mp, CH_V, 1)
                pe.wait_ge(s_pte, 4 * n + 4)
                weigh(2)
                weigh(3)
                pe.wait_ge(s_wlo, (g + 1) * NCH)
                for half in range(2):
                    pe.wait_ge(s_olo, 2 * n + half + 1)
                    for t in range(TB):
                        if half == 0 and more:
                            pe.wait_ge(s_vev, 2 * m + t + 1)
                        elif half == 0:
                            pe.wait_ge(s_vev, 2 * n + 2)
                        for h in (2 * half, 2 * half + 1):
                            tok = slice(t * P, (t + 1) * P)
                            for k, (o, w) in enumerate(((ohi, whi), (ohi, wlo), (olo, whi))):
                                last = nc.tensor.matmul(PJ[t][:, :], o[:, h, tok], w[g % 2][:, CH_O + h, :],
                                                        start=(h == 0 and k == 0), stop=(h == HG - 1 and k == 2))
                        if half:
                            last.then_inc(s_wo, 1)

            items(pe, item)

        @block.scalar
        def _(act):
            def w_chunk(c, total, dst, par, free):
                k = total // 2 if isinstance(total, int) else None
                act.wait_ge(s_raw[par], 16 * ((total - par + 1) // 2) if k is not None else 8 * (total - par + 1))
                out = whi[dst][:, c, :] if isinstance(c, int) else whi[dst][:, bass.ds(c, 1), :].rearrange("p o d -> p (o d)")
                nc.scalar.activation(out, raw[:, par, :], ACT.Copy).then_inc(s_whi, 1)

            def v_evac(m, mp, t):
                act.wait_ge(s_proj, 6 * m + 5 + t)
                nc.scalar.activation(v_sb[mp][:, t, :], PJ[t][:, :], ACT.Copy).then_inc(s_vev, 1)

            for c in range(NCH):
                w_chunk(c, c + 1, 0, c % 2, None)
            v_evac(0, 0, 0)
            v_evac(0, 0, 1)

            def item(n, g, b, par, gn, more):
                m, mp = n + 1, 1 - par

                def qk_evac(i):
                    act.wait_ge(s_qkt, 4 * n + i + 1)
                    h0 = 2 * (i // 2)
                    nc.scalar.activation(qkt[i % 2][:, h0:h0 + 2, :].rearrange("p h n -> p (h n)"), TR[i % 2][:, :],
                                         ACT.Copy).then_inc(s_qke, 1)

                def exps(pair):
                    act.wait_ge(s_nmx, 2 * n + pair + 1)
                    for h in (2 * pair, 2 * pair + 1):
                        for t in range(TB):
                            lo, hi = (0, P) if t == 0 else (P, 3 * P)
                            nc.scalar.activation(pr[:, h, lo:hi], SC[h % 2][:, lo:hi], ACT.Exp,
                                                 bias=nmx[:, h, t:t + 1], scale=SCALE,
                                                 accum_out=rsum[:, h, t:t + 1]).then_inc(s_exp, 1)

                def pt_evac(h):
                    act.wait_ge(s_pt, 4 * n + h + 1)
                    nc.scalar.activation(prt[:, h, :], TR[h % 2][:, 0:KBLK * P], ACT.Copy).then_inc(s_pte, 1)

                def o_round(pair):
                    act.wait_ge(s_pv, 2 * n + pair + 1)
                    nc.scalar.activation(ohi[:, 2 * pair:2 * pair + 2, :].rearrange("p h n -> p (h n)"), OB[pair][:, :],
                                         ACT.Copy).then_inc(s_ohi, 1)

                act.wait_ge(s_sc, 4 * n)
                qk_evac(0)
                qk_evac(1)
                qk_evac(2)
                qk_evac(3)
                if g + 1 < G:
                    act.wait_ge(s_wo, 2 * B * g)
                    w_chunk(b, n + (NCH + 1), (g + 1) % 2, par, None)
                act.wait_ge(s_pt, 4 * n)
                exps(0)
                exps(1)
                act.wait_ge(s_pv, 2 * n)
                pt_evac(0)
                pt_evac(1)
                if more:
                    act.wait_ge(s_pv, 2 * n)
                    v_evac(m, mp, 0)
                pt_evac(2)
                pt_evac(3)
                act.wait_ge(s_wo, 2 * n)
                o_round(0)
                if more:
                    v_evac(m, mp, 1)
                o_round(1)

            items(act, item)

        @block.vector
        def _(dve):
            def w_chunk(c, total, dst):
                dve.wait_ge(s_whi, total)
                par_c = (lambda a: a[:, c, :] if isinstance(c, int) else a[:, bass.ds(c, 1), :].rearrange("p o d -> p (o d)"))
                return par_c(whi[dst]), par_c(wlo[dst])

            def rope_mul(m, i):
                t = i % 2
                dve.wait_ge(s_proj, 6 * m + i + 1)
                half = HD // 2
                r = rot[i // 2][:, t, :].rearrange("p (h s d) -> p h s d", h=HG, s=2)
                s = swp[:, t, :].rearrange("p (h d) -> p h d", h=HG)
                bank = PJ[t][:, :].rearrange("p (h d) -> p h d", h=HG)
                nc.vector.tensor_tensor(r, bank.rearrange("p h (s d) -> p h s d", s=2),
                                        trig[:, t, 0, :].unsqueeze(1).unsqueeze(1).broadcast_to([P, HG, 2, half]),
                                        ALU.mult)
                for k, (lo, hi) in enumerate(((0, half), (half, HD))):
                    src = bank[:, :, half - lo:half - lo + half]
                    last = nc.vector.tensor_tensor(s[:, :, lo:hi], src,
                                                   trig[:, t, 1 + k, :].unsqueeze(1).broadcast_to([P, HG, half]),
                                                   ALU.mult)
                last.then_inc(s_mul, 1)

            for c in range(NCH):
                hi, lo = w_chunk(c, c + 1, 0)
                nc.vector.tensor_tensor(lo, raw[:, c % 2, :], hi.bitcast(F32), ALU.subtract).then_inc(s_wlo, 1)
            dve.wait_ge(s_trig, 16)
            for i in range(4):
                if i >= 2:
                    dve.wait_ge(s_swp, i - 1)
                rope_mul(0, i)

            def item(n, g, b, par, gn, more):
                m = n + 1

                def maxima(pair):
                    for h in (2 * pair, 2 * pair + 1):
                        dve.wait_ge(s_sc, 4 * n + h + 1)
                        for t in range(TB):
                            lo, hi = (0, P) if t == 0 else (P, 3 * P)
                            nc.vector.reduce_max(mx[:, h, t:t + 1], SC[h % 2][:, lo:hi], AX.X).then_inc(s_mx, 1)
                    dve.wait_ge(s_mx, 8 * n + 4 * pair + 4)
                    pr2 = slice(2 * pair, 2 * pair + 2)
                    nc.vector.tensor_scalar(nmx[:, pr2, :].rearrange("p h t -> p (h t)"),
                                            mx[:, pr2, :].rearrange("p h t -> p (h t)"), -SCALE, None,
                                            ALU.mult).then_inc(s_nmx, 1)

                def normalise(pair):
                    pr2 = slice(2 * pair, 2 * pair + 2)
                    dve.wait_ge(s_exp, 8 * n + 4 * pair + 4)
                    nc.vector.reciprocal(rinv[:, pr2, :].rearrange("p h t -> p (h t)"),
                                         rsum[:, pr2, :].rearrange("p h t -> p (h t)")).then_inc(s_ri, 1)
                    dve.wait_ge(s_ri, 2 * n + pair + 1)
                    for h in (2 * pair, 2 * pair + 1):
                        for t in range(TB):
                            lo, hi = (0, P) if t == 0 else (P, 3 * P)
                            nc.vector.tensor_scalar(pr[:, h, lo:hi], pr[:, h, lo:hi], rinv[:, h, t:t + 1], None,
                                                    ALU.mult).then_inc(s_pr, 1)

                def rope(i):
                    if more:
                        dve.wait_ge(s_swp, 4 * m + i - 1)
                        dve.wait_ge(s_qkt, 4 * n + 4)
                        rope_mul(m, i)

                rope(0)
                if g + 1 < G:
                    dve.wait_ge(s_wo, 2 * B * g)
                    hi, lo = w_chunk(b, n + (NCH + 1), (g + 1) % 2)
                    nc.vector.tensor_tensor(lo, raw[:, par, :], hi.bitcast(F32), ALU.subtract).then_inc(s_wlo, 1)
                maxima(0)
                rope(1)
                normalise(0)
                rope(2)
                maxima(1)
                rope(3)
                normalise(1)
                dve.wait_ge(s_wo, 2 * n)
                for pair in range(2):
                    dve.wait_ge(s_ohi, 2 * n + pair + 1)
                    nc.vector.tensor_tensor(olo[:, 2 * pair:2 * pair + 2, :].rearrange("p h n -> p (h n)"), OB[pair][:, :],
                                            ohi[:, 2 * pair:2 * pair + 2, :].rearrange("p h n -> p (h n)").bitcast(F32),
                                            ALU.subtract).then_inc(s_olo, 1)
                if isinstance(n, int):
                    dve.wait_ge(s_xi[par], 16 * (n // 2 + 1))
                else:
                    dve.wait_ge(s_xi[par], 8 * (n - par) + 16)
                for t in range(TB):
                    dve.wait_ge(s_wo, 2 * n + t + 1)
                    nc.vector.tensor_tensor(xio[:, par, t, :], PJ[t][:, :], xio[:, par, t, :], ALU.add).then_inc(s_x1[t], 1)
                if g == G - 1:
                    k = n - g * B
                    for t in range(TB):
                        dve.wait_ge(s_x1[t], n + 1)
                        dve.wait_ge(s_mv, 2 * k)
                        nc.vector.bn_stats(bn[:, t, :], xio[:, par, t, :]).then_inc(s_bn, 1)
                        dve.wait_ge(s_bn, 4 * k + 2 * t + 1)
                        dst = mv2[:, 2 * b + t, :] if isinstance(b, int) else mv2[:, bass.ds(2 * b + t, 1), :].rearrange("p o d -> p (o d)")
                        nc.vector.memset(hold[:, :], 0.0)
                        nc.vector.bn_aggr(agg[:, t, :], bn[:, t, :]).then_inc(s_bn, 1)
                        dve.wait_ge(s_bn, 4 * k + 2 * t + 2)
                        nc.vector.tensor_copy(dst, agg[:, t, :]).then_inc(s_mv, 1)

            items(dve, item)
            dve.wait_ge(s_mv, 2 * B)


def cross_attention(nc, x1, ctx_in, gamma, sq, sk, mv2, mv3, x2, cst):
    ident = cst["ident"]
    ctx = ExitStack()
    with ctx:
        def sb(name, shape, dt):
            return ctx.enter_context(nc.sbuf_tensor(name, shape, dt))

        def pb(name):
            return ctx.enter_context(nc.psum_tensor(name, [P, 512], F32))

        def sem(name):
            return ctx.enter_context(nc.semaphore(name))

        gam = sb("gam", [P, 1], F32)
        tmp = sb("rs_tmp2", [P, 2, TILES], F32)
        rstd = sb("rstd2", [P, TILES], F32)
        cin = sb("cin", [P, 2, D], F32)
        xn = sb("xn2", [P, D], F32)
        qp = sb("qp", [P, 2, D], F32R)
        kp = sb("kp", [P, 2, D], F32R)
        qst = [sb(f"qst{i}", [P, XPT, D], F32R) for i in range(2)]
        kst = [sb(f"kst{i}", [P, XPT, D], F32R) for i in range(2)]
        vt = sb("vt", [P, 2, CB, P], F32)
        pr = sb("xpr", [P, 2, CB, D], F32)
        prt = [sb(f"xprt{i}", [P, XPT, CB, D], F32) for i in range(2)]
        nmx = sb("xnmx", [P, 2, CB], F32)
        rsum = sb("xrsum", [P, 2, CB, XPT], F32)
        rinv = sb("xrinv", [P, 2, CB, XPT], F32)
        rbc = sb("xrbc", [P, D], F32)
        onm = sb("xonm", [P, D], F32)
        bn = sb("bn3", [P, 6], F32)
        agg = sb("agg3", [P, 2], F32)
        hold = sb("hold3", [P, 1], F32)
        SC = [pb(f"xsc{i}") for i in range(CB)]
        TR = [pb(f"xtr{i}") for i in range(2)]
        OB = pb("xob")
        VB = pb("xvb")

        s_gam, s_var, s_sqrt, s_step = sem("x_gam"), sem("x_var"), sem("x_sqrt"), sem("x_step")
        s_xi = [sem(f"x_xi{i}") for i in range(2)]
        s_ci = [sem(f"x_ci{i}") for i in range(2)]
        s_qn, s_qlo = sem("x_qn"), sem("x_qlo")
        s_khi, s_klo = sem("x_khi"), sem("x_klo")
        s_qw, s_kw = sem("x_qw"), sem("x_kw")
        s_st = [sem(f"x_st{i}") for i in range(2)]
        s_vt, s_vte = sem("x_vt"), sem("x_vte")
        s_sc = sem("x_sc")
        s_mx = sem("x_mx")
        s_exp = sem("x_exp")
        s_ri = sem("x_ri")
        s_rb, s_rbe = sem("x_rb"), sem("x_rbe")
        s_on = sem("x_on")
        s_pt = sem("x_pt")
        s_pta, s_ptd = sem("x_pta"), sem("x_ptd")
        s_pv = sem("x_pv")
        s_x2 = sem("x_x2")
        s_bn, s_mv = sem("x_bn"), sem("x_mv")
        block = ctx.enter_context(nc.Block())

        cv = ctx_in.rearrange("b (t p) d -> (b t) p d", p=P)
        x1v = x1.rearrange("b p t d -> b t p d")

        def col(ap, n):
            return ap[:, n, :] if isinstance(n, int) else ap[:, bass.ds(n, 1), :].rearrange("p o d -> p (o d)")

        def all_tiles(eng, item):
            item(0, 0, True, True, True)
            item(1, 1, False, True, True)
            with eng.Fori(1, TILES // 2 - 1) as i:
                for t in range(2):
                    item(2 * i + t, t, False, True, True)
            item(TILES - 2, 0, False, True, False)
            item(TILES - 1, 1, False, False, False)

        def loads(n, t):
            return 16 * (n // 2 + 1) if isinstance(n, int) else 8 * (n - t) + 16

        @block.sync
        def _(sp):
            sp.dma_start(gam[:, :], gamma.rearrange("(a b) -> a b", a=1).broadcast_to([P, 1])).then_inc(s_gam, 16)

            def load(n, t, b=None):
                dst = x2[:, n, :] if isinstance(n, int) else x2[:, bass.ds(n, 1), :].rearrange("p o d -> p (o d)")
                if isinstance(n, int):
                    src, csrc = x1v[n // 2, t], cv[n]
                else:
                    src = x1v[bass.ds(b, 1), t].rearrange("o p d -> (o p) d")
                    csrc = cv[bass.ds(n, 1)].rearrange("o p d -> (o p) d")
                sp.dma_start(dst, src).then_inc(s_xi[t], 16)
                sp.dma_start(cin[:, t, :], csrc).then_inc(s_ci[t], 16)

            def write_parts(count, t):
                sp.dma_start(sq[t].rearrange("h p d -> p h d"), qp[:, :, :].bitcast(F32)).then_inc(s_qw, 16)
                sp.wait_ge(s_klo, count)
                sp.dma_start(sk[t].rearrange("h p d -> p h d"), kp[:, :, :].bitcast(F32)).then_inc(s_kw, 16)

            def read_stacks(n, t):
                sp.wait_ge(s_qw, 16 * n + 16)
                sp.wait_ge(s_kw, 16 * n + 16)
                qv = sq[t].rearrange("h (j r) d -> h r j d", j=XPT)
                kv = sk[t].rearrange("h (j r) d -> h r j d", j=XPT)
                for c in range(4):
                    rows = slice(XD * c, XD * (c + 1))
                    sp.dma_start(qst[t][rows, :, :].bitcast(F32), qv[c // 2]).then_inc(s_st[t], 16)
                    sp.dma_start(kst[t][rows, :, :].bitcast(F32), kv[c % 2]).then_inc(s_st[t], 16)

            for t in range(2):
                load(t, t)
            for t in range(2):
                sp.wait_ge(s_qlo, t + 1)
                write_parts(t + 1, t)
                read_stacks(t, t)

            def item(n, t, first, more, more2):
                if more2:
                    b = None if isinstance(n, int) else sp.snap((n - t) // 2 + 1)
                    sp.wait_ge(s_vt, n + 1)
                    sp.wait_ge(s_klo, n + 1)
                    load(n + 2, t, b)
                    sp.wait_ge(s_qlo, n + 3)
                    sp.wait_ge(s_st[t], 128 * (n // 2 + 1) if isinstance(n, int) else 64 * (n - t) + 128)
                    write_parts(n + 3, t)
                    sp.wait_ge(s_sc, 16 * n + 16)
                    read_stacks(n + 2, t)

            all_tiles(sp, item)

        @block.gpsimd
        def _(pool):
            def split(n, t):
                pool.wait_ge(s_ci[t], loads(n, t))
                pool.wait_ge(s_kw, 16 * n)
                pool.wait_ge(s_qn, 2 * n + 2)
                pool.wait_ge(s_qw, 16 * n)
                nc.gpsimd.tensor_tensor(qp[:, 1, :], xn[:, :], qp[:, 0, :].bitcast(F32),
                                        ALU.subtract).then_inc(s_qlo, 1)
                nc.gpsimd.tensor_copy(kp[:, 0, :], cin[:, t, :]).then_inc(s_khi, 1)
                pool.wait_ge(s_khi, n + 1)
                nc.gpsimd.tensor_tensor(kp[:, 1, :], cin[:, t, :], kp[:, 0, :].bitcast(F32),
                                        ALU.subtract).then_inc(s_klo, 1)

            for t in range(2):
                split(t, t)

            def item(n, t, first, more, more2):
                if more2:
                    split(n + 2, t)

            all_tiles(pool, item)

        @block.tensor
        def _(pe):
            def scores(n, t, h, banks=range(CB)):
                for q in banks:
                    if not (isinstance(n, int) and n == 0 and h == 0):
                        pe.wait_ge(s_exp, 16 * n + 4 * h - 3 + q)
                    nc.tensor.matmul(SC[q][:, :], qst[t][:, h, q * P:(q + 1) * P], kst[t][:, h, :],
                                     start=True, stop=True).then_inc(s_sc, 1)

            def stacks_here(n, t):
                pe.wait_ge(s_st[t], 128 * (n // 2 + 1) if isinstance(n, int) else 64 * (n - t) + 128)

            def output(n, t):
                pe.wait_ge(s_pta, 8 * n + 8)
                pe.wait_ge(s_ptd, 8 * n + 8)
                pe.wait_ge(s_vte, n + 1)
                pe.wait_ge(s_on, n)
                for c in range(CB):
                    for h in range(XPT):
                        last = nc.tensor.matmul(OB[XD * h:XD * (h + 1), :], vt[:, t, c, XD * h:XD * (h + 1)],
                                                prt[t][:, h, c, :], start=(c == 0), stop=(c == CB - 1))
                last.then_inc(s_pv, 1)
                pe.wait_ge(s_ri, n + 1)
                for q in range(CB):
                    for h in range(XPT):
                        last = nc.tensor.matmul(VB[XD * h:XD * (h + 1), q * P:(q + 1) * P],
                                                rinv[:, t, q, h:h + 1].broadcast_to([P, XD]), ident[:, :],
                                                start=True, stop=True)
                last.then_inc(s_rb, 1)

            stacks_here(0, 0)
            scores(0, 0, 0)

            def item(n, t, first, more, more2):
                pe.wait_ge(s_ci[t], loads(n, t))
                pe.wait_ge(s_vte, n)
                if not first:
                    pe.wait_ge(s_rbe, n - 1)
                for c in range(CB):
                    last = nc.tensor.transpose(VB[:, c * P:(c + 1) * P], cin[:, t, c * P:(c + 1) * P], ident[:, :])
                last.then_inc(s_vt, 1)
                for h in range(XPT):
                    def next_scores(banks):
                        if h + 1 < XPT:
                            scores(n, t, h + 1, banks)
                        elif more:
                            scores(n + 1, 1 - t, 0, banks)

                    def prob_transposes(c):
                        pe.wait_ge((s_pta, s_ptd)[c % 2], 8 * n + 2 * h + c // 2)
                        for q in range(CB):
                            last = nc.tensor.transpose(TR[c % 2][:, q * P:(q + 1) * P],
                                                       pr[:, h % 2, q, c * P:(c + 1) * P], ident[:, :])
                        last.then_inc(s_pt, 1)

                    if h + 1 == XPT and more:
                        stacks_here(n + 1, 1 - t)
                    next_scores([0])
                    next_scores([1])
                    pe.wait_ge(s_exp, 16 * n + 4 * h + 4)
                    prob_transposes(0)
                    prob_transposes(1)
                    next_scores([2, 3])
                    prob_transposes(2)
                    prob_transposes(3)
                    if h == 0 and not first:
                        output(n - 1, 1 - t)

            all_tiles(pe, item)
            output(TILES - 1, 1)

        @block.scalar
        def _(act):
            rstd_of_all(nc, act, None, None, rstd, tmp, s_var, 1, s_sqrt, s_step, XSCALE)

            def exps(n, t, h, banks=range(CB)):
                if not (isinstance(n, int) and n == 0 and h == 0):
                    act.wait_ge(s_pt, 16 * n + 4 * h - 4)
                for q in banks:
                    act.wait_ge(s_mx, 16 * n + 4 * h + q + 1)
                    nc.scalar.activation(pr[:, h % 2, q, :], SC[q][:, :], ACT.Exp, bias=nmx[:, h % 2, q:q + 1],
                                         accum_out=rsum[:, t, q, h:h + 1]).then_inc(s_exp, 1)

            exps(0, 0, 0)

            def item(n, t, first, more, more2):
                act.wait_ge(s_vt, n + 1)
                if not first:
                    act.wait_ge(s_pv, n - 1)
                nc.scalar.activation(vt[:, t, :, :].rearrange("p c n -> p (c n)"), VB[:, :], ACT.Copy).then_inc(s_vte, 1)
                for h in range(XPT):
                    for c in (0, 2):
                        if h + 1 < XPT:
                            exps(n, t, h + 1, (c, c + 1))
                        elif more:
                            exps(n + 1, 1 - t, 0, (c, c + 1))
                        act.wait_ge(s_pt, 16 * n + 4 * h + c + 1)
                        nc.scalar.activation(prt[t][:, h, c, :], TR[0][:, :], ACT.Copy).then_inc(s_pta, 1)
                    if h == 0 and not first:
                        sums_evac(n - 1)

            def sums_evac(n):
                act.wait_ge(s_rb, n + 1)
                act.wait_ge(s_on, n)
                nc.scalar.activation(rbc[:, :], VB[:, :], ACT.Copy).then_inc(s_rbe, 1)

            all_tiles(act, item)
            sums_evac(TILES - 1)

        @block.vector
        def _(dve):
            nc.vector.tensor_scalar(tmp[:, 0, :], mv2[:, :, 1], EPS, None, ALU.add).then_inc(s_var, 1)
            dve.wait_ge(s_var, 1)
            rstd_of_all(nc, None, dve, None, rstd[:, :], tmp, s_var, 1, s_sqrt, s_step, XSCALE)
            dve.wait_ge(s_gam, 16)

            def normed(n, t, parts=(0, 1)):
                if 0 in parts:
                    dve.wait_ge(s_xi[t], loads(n, t))
                    dve.wait_ge(s_qlo, n)
                    dve.wait_ge(s_qw, 16 * n)
                i = slice(n, n + 1) if isinstance(n, int) else bass.ds(n, 1)
                for out in [(xn[:, :], qp[:, 0, :])[k] for k in parts]:
                    nc.vector.tensor_scalar(out, col(x2, n), mv2[:, i, 0], rstd[:, i],
                                            ALU.subtract, ALU.mult).then_inc(s_qn, 1)

            def maxima(n, h, banks=range(CB)):
                for q in banks:
                    dve.wait_ge(s_sc, 16 * n + 4 * h + q + 1)
                    nc.vector.tensor_reduce(nmx[:, h % 2, q:q + 1], SC[q][:, :], AX.X, ALU.max,
                                            negate=True).then_inc(s_mx, 1)

            def output(n):
                dve.wait_ge(s_rbe, n + 1)
                nc.vector.tensor_tensor(onm[:, :], OB[:, :], rbc[:, :], ALU.mult).then_inc(s_on, 1)

            def residual(n):
                dve.wait_ge(s_on, n + 1)
                nc.vector.scalar_tensor_tensor(col(x2, n), onm[:, :], gam[:, 0:1], col(x2, n), ALU.mult,
                                               ALU.add).then_inc(s_x2, 1)

            def statistics(n):
                dve.wait_ge(s_x2, n + 1)
                dve.wait_ge(s_mv, n)
                nc.vector.memset(hold[:, :], 0.0)
                nc.vector.bn_stats(bn[:, :], col(x2, n)).then_inc(s_bn, 1)

            def mean_and_variance(n):
                dve.wait_ge(s_bn, 2 * n + 1)
                nc.vector.memset(hold[:, :], 0.0)
                nc.vector.bn_aggr(agg[:, :], bn[:, :]).then_inc(s_bn, 1)

            def keep_statistics(n):
                dve.wait_ge(s_bn, 2 * n + 2)
                nc.vector.tensor_copy(col(mv3, n), agg[:, :]).then_inc(s_mv, 1)

            def between(n, t, h, k, first, more2):
                if not first and (h, k) == (1, 0):
                    output(n - 1)
                if not first and (h, k) == (1, 1):
                    residual(n - 1)
                if not first and (h, k) == (2, 0):
                    statistics(n - 1)
                if not first and (h, k) == (2, 1):
                    mean_and_variance(n - 1)
                if not first and (h, k) == (3, 0):
                    keep_statistics(n - 1)
                if more2 and (h, k) == (2, 1):
                    normed(n + 2, t, [0])
                if more2 and (h, k) == (3, 0):
                    normed(n + 2, t, [1])

            for t in range(2):
                normed(t, t)
            maxima(0, 0)

            def item(n, t, first, more, more2):
                for h in range(XPT):
                    for c in (1, 3):
                        if h + 1 < XPT:
                            maxima(n, h + 1, (c - 1, c))
                        elif more:
                            maxima(n + 1, 0, (c - 1, c))
                        between(n, t, h, c // 2, first, more2)
                        dve.wait_ge(s_pt, 16 * n + 4 * h + c + 1)
                        nc.vector.tensor_copy(prt[t][:, h, c, :], TR[1][:, :]).then_inc(s_ptd, 1)
                dve.wait_ge(s_exp, 16 * n + 16)
                nc.vector.reciprocal(rinv[:, t, :, :].rearrange("p q h -> p (q h)"),
                                     rsum[:, t, :, :].rearrange("p q h -> p (q h)")).then_inc(s_ri, 1)

            all_tiles(dve, item)
            for finish in (output, residual, statistics, mean_and_variance, keep_statistics):
                finish(TILES - 1)
            dve.wait_ge(s_mv, TILES)


def expert_mix(nc, router_w, router_b, expert_w, expert_b, mv3, x2, out, cst):
    ident, tri, ones = cst["ident"], cst["tri"], cst["ones"]
    ctx = ExitStack()
    with ctx:
        def sb(name, shape, dt):
            return ctx.enter_context(nc.sbuf_tensor(name, shape, dt))

        def pb(name):
            return ctx.enter_context(nc.psum_tensor(name, [P, 512], F32))

        def sem(name):
            return ctx.enter_context(nc.semaphore(name))

        TE = TILES * E
        PER = TE // 4
        z = sb("z", [P, TILES, D], F32)
        ew = sb("ew", [P, CB, D], F32)
        ewp = [sb(f"ewp{i}", [P, CB, D], F32R) for i in range(2)]
        rw = sb("rw", [P, CB, E], F32)
        rwp = [sb(f"rwp{i}", [P, CB, E], F32R) for i in range(2)]
        eb = sb("eb", [P, D], F32)
        rb = sb("rb", [P, E], F32)
        tmp = sb("rs_tmp3", [P, 2, TILES], F32)
        rstd = sb("rstd3", [P, TILES], F32)
        xn = sb("xn3", [P, 2, D], F32)
        xp = [sb(f"xp{i}", [P, 2, CB * P], F32R) for i in range(2)]
        prob = sb("prob", [P, TILES, E], F32)
        rmax = sb("rmax", [P, TILES], F32)
        rinv = sb("rinv3", [P, TILES], F32)
        bits = sb("bits", [P, 2, E], I32)
        thr = sb("thr", [P, E], I32)
        add = sb("add", [P, E], I32)
        cand = sb("cand", [P, E], I32)
        taken = sb("taken", [P, TILES, E], BF16)
        equal = sb("equal", [P, TILES, E], BF16)
        count = sb("count", [P, E], F32)
        total = sb("total", [P, TILES, E], F32)
        run = [sb(f"run{i}", [P, TILES, E], F32) for i in range(2)]
        coef = sb("coef", [P, TILES], F32)
        TR = [pb(f"f_tr{i}") for i in range(2)]
        ZB = [pb(f"f_z{i}") for i in range(2)]
        LB = [pb(f"f_l{i}") for i in range(2)]
        CN = pb("f_cn")
        TB2 = pb("f_tb")

        s_w, s_b = sem("f_w"), sem("f_b")
        s_whi, s_wlo = sem("f_whi"), sem("f_wlo")
        s_var, s_sqrt, s_step = sem("f_var"), sem("f_sqrt"), sem("f_rstep")
        s_xn, s_tr, s_hi, s_lo = sem("f_xn"), sem("f_tr"), sem("f_hi"), sem("f_lo")
        s_lg, s_lge, s_z, s_ze = sem("f_lg"), sem("f_lge"), sem("f_z"), sem("f_ze")
        s_soft, s_exp = sem("f_soft"), sem("f_exp")
        s_cand, s_cnt, s_srch = sem("f_cand"), sem("f_cnt"), sem("f_srch")
        s_pick, s_rank = sem("f_pick"), sem("f_rank")
        s_out, s_st = sem("f_out"), sem("f_st")
        block = ctx.enter_context(nc.Block())
        ov = out.rearrange("b (t p) d -> b p t d", p=P)

        def col(ap, n):
            return ap[:, bass.ds(n, 1), :].rearrange("p o d -> p (o d)")

        def flat(ap):
            return ap.rearrange("p a b -> p (a b)")

        @block.sync
        def _(sp):
            sp.dma_start(ew[:, :, :], expert_w.rearrange("(c p) n -> p c n", p=P)).then_inc(s_w, 16)
            sp.dma_start(rw[:, :, :], router_w.rearrange("(c p) n -> p c n", p=P)).then_inc(s_w, 16)
            sp.dma_start(eb[:, :], expert_b.rearrange("(a n) -> a n", a=1).broadcast_to([P, D])).then_inc(s_b, 16)
            sp.dma_start(rb[:, :], router_b.rearrange("(a n) -> a n", a=1).broadcast_to([P, E])).then_inc(s_b, 16)
            def turn(b):
                sp.wait_ge(s_out, 2 * b + 2)
                sp.dma_start(ov[bass.ds(b, 1)].rearrange("o p t d -> (o p) t d"),
                             z[:, bass.ds(2 * b, 2), :]).then_inc(s_st, 16)

            turns(sp, B, turn)
            sp.wait_ge(s_st, 16 * B)

        @block.tensor
        def _(pe):
            pe.wait_ge(s_wlo, 2)
            def turn(i):
                for t in range(2):
                    n = 2 * i + t
                    pe.wait_ge(s_xn, n + 1)
                    pe.wait_ge(s_lo, 2 * i)
                    for c in range(CB):
                        last = nc.tensor.transpose(TR[t][:, c * P:(c + 1) * P], xn[:, t, c * P:(c + 1) * P], ident[:, :])
                    last.then_inc(s_tr, 1)
                for t in range(2):
                    n = 2 * i + t
                    pe.wait_ge(s_lo, n + 1)
                    for out_bank, w, last_sem in ((LB[t][:, 0:E], rwp, s_lg), (ZB[t][:, :], ewp, s_z)):
                        pe.wait_ge(s_lge if last_sem is s_lg else s_ze, 2 * i)
                        k = 0
                        for c in range(CB):
                            for a, b in ((0, 0), (0, 1), (1, 0)):
                                last = nc.tensor.matmul(out_bank, xp[t][:, a, c * P:(c + 1) * P], w[b][:, c, :],
                                                        start=(k == 0), stop=(k == 3 * CB - 1))
                                k += 1
                        last.then_inc(last_sem, 1)

            turns(pe, TILES // 2, turn)

            def count_taken():
                for i in range(4):
                    last = nc.tensor.matmul(CN[:, 0:PER], ones[:, :], flat(taken[:, i * (TILES // 4):(i + 1) * (TILES // 4), :]),
                                            start=(i == 0), stop=(i == 3))
                last.then_inc(s_cnt, 1)

            with pe.Fori(0, 30) as r:
                pe.wait_ge(s_cand, r + 1)
                count_taken()
            pe.wait_ge(s_pick, 2)
            count_taken()
            nc.tensor.matmul(CN[:, :] if False else TR[0][:, :], tri[:, :], flat(equal[:, :, :]), start=True, stop=True)
            nc.tensor.matmul(TB2[:, :], ones[:, :], flat(equal[:, :, :]), start=True, stop=True).then_inc(s_rank, 1)

        @block.scalar
        def _(act):
            act.wait_ge(s_w, 32)
            nc.scalar.activation(flat(ewp[0][:, :, :]), flat(ew[:, :, :]), ACT.Copy).then_inc(s_whi, 1)
            nc.scalar.activation(flat(rwp[0][:, :, :]), flat(rw[:, :, :]), ACT.Copy).then_inc(s_whi, 1)
            rstd_of_all(nc, act, None, None, rstd, tmp, s_var, 1, s_sqrt, s_step, 1.0)
            def turn(i):
                for t in range(2):
                    n = 2 * i + t
                    act.wait_ge(s_tr, n + 1)
                    act.wait_ge(s_z, 2 * i)
                    nc.scalar.activation(xp[t][:, 0, :], TR[t][:, :], ACT.Copy).then_inc(s_hi, 1)

            turns(act, TILES // 2, turn)
            act.wait_ge(s_soft, 2)
            nc.scalar.activation(flat(prob[:, :, :]), flat(prob[:, :, :]), ACT.Exp).then_inc(s_exp, 1)

        @block.gpsimd
        def _(pool):
            pass

        @block.vector
        def _(dve):
            dve.wait_ge(s_whi, 2)
            nc.vector.tensor_tensor(flat(ewp[1][:, :, :]), flat(ew[:, :, :]), flat(ewp[0][:, :, :]).bitcast(F32),
                                    ALU.subtract).then_inc(s_wlo, 1)
            nc.vector.tensor_tensor(flat(rwp[1][:, :, :]), flat(rw[:, :, :]), flat(rwp[0][:, :, :]).bitcast(F32),
                                    ALU.subtract).then_inc(s_wlo, 1)
            nc.vector.tensor_scalar(tmp[:, 0, :], mv3[:, :, 1], EPS, None, ALU.add).then_inc(s_var, 1)
            dve.wait_ge(s_var, 1)
            rstd_of_all(nc, None, dve, None, rstd[:, :], tmp, s_var, 1, s_sqrt, s_step, 1.0)
            dve.wait_ge(s_b, 32)
            def turn(i):
                for t in range(2):
                    n = 2 * i + t
                    dve.wait_ge(s_tr, 2 * i)
                    nc.vector.tensor_scalar(xn[:, t, :], col(x2, n), mv3[:, bass.ds(n, 1), 0], rstd[:, bass.ds(n, 1)],
                                            ALU.subtract, ALU.mult).then_inc(s_xn, 1)
                for t in range(2):
                    n = 2 * i + t
                    dve.wait_ge(s_hi, n + 1)
                    nc.vector.tensor_tensor(xp[t][:, 1, :], TR[t][:, :], xp[t][:, 0, :].bitcast(F32),
                                            ALU.subtract).then_inc(s_lo, 1)
                for t in range(2):
                    n = 2 * i + t
                    dve.wait_ge(s_lg, n + 1)
                    nc.vector.tensor_tensor(col(prob, n), LB[t][:, 0:E], rb[:, :], ALU.add).then_inc(s_lge, 1)
                    dve.wait_ge(s_z, n + 1)
                    nc.vector.tensor_tensor(col(z, n), ZB[t][:, :], eb[:, :], ALU.add).then_inc(s_ze, 1)

            turns(dve, TILES // 2, turn)

            def by_tile(ap):
                return ap.unsqueeze(2).broadcast_to([P, TILES, E])

            dve.wait_ge(s_lge, TILES)
            nc.vector.reduce_max(rmax[:, :], prob[:, :, :], AX.X).then_inc(s_soft, 1)
            dve.wait_ge(s_soft, 1)
            nc.vector.tensor_tensor(prob[:, :, :], prob[:, :, :], by_tile(rmax[:, :]), ALU.subtract).then_inc(s_soft, 1)
            nc.vector.memset(thr[:, :], 0).then_inc(s_soft, 1)
            nc.vector.memset(bits[:, 0, :], 1 << 29).then_inc(s_soft, 1)
            nc.vector.memset(cand[:, :], 1 << 29).then_inc(s_soft, 1)
            dve.wait_ge(s_exp, 1)
            nc.vector.reduce_sum(rmax[:, :], prob[:, :, :], AX.X).then_inc(s_soft, 1)
            dve.wait_ge(s_soft, 6)
            nc.vector.reciprocal(rinv[:, :], rmax[:, :]).then_inc(s_soft, 1)
            dve.wait_ge(s_soft, 7)
            nc.vector.tensor_tensor(prob[:, :, :], prob[:, :, :], by_tile(rinv[:, :]), ALU.mult).then_inc(s_soft, 1)
            dve.wait_ge(s_soft, 8)

            def by_expert(ap):
                return ap.unsqueeze(1).broadcast_to([P, TILES, E])

            STEPS = 5

            def counted(c):
                dve.wait_ge(s_cnt, c)
                return nc.vector.reduce_sum(count[:, :], CN[:, 0:PER].rearrange("p (t e) -> p e t", e=E), AX.X)

            with dve.Fori(0, 15) as i:
                for k in range(2):
                    r = 2 * i + k
                    nc.vector.tensor_tensor(taken[:, :, :], prob[:, :, :], by_expert(cand[:, :].bitcast(F32)),
                                            ALU.is_ge).then_inc(s_cand, 1)
                    nc.vector.tensor_scalar(bits[:, 1 - k, :], bits[:, k, :], 1, None,
                                            ALU.logical_shift_right).then_inc(s_srch, 1)
                    counted(r + 1).then_inc(s_srch, 1)
                    dve.wait_ge(s_srch, STEPS * r + 2)
                    nc.vector.scalar_tensor_tensor(add[:, :], count[:, :], float(TOPK), bits[:, k, :], ALU.is_ge,
                                                   ALU.mult).then_inc(s_srch, 1)
                    dve.wait_ge(s_srch, STEPS * r + 3)
                    nc.vector.tensor_tensor(thr[:, :], thr[:, :], add[:, :], ALU.bitwise_or).then_inc(s_srch, 1)
                    dve.wait_ge(s_srch, STEPS * r + 4)
                    nc.vector.tensor_tensor(cand[:, :], thr[:, :], bits[:, 1 - k, :], ALU.bitwise_or).then_inc(s_srch, 1)
                    dve.wait_ge(s_srch, STEPS * r + 5)

            t_f = by_expert(thr[:, :].bitcast(F32))
            nc.vector.tensor_tensor(taken[:, :, :], prob[:, :, :], t_f, ALU.is_gt).then_inc(s_pick, 1)
            nc.vector.tensor_tensor(equal[:, :, :], prob[:, :, :], t_f, ALU.is_equal).then_inc(s_pick, 1)
            steps = [2]

            def step(ins):
                steps[0] += 1
                ins.then_inc(s_pick, 1)
                dve.wait_ge(s_pick, steps[0])

            step(counted(31))
            step(nc.vector.tensor_scalar(count[:, :], count[:, :], -1.0, float(TOPK), ALU.mult, ALU.add))
            dve.wait_ge(s_rank, 1)
            step(nc.vector.tensor_copy(flat(total[:, :, :]), TB2[:, :]))
            step(nc.vector.tensor_copy(flat(run[0][:, :, :]), TB2[:, :]))
            a, shift = 0, 1
            while shift < TILES:
                src, dst = run[a], run[1 - a]
                step(nc.vector.tensor_copy(dst[:, 0:shift, :], src[:, 0:shift, :]))
                step(nc.vector.tensor_tensor(dst[:, shift:TILES, :], src[:, shift:TILES, :],
                                             src[:, 0:TILES - shift, :], ALU.add))
                a, shift = 1 - a, 2 * shift
            rank = run[a]
            step(nc.vector.tensor_tensor(rank[:, :, :], rank[:, :, :], total[:, :, :], ALU.subtract))
            step(nc.vector.tensor_tensor(flat(rank[:, :, :]), TR[0][:, :], flat(rank[:, :, :]), ALU.add))
            step(nc.vector.tensor_tensor(rank[:, :, :], rank[:, :, :], by_expert(count[:, :]), ALU.is_le))
            step(nc.vector.tensor_tensor(rank[:, :, :], rank[:, :, :], equal[:, :, :], ALU.mult))
            step(nc.vector.tensor_tensor(rank[:, :, :], rank[:, :, :], taken[:, :, :], ALU.add))
            step(nc.vector.tensor_tensor(rank[:, :, :], rank[:, :, :], prob[:, :, :], ALU.mult))
            step(nc.vector.reduce_sum(coef[:, :], rank[:, :, :], AX.X))
            dve.wait_ge(s_ze, TILES)
            with dve.Fori(0, TILES) as n:
                nc.vector.scalar_tensor_tensor(col(z, n), col(z, n), coef[:, bass.ds(n, 1)], col(x2, n), ALU.mult,
                                               ALU.add).then_inc(s_out, 1)


def decoder_layer(nc, x, ctx_in, w_all, gamma, router_w, router_b, expert_w, expert_b, rope, out):
    xt = nc.dram_tensor("xt_scratch", [B, P, 2, CB, L], F32).ap()
    x1 = nc.dram_tensor("x1_scratch", [B, P, TB, D], F32).ap()
    sq = nc.dram_tensor("sq_scratch", [2, 2, P, D], F32).ap()
    sk = nc.dram_tensor("sk_scratch", [2, 2, P, D], F32).ap()
    ctx = ExitStack()
    with ctx:
        def sb(name, shape, dt):
            return ctx.enter_context(nc.sbuf_tensor(name, shape, dt))

        cst = dict(ident=sb("ident", [P, P], F32), identb=sb("identb", [P, P], BF16), mask=sb("mask", [P, P], BF16),
                   ones=sb("ones", [P, P], BF16), tri=sb("tri", [P, P], BF16))
        mv2 = sb("mv2", [P, TILES, 2], F32)
        mv3 = sb("mv3", [P, TILES, 2], F32)
        layer_norm_1(nc, x, xt, cst)
        self_attention(nc, x, w_all, rope, xt, x1, mv2, cst)
        x2 = sb("x2", [P, TILES, D], F32)
        cross_attention(nc, x1, ctx_in, gamma, sq, sk, mv2, mv3, x2, cst)
        expert_mix(nc, router_w, router_b, expert_w, expert_b, mv3, x2, out, cst)


def rope_table():
    inv = (1.0 / np.power(np.float32(10000.0), np.arange(0, HD, 2, dtype=np.float32) / np.float32(HD))).astype(np.float32)
    ang = (np.arange(L, dtype=np.float32)[:, None] * inv[None, :]).astype(np.float64)
    cos, sin = np.cos(ang), np.sin(ang)
    table = np.stack([cos, -sin, sin], 1).astype(np.float32)
    return np.ascontiguousarray(table.reshape(TB, P, 3, HD // 2).transpose(1, 0, 2, 3))


def kernel(**inputs):
    import numpy as _np
    import concourse.bacc as _bacc
    from concourse import mybir as _mybir
    from concourse.bass_utils import run_bass_kernel_spmd as _run

    nc = _bacc.Bacc("TRN2", target_bir_lowering=False, num_devices=1)
    wq, wk, wv, wo = (_np.asarray(inputs[f"L0_attn_w{k}"]) for k in "qkvo")
    proj = [w.reshape(CB, P, G, GW).transpose(2, 0, 1, 3) for w in (wq, wk, wv)]
    w_all = _np.ascontiguousarray(_np.concatenate(proj + [wo.reshape(G, HG, P, D)], axis=1))
    feeds = {
        "x": inputs["x"], "ctx_in": inputs["ctx_2048"], "w_all": w_all,
        "gamma": _np.asarray(inputs["L0_xattn_gamma"]).reshape(1), "router_w": inputs["L0_ffn_router_w"],
        "router_b": inputs["L0_ffn_router_b"], "expert_w": inputs["L0_ffn_expert_w"],
        "expert_b": inputs["L0_ffn_expert_b"], "rope": rope_table(),
    }
    arrays, args = {}, {}
    for name, a in feeds.items():
        a = _np.ascontiguousarray(a)
        arrays[f"in_{name}_dram"] = a
        args[name] = nc.dram_tensor(f"in_{name}_dram", a.shape, _mybir.dt.from_np(a.dtype), kind="ExternalInput").ap()
    out = nc.dram_tensor("out_0_dram", (B, L, D), _mybir.dt.float32, kind="ExternalOutput").ap()
    decoder_layer(nc, out=out, **args)
    r = _run(nc, [arrays], core_ids=[0])
    return r.results[0]["out_0_dram"]
```

```python
import concourse.bass as bass
from concourse import mybir
from contextlib import ExitStack
import numpy as np

F32 = mybir.dt.float32
F32R = mybir.dt.float32r
BF16 = mybir.dt.bfloat16
I32 = mybir.dt.int32
ALU = mybir.AluOpType
ACT = mybir.ActivationFunctionType
AX = mybir.AxisListType

P = 128
B, L, D = 16, 256, 512
TILES = B * L // P
TB = L // P
CB = D // P
H, HD = 16, 128
HG = 4
G = H // HG
GW = HG * HD
NCH = 3 * CB + HG
KBLK = 3
XH, XD = 8, 32
XPT = P // XD
E = 16
TOPK = B * L // E
EPS = 1e-5
MASKED = -3.0e38
SCALE = HD ** -0.5
XSCALE = XD ** -0.5
CH_Q, CH_K, CH_V, CH_O = 0, CB, 2 * CB, 3 * CB


def turns(eng, count, body):
    body(0)
    with eng.Fori(1, count) as i:
        body(i)


def rstd_of_all(nc, act, dve, rstd, tmp, s_in, s_sqrt, s_step, turn=0, scale=1.0):
    if act is not None:
        act.wait_ge(s_in, turn + 1)
        nc.scalar.activation(tmp[:, 1, :], tmp[:, 0, :], ACT.Sqrt).then_inc(s_sqrt, 1)
    if dve is not None:
        steps = [5 * turn]

        def step(ins):
            steps[0] += 1
            ins.then_inc(s_step, 1)
            dve.wait_ge(s_step, steps[0])

        dve.wait_ge(s_sqrt, turn + 1)
        step(nc.vector.reciprocal(rstd, tmp[:, 1, :]))
        step(nc.vector.tensor_tensor(tmp[:, 1, :], rstd, rstd, ALU.mult))
        step(nc.vector.tensor_tensor(tmp[:, 1, :], tmp[:, 1, :], tmp[:, 0, :], ALU.mult))
        step(nc.vector.tensor_scalar(tmp[:, 1, :], tmp[:, 1, :], -0.5 * scale, 1.5 * scale, ALU.mult, ALU.add))
        step(nc.vector.tensor_tensor(rstd, rstd, tmp[:, 1, :], ALU.mult))


def layer_norm_1(nc, x, w_all, xt, cst, wts):
    ident = cst["ident"]
    whi, wlo, raw = wts["hi"], wts["lo"], wts["raw"]
    s_raw, s_whi, s_wlo = wts["s_raw"], wts["s_hi"], wts["s_lo"]
    ctx = ExitStack()
    with ctx:
        def sb(name, shape, dt):
            return ctx.enter_context(nc.sbuf_tensor(name, shape, dt))

        def sem(name):
            return ctx.enter_context(nc.semaphore(name))

        QUARTERS = 4
        per = TILES // QUARTERS
        pairs = B // 2
        x_all = sb("x_all", [P, TILES, D], F32)
        bn = sb("bn1", [P, TILES, 6], F32)
        mv = sb("mv1", [P, TILES, 2], F32)
        tmp = sb("rs_tmp1", [P, 2, TILES], F32)
        rstd = sb("rstd1", [P, TILES], F32)
        xn = sb("xn1", [P, 2, D], F32)
        parts = [sb(f"parts{i}", [P, 2, CB, L], F32R) for i in range(2)]
        ps = [ctx.enter_context(nc.psum_tensor(f"n1ps{i}", [P, CB, P], F32)) for i in range(2)]

        s_x = [sem(f"n1_x{i}") for i in range(QUARTERS)]
        s_const = sem("n1_const")
        s_bn, s_mv, s_var = sem("n1_bn"), sem("n1_mv"), sem("n1_var")
        s_sqrt, s_step = sem("n1_sqrt"), sem("n1_step")
        s_xn, s_tr, s_hi, s_lo = sem("n1_xn"), sem("n1_tr"), sem("n1_hi"), sem("n1_lo")
        s_out = [sem(f"n1_out{i}") for i in range(2)]
        xv = x.rearrange("b (t p) d -> p (b t) d", p=P)
        block = ctx.enter_context(nc.Block())

        def tok(t):
            return slice(t * P, (t + 1) * P)

        @block.sync
        def _(sp):
            def load_x(i):
                sp.dma_start(x_all[:, i * per:(i + 1) * per, :], xv[:, i * per:(i + 1) * per, :]).then_inc(s_x[i], 16)

            def load_w(b, m):
                src = w_all[0, b] if isinstance(b, int) else w_all[0, bass.ds(b, 1)].rearrange("o p d -> (o p) d")
                sp.dma_start(raw[:, m, :], src).then_inc(s_raw[m], 16)

            load_x(0)
            load_w(0, 0)
            load_w(1, 1)
            for i in range(1, QUARTERS):
                load_x(i)

            def pair(j, more):
                for m in range(2):
                    b = 2 * j + m
                    sp.wait_ge(s_lo, 2 * b + 2)
                    dst = xt[b] if isinstance(b, int) else xt[bass.ds(b, 1)].rearrange("o p h c n -> (o p) h c n")
                    sp.dma_start(dst, parts[m][:, :, :, :].bitcast(F32)).then_inc(s_out[m], 16)
                    if more:
                        sp.wait_ge(s_wlo, b + 1)
                        load_w(b + 2, m)

            pair(0, True)
            with sp.Fori(1, pairs - 1) as j:
                pair(j, True)
            pair(pairs - 1, False)
            for m in range(2):
                sp.wait_ge(s_out[m], 16 * pairs)

        @block.gpsimd
        def _(pool):
            nc.gpsimd.memset(ident[:, :], 0.0).then_inc(s_const, 1)
            nc.gpsimd.memset(cst["identb"][:, :], 0.0).then_inc(s_const, 1)
            nc.gpsimd.memset(cst["mask"][:, :], 0.0).then_inc(s_const, 1)
            nc.gpsimd.memset(cst["ones"][:, :], 1.0).then_inc(s_const, 1)
            nc.gpsimd.memset(cst["tri"][:, :], 1.0).then_inc(s_const, 1)
            pool.wait_ge(s_const, 5)
            for m in (ident, cst["identb"]):
                nc.gpsimd.affine_select(out=m[:, :], in_=m[:, :], compare_op=ALU.not_equal, fill=1.0, base=0,
                                        pattern=[[-1, P]], channel_multiplier=1).then_inc(s_const, 1)
            nc.gpsimd.affine_select(out=cst["mask"][:, :], in_=cst["mask"][:, :], compare_op=ALU.is_ge, fill=MASKED,
                                    base=0, pattern=[[-1, P]], channel_multiplier=1).then_inc(s_const, 1)
            nc.gpsimd.affine_select(out=cst["tri"][:, :], in_=cst["tri"][:, :], compare_op=ALU.is_ge, fill=0.0,
                                    base=0, pattern=[[1, P]], channel_multiplier=-1).then_inc(s_const, 1)
            for c in range(NCH):
                pool.wait_ge(s_whi, c + 1)
                nc.gpsimd.tensor_tensor(wlo[:, c, :], raw[:, c % 2, :], whi[:, c, :].bitcast(F32),
                                        ALU.subtract).then_inc(s_wlo, 1)

        @block.vector
        def _(dve):
            def stats(t):
                nc.vector.bn_stats(bn[:, t, :], x_all[:, t, :]).then_inc(s_bn, 1)

            def normed(n):
                if n >= 2:
                    dve.wait_ge(s_tr, n - 1)
                nc.vector.tensor_scalar(xn[:, n % 2, :], x_all[:, n, :], mv[:, n, 0:1], rstd[:, n:n + 1],
                                        ALU.subtract, ALU.mult).then_inc(s_xn, 1)

            def rest(n):
                dve.wait_ge(s_hi, n + 1)
                m = n // 2 % 2
                nc.vector.tensor_tensor(parts[m][:, 1, :, tok(n % 2)], ps[n % 2][:, :, :],
                                        parts[m][:, 0, :, tok(n % 2)].bitcast(F32), ALU.subtract).then_inc(s_lo, 1)

            dve.wait_ge(s_x[0], 16)
            for t in range(per):
                stats(t)
            for i in range(QUARTERS):
                q = slice(i * per, (i + 1) * per)
                dve.wait_ge(s_bn, (i + 1) * per)
                for t in range(i * per, (i + 1) * per):
                    nc.vector.bn_aggr(mv[:, t, :], bn[:, t, :]).then_inc(s_mv, 1)
                dve.wait_ge(s_mv, (i + 1) * per)
                nc.vector.tensor_scalar(tmp[:, 0, q], mv[:, q, 1], EPS, None, ALU.add).then_inc(s_var, 1)
                rstd_of_all(nc, None, dve, rstd[:, q], tmp[:, :, q], s_var, s_sqrt, s_step, i)
                normed(i * per)
                normed(i * per + 1)
                if i + 1 < QUARTERS:
                    dve.wait_ge(s_x[i + 1], 16)
                for n in range(i * per, (i + 1) * per):
                    if n + 2 < (i + 1) * per:
                        normed(n + 2)
                    if i + 1 < QUARTERS:
                        stats(n + per)
                    rest(n)

        @block.scalar
        def _(act):
            def quarter(i):
                q = slice(0, per) if isinstance(i, int) else bass.ds(i * per, per)
                rstd_of_all(nc, act, None, rstd, tmp[:, :, q], s_var, s_sqrt, s_step, i)
                for k in range(per // 2):
                    b, m = i * (per // 2) + k, k % 2
                    if not (isinstance(b, int) and b < 2):
                        act.wait_ge(s_out[m], 8 * (b - m))
                    for t in range(TB):
                        act.wait_ge(s_tr, 2 * b + t + 1)
                        nc.scalar.activation(parts[m][:, 0, :, tok(t)], ps[t][:, :, :], ACT.Copy).then_inc(s_hi, 1)
                    act.wait_ge(s_raw[m], 8 * (b - m) + 16)
                    dst = whi[:, b, :] if isinstance(b, int) else whi[:, bass.ds(b, 1), :].rearrange("p o d -> p (o d)")
                    nc.scalar.activation(dst, raw[:, m, :], ACT.Copy).then_inc(s_whi, 1)

            turns(act, QUARTERS, quarter)

        @block.tensor
        def _(pe):
            pe.wait_ge(s_const, 9)

            def turn(b):
                for t in range(TB):
                    pe.wait_ge(s_xn, 2 * b + t + 1)
                    if not (isinstance(b, int) and b == 0):
                        pe.wait_ge(s_lo, 2 * b + t - 1)
                    for c in range(CB):
                        last = nc.tensor.transpose(ps[t][:, c, :], xn[:, t, c * P:(c + 1) * P], ident[:, :])
                    last.then_inc(s_tr, 1)

            turns(pe, B, turn)


def self_attention(nc, x, w_all, rope, xt, x1, mv2, cst, wts):
    ident, identb, mask = cst["ident"], cst["identb"], cst["mask"]
    ctx = ExitStack()
    with ctx:
        def sb(name, shape, dt):
            return ctx.enter_context(nc.sbuf_tensor(name, shape, dt))

        def pb(name):
            return ctx.enter_context(nc.psum_tensor(name, [P, 512], F32))

        def sem(name):
            return ctx.enter_context(nc.semaphore(name))

        whi = [wts["hi"], sb("whi1", [P, NCH, 512], F32R)]
        wlo = [wts["lo"], sb("wlo1", [P, NCH, 512], F32R)]
        raw = wts["raw"]
        s_raw, s_whi, s_wlo = wts["s_raw"], wts["s_hi"], wts["s_lo"]
        xnt = [sb(f"xnt{i}", [P, 2, CB, L], F32R) for i in range(2)]
        rot = [sb(f"rot{i}", [P, TB, GW], F32) for i in range(2)]
        swp = sb("swp", [P, 2, GW], F32)
        v_sb = [sb(f"v{i}", [P, TB, GW], F32) for i in range(2)]
        qkt = [sb(f"qkt{i}", [P, HG, L], F32) for i in range(2)]
        pr = sb("pr", [P, HG, KBLK * P], F32)
        prt = sb("prt", [P, HG, KBLK * P], F32)
        ohi = sb("ohi", [P, HG, L], F32R)
        olo = sb("olo", [P, HG, L], F32R)
        xio = sb("xio", [P, 2, TB, D], F32)
        trig = sb("trig", [P, TB, 3, HD // 2], F32)
        mx = sb("mx", [P, HG, TB], F32)
        nmx = sb("nmx", [P, HG, TB], F32)
        rsum = sb("rsum", [P, HG, TB], F32)
        rinv = sb("rinv", [P, HG, TB], F32)
        bn = sb("bn2", [P, TB, 6], F32)
        agg = sb("agg2", [P, TB, 2], F32)
        hold = sb("hold2", [P, 1], F32)

        PJ = [pb("pj0"), pb("pj1")]
        TR = [pb("tr0"), pb("tr1")]
        SC = [pb("sc0"), pb("sc1")]
        OB = [pb("ob0"), pb("ob1")]

        s_trig = sem("a_trig")
        s_xn = [sem(f"a_xn{i}") for i in range(2)]
        s_xi = [sem(f"a_xi{i}") for i in range(2)]
        s_xo = [sem(f"a_xo{i}") for i in range(2)]
        s_proj = sem("a_proj")
        s_mul = sem("a_mul")
        s_swp = sem("a_swp")
        s_vev = sem("a_vev")
        s_qkt = sem("a_qkt")
        s_qke = sem("a_qke")
        s_sc = sem("a_sc")
        s_mx, s_nmx = sem("a_mx"), sem("a_nmx")
        s_exp = sem("a_exp")
        s_ri, s_pr = sem("a_ri"), sem("a_pr")
        s_pt = sem("a_pt")
        s_pte = sem("a_pte")
        s_pv = sem("a_pv")
        s_ohi, s_olo = sem("a_ohi"), sem("a_olo")
        s_wo = sem("a_wo")
        s_x1 = [sem(f"a_x1{i}") for i in range(TB)]
        s_bn, s_mv = sem("a_bn"), sem("a_mv")
        block = ctx.enter_context(nc.Block())

        xv = x.rearrange("b (t p) d -> b p t d", p=P)
        ITEMS = G * B

        def items(eng, item, ahead=True):
            for g in range(G):
                if g == 0:
                    item(0, 0, 0, 0, 0, True)
                    item(1, 0, 1, 1, 0, True)
                with eng.Fori(1 if g == 0 else 0, B // 2 - 1) as j:
                    for par in range(2):
                        item(2 * j + (g * B + par), g, 2 * j + par, par, g, True)
                item(g * B + B - 2, g, B - 2, 0, g, True)
                item(g * B + B - 1, g, B - 1, 1, g + 1, g + 1 < G)

        def one(ap, i):
            return ap[bass.ds(i, 1)].rearrange("o p a d -> (o p) a d") if not isinstance(i, int) else ap[i]

        @block.sync
        def _(sp):
            sp.dma_start(trig[:, :, :, :], rope).then_inc(s_trig, 16)
            for m in range(2):
                sp.dma_start(xnt[m][:, :, :, :].bitcast(F32), xt[m]).then_inc(s_xn[m], 16)

            def item(n, g, b, par, gn, more):
                half = (n - par) // 2 if isinstance(n, int) else None
                stored = 16 * half if half is not None else 8 * (n - par)
                sp.wait_ge(s_xo[par], stored)
                src = (xv if g == 0 else x1)
                src = src[b] if isinstance(b, int) else src[bass.ds(b, 1)].rearrange("o p t d -> (o p) t d")
                sp.dma_start(xio[:, par, :, :], src).then_inc(s_xi[par], 16)
                if g + 1 < G:
                    sp.wait_ge(s_wlo, n + (NCH - 1))
                    wsrc = w_all[g + 1, b] if isinstance(b, int) else w_all[g + 1, bass.ds(b, 1)].rearrange("o p d -> (o p) d")
                    sp.dma_start(raw[:, par, :], wsrc).then_inc(s_raw[par], 16)
                if isinstance(b, int):
                    b2, there = (b + 2) % B, g + (b + 2) // B < G
                else:
                    b2, there = b + 2, True
                if there:
                    sp.wait_ge(s_proj, 6 * n + 6)
                    xsrc = xt[b2] if isinstance(b2, int) else xt[bass.ds(b2, 1)].rearrange("o p h c n -> (o p) h c n")
                    sp.dma_start(xnt[par][:, :, :, :].bitcast(F32), xsrc).then_inc(s_xn[par], 16)
                for t in range(TB):
                    sp.wait_ge(s_x1[t], n + 1)
                dst = x1[b] if isinstance(b, int) else x1[bass.ds(b, 1)].rearrange("o p t d -> (o p) t d")
                sp.dma_start(dst, xio[:, par, :, :]).then_inc(s_xo[par], 16)

            items(sp, item)
            for par in range(2):
                sp.wait_ge(s_xo[par], 16 * ITEMS // 2)

        @block.gpsimd
        def _(pool):
            def rotate(m):
                for i in range(4):
                    pool.wait_ge(s_mul, 4 * m + i + 1)
                    r = rot[i // 2][:, i % 2, :]
                    nc.gpsimd.tensor_tensor(r, r, swp[:, i % 2, :], ALU.add).then_inc(s_swp, 1)

            rotate(0)
            items(pool, lambda n, g, b, par, gn, more: rotate(n + 1) if more else None)

        @block.tensor
        def _(pe):
            def project(bank, m, gn, par, kind, t):
                k = 0
                for c in range(CB):
                    tok = slice(t * P, (t + 1) * P)
                    for xpart, w in ((0, whi), (0, wlo), (1, whi)):
                        last = nc.tensor.matmul(bank[:, :], xnt[par][:, xpart, c, tok], w[gn % 2][:, kind + c, :],
                                                start=(k == 0), stop=(k == 3 * CB - 1))
                        k += 1
                last.then_inc(s_proj, 1)

            def xn_here(m, par):
                if isinstance(m, int):
                    pe.wait_ge(s_xn[par], 16 * (m // 2 + 1))
                else:
                    pe.wait_ge(s_xn[par], 8 * (m - par) + 16)

            pe.wait_ge(s_wlo, NCH)
            xn_here(0, 0)
            project(PJ[0], 0, 0, 0, CH_Q, 0)
            project(PJ[1], 0, 0, 0, CH_Q, 1)
            pe.wait_ge(s_mul, 1)
            project(PJ[0], 0, 0, 0, CH_K, 0)
            pe.wait_ge(s_mul, 2)
            project(PJ[1], 0, 0, 0, CH_K, 1)
            pe.wait_ge(s_mul, 3)
            project(PJ[0], 0, 0, 0, CH_V, 0)
            pe.wait_ge(s_mul, 4)
            project(PJ[1], 0, 0, 0, CH_V, 1)

            def item(n, g, b, par, gn, more):
                m, mp = n + 1, 1 - par

                def transposes(i):
                    src, h0 = rot[i % 2], 2 * (i // 2)
                    for h in range(2):
                        for t in range(TB):
                            last = nc.tensor.transpose(TR[i % 2][:, (h * TB + t) * P:(h * TB + t + 1) * P],
                                                       src[:, t, (h0 + h) * HD:(h0 + h + 1) * HD], ident[:, :])
                    last.then_inc(s_qkt, 1)

                def scores(h):
                    bank = SC[h % 2]
                    qT, kT = qkt[0][:, h, :], qkt[1][:, h, :]
                    nc.tensor.matmul(bank[:, 0:P], qT[:, 0:P], kT[:, 0:P], start=True, stop=False)
                    nc.tensor.matmul(bank[:, 0:P], identb[:, :], mask[:, :], start=False, stop=True)
                    nc.tensor.matmul(bank[:, P:3 * P], qT[:, P:2 * P], kT[:, 0:2 * P], start=True, stop=False)
                    nc.tensor.matmul(bank[:, 2 * P:3 * P], identb[:, :], mask[:, :], start=False,
                                     stop=True).then_inc(s_sc, 1)

                def prob_transposes(h):
                    for k in range(KBLK):
                        last = nc.tensor.transpose(TR[h % 2][:, k * P:(k + 1) * P], pr[:, h, k * P:(k + 1) * P],
                                                   ident[:, :])
                    last.then_inc(s_pt, 1)

                def weigh(h):
                    bank, o = OB[h // 2], (h % 2) * L
                    hd = slice(h * HD, (h + 1) * HD)
                    nc.tensor.matmul(bank[:, o:o + L], v_sb[par][:, 0, hd], prt[:, h, 0:2 * P], start=True, stop=False)
                    last = nc.tensor.matmul(bank[:, o + P:o + L], v_sb[par][:, 1, hd], prt[:, h, 2 * P:3 * P],
                                            start=False, stop=True)
                    if h % 2:
                        last.then_inc(s_pv, 1)

                pe.wait_ge(s_swp, 4 * n + 4)
                pe.wait_ge(s_pte, 4 * n)
                transposes(0)
                transposes(1)
                if more:
                    xn_here(m, mp)
                    pe.wait_ge(s_wlo, gn * NCH + 3 * CB)
                    pe.wait_ge(s_vev, 2 * n + 2)
                    pe.wait_ge(s_x1[0], n)
                    project(PJ[0], m, gn, mp, CH_Q, 0)
                pe.wait_ge(s_qke, 4 * n + 1)
                transposes(2)
                pe.wait_ge(s_qke, 4 * n + 2)
                transposes(3)
                pe.wait_ge(s_exp, 8 * n)
                scores(0)
                scores(1)
                if more:
                    pe.wait_ge(s_x1[1], n)
                    project(PJ[1], m, gn, mp, CH_Q, 1)
                    pe.wait_ge(s_mul, 4 * m + 1)
                    project(PJ[0], m, gn, mp, CH_K, 0)
                pe.wait_ge(s_qke, 4 * n + 4)
                pe.wait_ge(s_exp, 8 * n + 4)
                scores(2)
                scores(3)
                pe.wait_ge(s_pr, 8 * n + 4)
                prob_transposes(0)
                prob_transposes(1)
                if more:
                    pe.wait_ge(s_mul, 4 * m + 2)
                    project(PJ[1], m, gn, mp, CH_K, 1)
                    pe.wait_ge(s_mul, 4 * m + 3)
                    project(PJ[0], m, gn, mp, CH_V, 0)
                pe.wait_ge(s_pr, 8 * n + 8)
                pe.wait_ge(s_pte, 4 * n + 1)
                prob_transposes(2)
                pe.wait_ge(s_pte, 4 * n + 2)
                prob_transposes(3)
                pe.wait_ge(s_vev, 2 * n + 2)
                pe.wait_ge(s_olo, 2 * n)
                weigh(0)
                weigh(1)
                if more:
                    pe.wait_ge(s_mul, 4 * m + 4)
                    project(PJ[1], m, gn, mp, CH_V, 1)
                pe.wait_ge(s_pte, 4 * n + 4)
                weigh(2)
                weigh(3)
                pe.wait_ge(s_wlo, (g + 1) * NCH)
                for half in range(2):
                    pe.wait_ge(s_olo, 2 * n + half + 1)
                    for t in range(TB):
                        if half == 0 and more:
                            pe.wait_ge(s_vev, 2 * m + t + 1)
                        elif half == 0:
                            pe.wait_ge(s_vev, 2 * n + 2)
                        for h in (2 * half, 2 * half + 1):
                            tok = slice(t * P, (t + 1) * P)
                            for k, (o, w) in enumerate(((ohi, whi), (ohi, wlo), (olo, whi))):
                                last = nc.tensor.matmul(PJ[t][:, :], o[:, h, tok], w[g % 2][:, CH_O + h, :],
                                                        start=(h == 0 and k == 0), stop=(h == HG - 1 and k == 2))
                        if half:
                            last.then_inc(s_wo, 1)

            items(pe, item)

        @block.scalar
        def _(act):
            def w_chunk(c, total, dst, par):
                act.wait_ge(s_raw[par], 8 * (total - par + 1))
                out = whi[dst][:, c, :] if isinstance(c, int) else whi[dst][:, bass.ds(c, 1), :].rearrange("p o d -> p (o d)")
                nc.scalar.activation(out, raw[:, par, :], ACT.Copy).then_inc(s_whi, 1)

            def v_evac(m, mp, t):
                act.wait_ge(s_proj, 6 * m + 5 + t)
                nc.scalar.activation(v_sb[mp][:, t, :], PJ[t][:, :], ACT.Copy).then_inc(s_vev, 1)

            v_evac(0, 0, 0)
            v_evac(0, 0, 1)

            def item(n, g, b, par, gn, more):
                m, mp = n + 1, 1 - par

                def qk_evac(i):
                    act.wait_ge(s_qkt, 4 * n + i + 1)
                    h0 = 2 * (i // 2)
                    nc.scalar.activation(qkt[i % 2][:, h0:h0 + 2, :].rearrange("p h n -> p (h n)"), TR[i % 2][:, :],
                                         ACT.Copy).then_inc(s_qke, 1)

                def exps(pair):
                    act.wait_ge(s_nmx, 2 * n + pair + 1)
                    for h in (2 * pair, 2 * pair + 1):
                        for t in range(TB):
                            lo, hi = (0, P) if t == 0 else (P, 3 * P)
                            nc.scalar.activation(pr[:, h, lo:hi], SC[h % 2][:, lo:hi], ACT.Exp,
                                                 bias=nmx[:, h, t:t + 1], scale=SCALE,
                                                 accum_out=rsum[:, h, t:t + 1]).then_inc(s_exp, 1)

                def pt_evac(h):
                    act.wait_ge(s_pt, 4 * n + h + 1)
                    nc.scalar.activation(prt[:, h, :], TR[h % 2][:, 0:KBLK * P], ACT.Copy).then_inc(s_pte, 1)

                def o_round(pair):
                    act.wait_ge(s_pv, 2 * n + pair + 1)
                    nc.scalar.activation(ohi[:, 2 * pair:2 * pair + 2, :].rearrange("p h n -> p (h n)"), OB[pair][:, :],
                                         ACT.Copy).then_inc(s_ohi, 1)

                act.wait_ge(s_sc, 4 * n)
                qk_evac(0)
                qk_evac(1)
                qk_evac(2)
                qk_evac(3)
                if g + 1 < G:
                    act.wait_ge(s_wo, 2 * B * g)
                    w_chunk(b, n + (NCH + 1), (g + 1) % 2, par)
                act.wait_ge(s_pt, 4 * n)
                exps(0)
                exps(1)
                act.wait_ge(s_pv, 2 * n)
                pt_evac(0)
                pt_evac(1)
                if more:
                    act.wait_ge(s_pv, 2 * n)
                    v_evac(m, mp, 0)
                pt_evac(2)
                pt_evac(3)
                act.wait_ge(s_wo, 2 * n)
                o_round(0)
                if more:
                    v_evac(m, mp, 1)
                o_round(1)

            items(act, item)

        @block.vector
        def _(dve):
            def w_chunk(c, total, dst):
                dve.wait_ge(s_whi, total)
                par_c = (lambda a: a[:, c, :] if isinstance(c, int) else a[:, bass.ds(c, 1), :].rearrange("p o d -> p (o d)"))
                return par_c(whi[dst]), par_c(wlo[dst])

            def rope_mul(m, i):
                t = i % 2
                dve.wait_ge(s_proj, 6 * m + i + 1)
                half = HD // 2
                r = rot[i // 2][:, t, :].rearrange("p (h s d) -> p h s d", h=HG, s=2)
                s = swp[:, t, :].rearrange("p (h d) -> p h d", h=HG)
                bank = PJ[t][:, :].rearrange("p (h d) -> p h d", h=HG)
                nc.vector.tensor_tensor(r, bank.rearrange("p h (s d) -> p h s d", s=2),
                                        trig[:, t, 0, :].unsqueeze(1).unsqueeze(1).broadcast_to([P, HG, 2, half]),
                                        ALU.mult)
                for k, (lo, hi) in enumerate(((0, half), (half, HD))):
                    src = bank[:, :, half - lo:half - lo + half]
                    last = nc.vector.tensor_tensor(s[:, :, lo:hi], src,
                                                   trig[:, t, 1 + k, :].unsqueeze(1).broadcast_to([P, HG, half]),
                                                   ALU.mult)
                last.then_inc(s_mul, 1)

            dve.wait_ge(s_trig, 16)
            for i in range(4):
                if i >= 2:
                    dve.wait_ge(s_swp, i - 1)
                rope_mul(0, i)

            def item(n, g, b, par, gn, more):
                m = n + 1

                def maxima(pair):
                    for h in (2 * pair, 2 * pair + 1):
                        dve.wait_ge(s_sc, 4 * n + h + 1)
                        for t in range(TB):
                            lo, hi = (0, P) if t == 0 else (P, 3 * P)
                            nc.vector.reduce_max(mx[:, h, t:t + 1], SC[h % 2][:, lo:hi], AX.X).then_inc(s_mx, 1)
                    dve.wait_ge(s_mx, 8 * n + 4 * pair + 4)
                    pr2 = slice(2 * pair, 2 * pair + 2)
                    nc.vector.tensor_scalar(nmx[:, pr2, :].rearrange("p h t -> p (h t)"),
                                            mx[:, pr2, :].rearrange("p h t -> p (h t)"), -SCALE, None,
                                            ALU.mult).then_inc(s_nmx, 1)

                def normalise(pair):
                    pr2 = slice(2 * pair, 2 * pair + 2)
                    dve.wait_ge(s_exp, 8 * n + 4 * pair + 4)
                    nc.vector.reciprocal(rinv[:, pr2, :].rearrange("p h t -> p (h t)"),
                                         rsum[:, pr2, :].rearrange("p h t -> p (h t)")).then_inc(s_ri, 1)
                    dve.wait_ge(s_ri, 2 * n + pair + 1)
                    for h in (2 * pair, 2 * pair + 1):
                        for t in range(TB):
                            lo, hi = (0, P) if t == 0 else (P, 3 * P)
                            nc.vector.tensor_scalar(pr[:, h, lo:hi], pr[:, h, lo:hi], rinv[:, h, t:t + 1], None,
                                                    ALU.mult).then_inc(s_pr, 1)

                def rope(i):
                    if more:
                        dve.wait_ge(s_swp, 4 * m + i - 1)
                        dve.wait_ge(s_qkt, 4 * n + 4)
                        rope_mul(m, i)

                rope(0)
                if g + 1 < G:
                    dve.wait_ge(s_wo, 2 * B * g)
                    hi, lo = w_chunk(b, n + (NCH + 1), (g + 1) % 2)
                    nc.vector.tensor_tensor(lo, raw[:, par, :], hi.bitcast(F32), ALU.subtract).then_inc(s_wlo, 1)
                maxima(0)
                rope(1)
                normalise(0)
                rope(2)
                maxima(1)
                rope(3)
                normalise(1)
                dve.wait_ge(s_wo, 2 * n)
                for pair in range(2):
                    dve.wait_ge(s_ohi, 2 * n + pair + 1)
                    nc.vector.tensor_tensor(olo[:, 2 * pair:2 * pair + 2, :].rearrange("p h n -> p (h n)"), OB[pair][:, :],
                                            ohi[:, 2 * pair:2 * pair + 2, :].rearrange("p h n -> p (h n)").bitcast(F32),
                                            ALU.subtract).then_inc(s_olo, 1)
                if isinstance(n, int):
                    dve.wait_ge(s_xi[par], 16 * (n // 2 + 1))
                else:
                    dve.wait_ge(s_xi[par], 8 * (n - par) + 16)
                for t in range(TB):
                    dve.wait_ge(s_wo, 2 * n + t + 1)
                    nc.vector.tensor_tensor(xio[:, par, t, :], PJ[t][:, :], xio[:, par, t, :], ALU.add).then_inc(s_x1[t], 1)
                if g == G - 1:
                    k = n - g * B
                    for t in range(TB):
                        dve.wait_ge(s_x1[t], n + 1)
                        dve.wait_ge(s_mv, 2 * k)
                        nc.vector.bn_stats(bn[:, t, :], xio[:, par, t, :]).then_inc(s_bn, 1)
                        dve.wait_ge(s_bn, 4 * k + 2 * t + 1)
                        dst = mv2[:, 2 * b + t, :] if isinstance(b, int) else mv2[:, bass.ds(2 * b + t, 1), :].rearrange("p o d -> p (o d)")
                        nc.vector.memset(hold[:, :], 0.0)
                        nc.vector.bn_aggr(agg[:, t, :], bn[:, t, :]).then_inc(s_bn, 1)
                        dve.wait_ge(s_bn, 4 * k + 2 * t + 2)
                        nc.vector.tensor_copy(dst, agg[:, t, :]).then_inc(s_mv, 1)

            items(dve, item)
            dve.wait_ge(s_mv, 2 * B)


def cross_attention(nc, x1, ctx_in, gamma, sq, sk, mv2, mv3, x2, cst):
    ident = cst["ident"]
    ctx = ExitStack()
    with ctx:
        def sb(name, shape, dt):
            return ctx.enter_context(nc.sbuf_tensor(name, shape, dt))

        def pb(name):
            return ctx.enter_context(nc.psum_tensor(name, [P, 512], F32))

        def sem(name):
            return ctx.enter_context(nc.semaphore(name))

        gam = sb("gam", [P, 1], F32)
        tmp = sb("rs_tmp2", [P, 2, TILES], F32)
        rstd = sb("rstd2", [P, TILES], F32)
        cin = sb("cin", [P, 2, D], F32)
        xn = sb("xn2", [P, D], F32)
        qp = sb("qp", [P, 2, D], F32R)
        kp = sb("kp", [P, 2, D], F32R)
        qst = [sb(f"qst{i}", [P, XPT, D], F32R) for i in range(2)]
        kst = [sb(f"kst{i}", [P, XPT, D], F32R) for i in range(2)]
        vt = sb("vt", [P, 2, CB, P], F32)
        pr = sb("xpr", [P, 2, CB, D], F32)
        prt = [sb(f"xprt{i}", [P, XPT, CB, D], F32) for i in range(2)]
        nmx = sb("xnmx", [P, 2, CB], F32)
        rsum = sb("xrsum", [P, 2, CB, XPT], F32)
        rinv = sb("xrinv", [P, 2, CB, XPT], F32)
        rbc = sb("xrbc", [P, D], F32)
        onm = sb("xonm", [P, D], F32)
        bn = sb("bn3", [P, 6], F32)
        agg = sb("agg3", [P, 2], F32)
        hold = sb("hold3", [P, 1], F32)
        SC = [pb(f"xsc{i}") for i in range(CB)]
        TR = [pb(f"xtr{i}") for i in range(2)]
        OB = pb("xob")
        VB = pb("xvb")

        s_gam, s_var, s_sqrt, s_step = sem("x_gam"), sem("x_var"), sem("x_sqrt"), sem("x_step")
        s_xi = [sem(f"x_xi{i}") for i in range(2)]
        s_ci = [sem(f"x_ci{i}") for i in range(2)]
        s_qn, s_qlo = sem("x_qn"), sem("x_qlo")
        s_khi, s_klo = sem("x_khi"), sem("x_klo")
        s_qw, s_kw = sem("x_qw"), sem("x_kw")
        s_st = [sem(f"x_st{i}") for i in range(2)]
        s_vt, s_vte = sem("x_vt"), sem("x_vte")
        s_sc = sem("x_sc")
        s_mx = sem("x_mx")
        s_exp = sem("x_exp")
        s_ri = sem("x_ri")
        s_rb, s_rbe = sem("x_rb"), sem("x_rbe")
        s_on = sem("x_on")
        s_pt = sem("x_pt")
        s_pta, s_ptd = sem("x_pta"), sem("x_ptd")
        s_pv = sem("x_pv")
        s_x2 = sem("x_x2")
        s_bn, s_mv = sem("x_bn"), sem("x_mv")
        block = ctx.enter_context(nc.Block())

        cv = ctx_in.rearrange("b (t p) d -> (b t) p d", p=P)
        x1v = x1.rearrange("b p t d -> b t p d")

        def col(ap, n):
            return ap[:, n, :] if isinstance(n, int) else ap[:, bass.ds(n, 1), :].rearrange("p o d -> p (o d)")

        def all_tiles(eng, item):
            item(0, 0, True, True, True)
            item(1, 1, False, True, True)
            with eng.Fori(1, TILES // 2 - 1) as i:
                for t in range(2):
                    item(2 * i + t, t, False, True, True)
            item(TILES - 2, 0, False, True, False)
            item(TILES - 1, 1, False, False, False)

        def loads(n, t):
            return 16 * (n // 2 + 1) if isinstance(n, int) else 8 * (n - t) + 16

        @block.sync
        def _(sp):
            sp.dma_start(gam[:, :], gamma.rearrange("(a b) -> a b", a=1).broadcast_to([P, 1])).then_inc(s_gam, 16)

            def load(n, t, b=None):
                dst = x2[:, n, :] if isinstance(n, int) else x2[:, bass.ds(n, 1), :].rearrange("p o d -> p (o d)")
                if isinstance(n, int):
                    src, csrc = x1v[n // 2, t], cv[n]
                else:
                    src = x1v[bass.ds(b, 1), t].rearrange("o p d -> (o p) d")
                    csrc = cv[bass.ds(n, 1)].rearrange("o p d -> (o p) d")
                sp.dma_start(dst, src).then_inc(s_xi[t], 16)
                sp.dma_start(cin[:, t, :], csrc).then_inc(s_ci[t], 16)

            def write_parts(count, t):
                sp.dma_start(sq[t].rearrange("h p d -> p h d"), qp[:, :, :].bitcast(F32)).then_inc(s_qw, 16)
                sp.wait_ge(s_klo, count)
                sp.dma_start(sk[t].rearrange("h p d -> p h d"), kp[:, :, :].bitcast(F32)).then_inc(s_kw, 16)

            def read_stacks(n, t):
                sp.wait_ge(s_qw, 16 * n + 16)
                sp.wait_ge(s_kw, 16 * n + 16)
                qv = sq[t].rearrange("h (j r) d -> h r j d", j=XPT)
                kv = sk[t].rearrange("h (j r) d -> h r j d", j=XPT)
                for c in range(4):
                    rows = slice(XD * c, XD * (c + 1))
                    sp.dma_start(qst[t][rows, :, :].bitcast(F32), qv[c // 2]).then_inc(s_st[t], 16)
                    sp.dma_start(kst[t][rows, :, :].bitcast(F32), kv[c % 2]).then_inc(s_st[t], 16)

            for t in range(2):
                load(t, t)
            for t in range(2):
                sp.wait_ge(s_qlo, t + 1)
                write_parts(t + 1, t)
                read_stacks(t, t)

            def item(n, t, first, more, more2):
                if more2:
                    b = None if isinstance(n, int) else sp.snap((n - t) // 2 + 1)
                    sp.wait_ge(s_vt, n + 1)
                    sp.wait_ge(s_klo, n + 1)
                    load(n + 2, t, b)
                    sp.wait_ge(s_qlo, n + 3)
                    sp.wait_ge(s_st[t], 128 * (n // 2 + 1) if isinstance(n, int) else 64 * (n - t) + 128)
                    write_parts(n + 3, t)
                    sp.wait_ge(s_sc, 16 * n + 16)
                    read_stacks(n + 2, t)

            all_tiles(sp, item)

        @block.gpsimd
        def _(pool):
            def split(n, t):
                pool.wait_ge(s_ci[t], loads(n, t))
                pool.wait_ge(s_kw, 16 * n)
                pool.wait_ge(s_qn, 2 * n + 2)
                pool.wait_ge(s_qw, 16 * n)
                nc.gpsimd.tensor_tensor(qp[:, 1, :], xn[:, :], qp[:, 0, :].bitcast(F32),
                                        ALU.subtract).then_inc(s_qlo, 1)
                nc.gpsimd.tensor_copy(kp[:, 0, :], cin[:, t, :]).then_inc(s_khi, 1)
                pool.wait_ge(s_khi, n + 1)
                nc.gpsimd.tensor_tensor(kp[:, 1, :], cin[:, t, :], kp[:, 0, :].bitcast(F32),
                                        ALU.subtract).then_inc(s_klo, 1)

            for t in range(2):
                split(t, t)

            def item(n, t, first, more, more2):
                if more2:
                    split(n + 2, t)

            all_tiles(pool, item)

        @block.tensor
        def _(pe):
            def scores(n, t, h, banks=range(CB)):
                for q in banks:
                    if not (isinstance(n, int) and n == 0 and h == 0):
                        pe.wait_ge(s_exp, 16 * n + 4 * h - 3 + q)
                    nc.tensor.matmul(SC[q][:, :], qst[t][:, h, q * P:(q + 1) * P], kst[t][:, h, :],
                                     start=True, stop=True).then_inc(s_sc, 1)

            def stacks_here(n, t):
                pe.wait_ge(s_st[t], 128 * (n // 2 + 1) if isinstance(n, int) else 64 * (n - t) + 128)

            def output(n, t):
                pe.wait_ge(s_pta, 8 * n + 8)
                pe.wait_ge(s_ptd, 8 * n + 8)
                pe.wait_ge(s_vte, n + 1)
                pe.wait_ge(s_on, n)
                for c in range(CB):
                    for h in range(XPT):
                        last = nc.tensor.matmul(OB[XD * h:XD * (h + 1), :], vt[:, t, c, XD * h:XD * (h + 1)],
                                                prt[t][:, h, c, :], start=(c == 0), stop=(c == CB - 1))
                last.then_inc(s_pv, 1)
                pe.wait_ge(s_ri, n + 1)
                for q in range(CB):
                    for h in range(XPT):
                        last = nc.tensor.matmul(VB[XD * h:XD * (h + 1), q * P:(q + 1) * P],
                                                rinv[:, t, q, h:h + 1].broadcast_to([P, XD]), ident[:, :],
                                                start=True, stop=True)
                last.then_inc(s_rb, 1)

            stacks_here(0, 0)
            scores(0, 0, 0)

            def item(n, t, first, more, more2):
                pe.wait_ge(s_ci[t], loads(n, t))
                pe.wait_ge(s_vte, n)
                if not first:
                    pe.wait_ge(s_rbe, n - 1)
                for c in range(CB):
                    last = nc.tensor.transpose(VB[:, c * P:(c + 1) * P], cin[:, t, c * P:(c + 1) * P], ident[:, :])
                last.then_inc(s_vt, 1)
                for h in range(XPT):
                    def next_scores(banks):
                        if h + 1 < XPT:
                            scores(n, t, h + 1, banks)
                        elif more:
                            scores(n + 1, 1 - t, 0, banks)

                    def prob_transposes(c):
                        pe.wait_ge((s_pta, s_ptd)[c % 2], 8 * n + 2 * h + c // 2)
                        for q in range(CB):
                            last = nc.tensor.transpose(TR[c % 2][:, q * P:(q + 1) * P],
                                                       pr[:, h % 2, q, c * P:(c + 1) * P], ident[:, :])
                        last.then_inc(s_pt, 1)

                    if h + 1 == XPT and more:
                        stacks_here(n + 1, 1 - t)
                    next_scores([0])
                    next_scores([1])
                    pe.wait_ge(s_exp, 16 * n + 4 * h + 4)
                    prob_transposes(0)
                    prob_transposes(1)
                    next_scores([2, 3])
                    prob_transposes(2)
                    prob_transposes(3)
                    if h == 0 and not first:
                        output(n - 1, 1 - t)

            all_tiles(pe, item)
            output(TILES - 1, 1)

        @block.scalar
        def _(act):
            rstd_of_all(nc, act, None, rstd, tmp, s_var, s_sqrt, s_step, scale=XSCALE)

            def exps(n, t, h, banks=range(CB)):
                if not (isinstance(n, int) and n == 0 and h == 0):
                    act.wait_ge(s_pt, 16 * n + 4 * h - 4)
                for q in banks:
                    act.wait_ge(s_mx, 16 * n + 4 * h + q + 1)
                    nc.scalar.activation(pr[:, h % 2, q, :], SC[q][:, :], ACT.Exp, bias=nmx[:, h % 2, q:q + 1],
                                         accum_out=rsum[:, t, q, h:h + 1]).then_inc(s_exp, 1)

            exps(0, 0, 0)

            def item(n, t, first, more, more2):
                act.wait_ge(s_vt, n + 1)
                if not first:
                    act.wait_ge(s_pv, n - 1)
                nc.scalar.activation(vt[:, t, :, :].rearrange("p c n -> p (c n)"), VB[:, :], ACT.Copy).then_inc(s_vte, 1)
                for h in range(XPT):
                    for c in (0, 2):
                        if h + 1 < XPT:
                            exps(n, t, h + 1, (c, c + 1))
                        elif more:
                            exps(n + 1, 1 - t, 0, (c, c + 1))
                        act.wait_ge(s_pt, 16 * n + 4 * h + c + 1)
                        nc.scalar.activation(prt[t][:, h, c, :], TR[0][:, :], ACT.Copy).then_inc(s_pta, 1)
                    if h == 0 and not first:
                        sums_evac(n - 1)

            def sums_evac(n):
                act.wait_ge(s_rb, n + 1)
                act.wait_ge(s_on, n)
                nc.scalar.activation(rbc[:, :], VB[:, :], ACT.Copy).then_inc(s_rbe, 1)

            all_tiles(act, item)
            sums_evac(TILES - 1)

        @block.vector
        def _(dve):
            nc.vector.tensor_scalar(tmp[:, 0, :], mv2[:, :, 1], EPS, None, ALU.add).then_inc(s_var, 1)
            dve.wait_ge(s_var, 1)
            rstd_of_all(nc, None, dve, rstd[:, :], tmp, s_var, s_sqrt, s_step, scale=XSCALE)
            dve.wait_ge(s_gam, 16)

            def normed(n, t, parts=(0, 1)):
                if 0 in parts:
                    dve.wait_ge(s_xi[t], loads(n, t))
                    dve.wait_ge(s_qlo, n)
                    dve.wait_ge(s_qw, 16 * n)
                i = slice(n, n + 1) if isinstance(n, int) else bass.ds(n, 1)
                for out in [(xn[:, :], qp[:, 0, :])[k] for k in parts]:
                    nc.vector.tensor_scalar(out, col(x2, n), mv2[:, i, 0], rstd[:, i],
                                            ALU.subtract, ALU.mult).then_inc(s_qn, 1)

            def maxima(n, h, banks=range(CB)):
                for q in banks:
                    dve.wait_ge(s_sc, 16 * n + 4 * h + q + 1)
                    nc.vector.tensor_reduce(nmx[:, h % 2, q:q + 1], SC[q][:, :], AX.X, ALU.max,
                                            negate=True).then_inc(s_mx, 1)

            def output(n):
                dve.wait_ge(s_rbe, n + 1)
                nc.vector.tensor_tensor(onm[:, :], OB[:, :], rbc[:, :], ALU.mult).then_inc(s_on, 1)

            def residual(n):
                dve.wait_ge(s_on, n + 1)
                nc.vector.scalar_tensor_tensor(col(x2, n), onm[:, :], gam[:, 0:1], col(x2, n), ALU.mult,
                                               ALU.add).then_inc(s_x2, 1)

            def statistics(n):
                dve.wait_ge(s_x2, n + 1)
                dve.wait_ge(s_mv, n)
                nc.vector.memset(hold[:, :], 0.0)
                nc.vector.bn_stats(bn[:, :], col(x2, n)).then_inc(s_bn, 1)

            def mean_and_variance(n):
                dve.wait_ge(s_bn, 2 * n + 1)
                nc.vector.memset(hold[:, :], 0.0)
                nc.vector.bn_aggr(agg[:, :], bn[:, :]).then_inc(s_bn, 1)

            def keep_statistics(n):
                dve.wait_ge(s_bn, 2 * n + 2)
                nc.vector.tensor_copy(col(mv3, n), agg[:, :]).then_inc(s_mv, 1)

            def between(n, t, h, k, first, more2):
                if not first and (h, k) == (1, 0):
                    output(n - 1)
                if not first and (h, k) == (1, 1):
                    residual(n - 1)
                if not first and (h, k) == (2, 0):
                    statistics(n - 1)
                if not first and (h, k) == (2, 1):
                    mean_and_variance(n - 1)
                if not first and (h, k) == (3, 0):
                    keep_statistics(n - 1)
                if more2 and (h, k) == (2, 1):
                    normed(n + 2, t, [0])
                if more2 and (h, k) == (3, 0):
                    normed(n + 2, t, [1])

            for t in range(2):
                normed(t, t)
            maxima(0, 0)

            def item(n, t, first, more, more2):
                for h in range(XPT):
                    for c in (1, 3):
                        if h + 1 < XPT:
                            maxima(n, h + 1, (c - 1, c))
                        elif more:
                            maxima(n + 1, 0, (c - 1, c))
                        between(n, t, h, c // 2, first, more2)
                        dve.wait_ge(s_pt, 16 * n + 4 * h + c + 1)
                        nc.vector.tensor_copy(prt[t][:, h, c, :], TR[1][:, :]).then_inc(s_ptd, 1)
                dve.wait_ge(s_exp, 16 * n + 16)
                nc.vector.reciprocal(rinv[:, t, :, :].rearrange("p q h -> p (q h)"),
                                     rsum[:, t, :, :].rearrange("p q h -> p (q h)")).then_inc(s_ri, 1)

            all_tiles(dve, item)
            for finish in (output, residual, statistics, mean_and_variance, keep_statistics):
                finish(TILES - 1)
            dve.wait_ge(s_mv, TILES)


def expert_mix(nc, router_w, router_b, expert_w, expert_b, mv3, x2, out, cst):
    ident, tri, ones = cst["ident"], cst["tri"], cst["ones"]
    ctx = ExitStack()
    with ctx:
        def sb(name, shape, dt):
            return ctx.enter_context(nc.sbuf_tensor(name, shape, dt))

        def pb(name):
            return ctx.enter_context(nc.psum_tensor(name, [P, 512], F32))

        def sem(name):
            return ctx.enter_context(nc.semaphore(name))

        TE = TILES * E
        BITS = 30
        PER = TE // 4
        z = sb("z", [P, TILES, D], F32)
        ew = sb("ew", [P, CB, D], F32)
        ewp = [sb(f"ewp{i}", [P, CB, D], F32R) for i in range(2)]
        rw = sb("rw", [P, CB, E], F32)
        rwp = [sb(f"rwp{i}", [P, CB, E], F32R) for i in range(2)]
        eb = sb("eb", [P, D], F32)
        rb = sb("rb", [P, E], F32)
        tmp = sb("rs_tmp3", [P, 2, TILES], F32)
        rstd = sb("rstd3", [P, TILES], F32)
        xn = sb("xn3", [P, 2, D], F32)
        xp = [sb(f"xp{i}", [P, 2, CB * P], F32R) for i in range(2)]
        prob = sb("prob", [P, TILES, E], F32)
        rmax = sb("rmax", [P, TILES], F32)
        rinv = sb("rinv3", [P, TILES], F32)
        bits = sb("bits", [P, 2, E], I32)
        thr = sb("thr", [P, E], I32)
        add = sb("add", [P, E], I32)
        cand = sb("cand", [P, E], I32)
        taken = sb("taken", [P, TILES, E], BF16)
        equal = sb("equal", [P, TILES, E], BF16)
        count = sb("count", [P, E], F32)
        total = sb("total", [P, TILES, E], F32)
        run = [sb(f"run{i}", [P, TILES, E], F32) for i in range(2)]
        coef = sb("coef", [P, TILES], F32)
        hold = sb("hold4", [P, 1], F32)
        held_out = sb("held_out", [P, 2], F32)
        TR = [pb(f"f_tr{i}") for i in range(2)]
        ZB = [pb(f"f_z{i}") for i in range(2)]
        LB = pb("f_l")
        CN = pb("f_cn")
        TB2 = pb("f_tb")

        s_w, s_b = sem("f_w"), sem("f_b")
        s_whi, s_wlo = sem("f_whi"), sem("f_wlo")
        s_var, s_sqrt, s_step = sem("f_var"), sem("f_sqrt"), sem("f_rstep")
        s_xn, s_tr, s_hi, s_lo = sem("f_xn"), sem("f_tr"), sem("f_hi"), sem("f_lo")
        s_keep = sem("f_keep")
        s_lg = sem("f_lg")
        s_zact = sem("f_zact")
        s_zlo = sem("f_zlo")
        s_z, s_zb = sem("f_z"), sem("f_zb")
        s_hold = sem("f_hold")
        s_soft, s_exp = sem("f_soft"), sem("f_exp")
        s_cand, s_cnt, s_srch = sem("f_cand"), sem("f_cnt"), sem("f_srch")
        s_pick, s_rank = sem("f_pick"), sem("f_rank")
        s_out, s_st = sem("f_out"), sem("f_st")
        block = ctx.enter_context(nc.Block())
        ov = out.rearrange("b (t p) d -> b p t d", p=P)

        def col(ap, n):
            return ap[:, bass.ds(n, 1), :].rearrange("p o d -> p (o d)")

        def flat(ap):
            return ap.rearrange("p a b -> p (a b)")

        @block.sync
        def _(sp):
            sp.dma_start(ew[:, :, :], expert_w.rearrange("(c p) n -> p c n", p=P)).then_inc(s_w, 16)
            sp.dma_start(rw[:, :, :], router_w.rearrange("(c p) n -> p c n", p=P)).then_inc(s_w, 16)
            sp.dma_start(eb[:, :], expert_b.rearrange("(a n) -> a n", a=1).broadcast_to([P, D])).then_inc(s_b, 16)
            sp.dma_start(rb[:, :], router_b.rearrange("(a n) -> a n", a=1).broadcast_to([P, E])).then_inc(s_b, 16)
            def turn(b):
                sp.wait_ge(s_out, 2 * b + 2)
                sp.dma_start(ov[bass.ds(b, 1)].rearrange("o p t d -> (o p) t d"),
                             z[:, bass.ds(2 * b, 2), :]).then_inc(s_st, 16)

            turns(sp, B, turn)
            sp.wait_ge(s_st, 16 * B)

        def lookahead(eng, first, step):
            for t in range(2):
                first(t)
            for t in range(2):
                step(t, t, True)
            with eng.Fori(1, TILES // 2 - 1) as i:
                for t in range(2):
                    step(2 * i + t, t, True)
            for t in range(2):
                step(TILES - 2 + t, t, False)

        def at(n):
            return slice(n, n + 1) if isinstance(n, int) else bass.ds(n, 1)

        @block.tensor
        def _(pe):
            pe.wait_ge(s_wlo, 2)

            def product(out_bank, t, w):
                k = 0
                for c in range(CB):
                    for a, b in ((0, 0), (0, 1), (1, 0)):
                        last = nc.tensor.matmul(out_bank, xp[t][:, a, c * P:(c + 1) * P], w[b][:, c, :],
                                                start=(k == 0), stop=(k == 3 * CB - 1))
                        k += 1
                return last

            def transposes(n, t):
                pe.wait_ge(s_xn, n + 1)
                if not (isinstance(n, int) and n < 2):
                    pe.wait_ge(s_lo, n - 1)
                    pe.wait_ge(s_keep, n - 1)
                for c in range(CB):
                    last = nc.tensor.transpose(TR[t][:, c * P:(c + 1) * P], xn[:, t, c * P:(c + 1) * P], ident[:, :])
                last.then_inc(s_tr, 1)

            def logits(n, t, more2):
                pe.wait_ge(s_lo, n + 1)
                product(LB[:, bass.ds(n * E, E)], t, rwp).then_inc(s_lg, 1)
                if more2:
                    transposes(n + 2, t)

            lookahead(pe, lambda t: transposes(t, t), logits)

            def count_taken():
                for i in range(4):
                    last = nc.tensor.matmul(CN[:, 0:PER], ones[:, :], flat(taken[:, i * (TILES // 4):(i + 1) * (TILES // 4), :]),
                                            start=(i == 0), stop=(i == 3))
                last.then_inc(s_cnt, 1)

            def expert(n, t):
                pe.wait_ge(s_zlo, 2 * n + 2)
                product(ZB[t][:, :], t, ewp).then_inc(s_z, 1)

            def rounds(i):
                for t in range(2):
                    expert(2 * i + t, t)
                    pe.wait_ge(s_cand, 2 * i + t + 1)
                    count_taken()

            turns(pe, BITS // 2, rounds)
            for n in range(BITS, TILES):
                expert(n, n % 2)
            pe.wait_ge(s_pick, 2)
            count_taken()
            nc.tensor.matmul(TR[0][:, :], tri[:, :], flat(equal[:, :, :]), start=True, stop=True)
            nc.tensor.matmul(TB2[:, :], ones[:, :], flat(equal[:, :, :]), start=True, stop=True).then_inc(s_rank, 1)

        @block.scalar
        def _(act):
            act.wait_ge(s_w, 32)
            nc.scalar.activation(flat(ewp[0][:, :, :]), flat(ew[:, :, :]), ACT.Copy).then_inc(s_whi, 1)
            nc.scalar.activation(flat(rwp[0][:, :, :]), flat(rw[:, :, :]), ACT.Copy).then_inc(s_whi, 1)
            rstd_of_all(nc, act, None, rstd, tmp, s_var, s_sqrt, s_step)

            def split(n, t, more2):
                act.wait_ge(s_tr, n + 1)
                if not (isinstance(n, int) and n < 2):
                    act.wait_ge(s_lg, n - 1)
                nc.scalar.activation(xp[t][:, 0, :], TR[t][:, :], ACT.Copy).then_inc(s_hi, 1)
                act.wait_ge(s_lo, n + 1)
                nc.scalar.activation(z[:, at(n), :].rearrange("p o d -> p (o d)"), TR[t][:, :],
                                     ACT.Copy).then_inc(s_keep, 1)

            lookahead(act, lambda t: None, split)
            act.wait_ge(s_soft, 3)
            nc.scalar.activation(flat(prob[:, :, :]), flat(prob[:, :, :]), ACT.Exp).then_inc(s_exp, 1)
            act.wait_ge(s_keep, TILES)

            def z_round(n, t):
                nc.scalar.activation(xp[t][:, 0, :], z[:, at(n), :].rearrange("p o d -> p (o d)"),
                                     ACT.Copy).then_inc(s_zact, 1)

            def z_keep(n, t, more2):
                act.wait_ge(s_z, n + 1)
                nc.scalar.activation(z[:, at(n), :].rearrange("p o d -> p (o d)"), ZB[t][:, :],
                                     ACT.Copy).then_inc(s_zact, 1)
                if more2:
                    z_round(n + 2, t)

            act.wait_ge(s_lg, TILES)
            lookahead(act, lambda t: z_round(t, t), z_keep)

        @block.gpsimd
        def _(pool):
            nc.gpsimd.memset(hold[:, :], 0.0).then_inc(s_hold, 1)
            pool.wait_ge(s_hold, 1)

            def z_rest(n, t, acts):
                pool.wait_ge(s_zact, acts)
                nc.gpsimd.tensor_tensor(held_out[:, t:t + 1], hold[:, :], hold[:, :], ALU.add).then_inc(s_zlo, 1)
                nc.gpsimd.tensor_tensor(xp[t][:, 1, :], z[:, at(n), :].rearrange("p o d -> p (o d)"),
                                        xp[t][:, 0, :].bitcast(F32), ALU.subtract).then_inc(s_zlo, 1)

            def z_bias(n, t, more2):
                if more2:
                    z_rest(n + 2, t, 2 * n + 4)
                else:
                    pool.wait_ge(s_zact, TILES + n + 1)
                zn = z[:, at(n), :].rearrange("p o d -> p (o d)")
                nc.gpsimd.tensor_tensor(zn, zn, eb[:, :], ALU.add).then_inc(s_zb, 1)

            pool.wait_ge(s_b, 32)
            lookahead(pool, lambda t: z_rest(t, t, t + 1), z_bias)

        @block.vector
        def _(dve):
            dve.wait_ge(s_whi, 2)
            nc.vector.tensor_tensor(flat(ewp[1][:, :, :]), flat(ew[:, :, :]), flat(ewp[0][:, :, :]).bitcast(F32),
                                    ALU.subtract).then_inc(s_wlo, 1)
            nc.vector.tensor_tensor(flat(rwp[1][:, :, :]), flat(rw[:, :, :]), flat(rwp[0][:, :, :]).bitcast(F32),
                                    ALU.subtract).then_inc(s_wlo, 1)
            nc.vector.tensor_scalar(tmp[:, 0, :], mv3[:, :, 1], EPS, None, ALU.add).then_inc(s_var, 1)
            dve.wait_ge(s_var, 1)
            rstd_of_all(nc, None, dve, rstd[:, :], tmp, s_var, s_sqrt, s_step)
            dve.wait_ge(s_b, 32)

            def normed(n, t):
                if not (isinstance(n, int) and n < 2):
                    dve.wait_ge(s_tr, n - 1)
                nc.vector.tensor_scalar(xn[:, t, :], x2[:, at(n), :].rearrange("p o d -> p (o d)"), mv3[:, at(n), 0],
                                        rstd[:, at(n)], ALU.subtract, ALU.mult).then_inc(s_xn, 1)

            def rest(n, t, more2):
                if more2:
                    normed(n + 2, t)
                dve.wait_ge(s_hi, n + 1)
                nc.vector.tensor_tensor(xp[t][:, 1, :], TR[t][:, :], xp[t][:, 0, :].bitcast(F32),
                                        ALU.subtract).then_inc(s_lo, 1)

            lookahead(dve, lambda t: normed(t, t), rest)

            def by_tile(ap):
                return ap.unsqueeze(2).broadcast_to([P, TILES, E])

            dve.wait_ge(s_lg, TILES)
            nc.vector.tensor_tensor(prob[:, :, :], LB[:, :].rearrange("p (t e) -> p t e", e=E),
                                    rb[:, :].unsqueeze(1).broadcast_to([P, TILES, E]), ALU.add).then_inc(s_soft, 1)
            dve.wait_ge(s_soft, 1)
            nc.vector.reduce_max(rmax[:, :], prob[:, :, :], AX.X).then_inc(s_soft, 1)
            dve.wait_ge(s_soft, 2)
            nc.vector.tensor_tensor(prob[:, :, :], prob[:, :, :], by_tile(rmax[:, :]), ALU.subtract).then_inc(s_soft, 1)
            nc.vector.memset(thr[:, :], 0).then_inc(s_soft, 1)
            nc.vector.memset(bits[:, 0, :], 1 << 29).then_inc(s_soft, 1)
            nc.vector.memset(cand[:, :], 1 << 29).then_inc(s_soft, 1)
            dve.wait_ge(s_exp, 1)
            nc.vector.reduce_sum(rmax[:, :], prob[:, :, :], AX.X).then_inc(s_soft, 1)
            dve.wait_ge(s_soft, 7)
            nc.vector.reciprocal(rinv[:, :], rmax[:, :]).then_inc(s_soft, 1)
            dve.wait_ge(s_soft, 8)
            nc.vector.tensor_tensor(prob[:, :, :], prob[:, :, :], by_tile(rinv[:, :]), ALU.mult).then_inc(s_soft, 1)
            dve.wait_ge(s_soft, 9)

            def by_expert(ap):
                return ap.unsqueeze(1).broadcast_to([P, TILES, E])

            STEPS = 5

            def counted(c):
                dve.wait_ge(s_cnt, c)
                return nc.vector.reduce_sum(count[:, :], CN[:, 0:PER].rearrange("p (t e) -> p e t", e=E), AX.X)

            with dve.Fori(0, BITS // 2) as i:
                for k in range(2):
                    r = 2 * i + k
                    nc.vector.tensor_tensor(taken[:, :, :], prob[:, :, :], by_expert(cand[:, :].bitcast(F32)),
                                            ALU.is_ge).then_inc(s_cand, 1)
                    nc.vector.tensor_scalar(bits[:, 1 - k, :], bits[:, k, :], 1, None,
                                            ALU.logical_shift_right).then_inc(s_srch, 1)
                    counted(r + 1).then_inc(s_srch, 1)
                    dve.wait_ge(s_srch, STEPS * r + 2)
                    nc.vector.scalar_tensor_tensor(add[:, :], count[:, :], float(TOPK), bits[:, k, :], ALU.is_ge,
                                                   ALU.mult).then_inc(s_srch, 1)
                    dve.wait_ge(s_srch, STEPS * r + 3)
                    nc.vector.tensor_tensor(thr[:, :], thr[:, :], add[:, :], ALU.bitwise_or).then_inc(s_srch, 1)
                    dve.wait_ge(s_srch, STEPS * r + 4)
                    nc.vector.tensor_tensor(cand[:, :], thr[:, :], bits[:, 1 - k, :], ALU.bitwise_or).then_inc(s_srch, 1)
                    dve.wait_ge(s_srch, STEPS * r + 5)

            t_f = by_expert(thr[:, :].bitcast(F32))
            nc.vector.tensor_tensor(taken[:, :, :], prob[:, :, :], t_f, ALU.is_gt).then_inc(s_pick, 1)
            nc.vector.tensor_tensor(equal[:, :, :], prob[:, :, :], t_f, ALU.is_equal).then_inc(s_pick, 1)
            steps = [2]

            def step(ins):
                steps[0] += 1
                ins.then_inc(s_pick, 1)
                dve.wait_ge(s_pick, steps[0])

            step(counted(BITS + 1))
            step(nc.vector.tensor_scalar(count[:, :], count[:, :], -1.0, float(TOPK), ALU.mult, ALU.add))
            dve.wait_ge(s_rank, 1)
            step(nc.vector.tensor_copy(flat(total[:, :, :]), TB2[:, :]))
            step(nc.vector.tensor_copy(flat(run[0][:, :, :]), TB2[:, :]))
            a, shift = 0, 1
            while shift < TILES:
                src, dst = run[a], run[1 - a]
                step(nc.vector.tensor_copy(dst[:, 0:shift, :], src[:, 0:shift, :]))
                step(nc.vector.tensor_tensor(dst[:, shift:TILES, :], src[:, shift:TILES, :],
                                             src[:, 0:TILES - shift, :], ALU.add))
                a, shift = 1 - a, 2 * shift
            rank = run[a]
            step(nc.vector.tensor_tensor(rank[:, :, :], rank[:, :, :], total[:, :, :], ALU.subtract))
            step(nc.vector.tensor_tensor(flat(rank[:, :, :]), TR[0][:, :], flat(rank[:, :, :]), ALU.add))
            step(nc.vector.tensor_tensor(rank[:, :, :], rank[:, :, :], by_expert(count[:, :]), ALU.is_le))
            step(nc.vector.tensor_tensor(rank[:, :, :], rank[:, :, :], equal[:, :, :], ALU.mult))
            step(nc.vector.tensor_tensor(rank[:, :, :], rank[:, :, :], taken[:, :, :], ALU.add))
            step(nc.vector.tensor_tensor(rank[:, :, :], rank[:, :, :], prob[:, :, :], ALU.mult))
            step(nc.vector.reduce_sum(coef[:, :], rank[:, :, :], AX.X))
            dve.wait_ge(s_zb, TILES)
            with dve.Fori(0, TILES) as n:
                nc.vector.scalar_tensor_tensor(col(z, n), col(z, n), coef[:, bass.ds(n, 1)], col(x2, n), ALU.mult,
                                               ALU.add).then_inc(s_out, 1)


def decoder_layer(nc, x, ctx_in, w_all, gamma, router_w, router_b, expert_w, expert_b, rope, out):
    xt = nc.dram_tensor("xt_scratch", [B, P, 2, CB, L], F32).ap()
    x1 = nc.dram_tensor("x1_scratch", [B, P, TB, D], F32).ap()
    sq = nc.dram_tensor("sq_scratch", [2, 2, P, D], F32).ap()
    sk = nc.dram_tensor("sk_scratch", [2, 2, P, D], F32).ap()
    ctx = ExitStack()
    with ctx:
        def sb(name, shape, dt):
            return ctx.enter_context(nc.sbuf_tensor(name, shape, dt))

        cst = dict(ident=sb("ident", [P, P], F32), identb=sb("identb", [P, P], BF16), mask=sb("mask", [P, P], BF16),
                   ones=sb("ones", [P, P], BF16), tri=sb("tri", [P, P], BF16))
        mv2 = sb("mv2", [P, TILES, 2], F32)
        mv3 = sb("mv3", [P, TILES, 2], F32)
        with ExitStack() as weights:
            def wb(name, shape, dt):
                return weights.enter_context(nc.sbuf_tensor(name, shape, dt))

            def sem(name):
                return weights.enter_context(nc.semaphore(name))

            wts = dict(hi=wb("whi0", [P, NCH, 512], F32R), lo=wb("wlo0", [P, NCH, 512], F32R),
                       raw=wb("wraw", [P, 2, 512], F32), s_raw=[sem(f"w_raw{i}") for i in range(2)],
                       s_hi=sem("w_hi"), s_lo=sem("w_lo"))
            layer_norm_1(nc, x, w_all, xt, cst, wts)
            self_attention(nc, x, w_all, rope, xt, x1, mv2, cst, wts)
        x2 = sb("x2", [P, TILES, D], F32)
        cross_attention(nc, x1, ctx_in, gamma, sq, sk, mv2, mv3, x2, cst)
        expert_mix(nc, router_w, router_b, expert_w, expert_b, mv3, x2, out, cst)


def rope_table():
    inv = (1.0 / np.power(np.float32(10000.0), np.arange(0, HD, 2, dtype=np.float32) / np.float32(HD))).astype(np.float32)
    ang = (np.arange(L, dtype=np.float32)[:, None] * inv[None, :]).astype(np.float64)
    cos, sin = np.cos(ang), np.sin(ang)
    table = np.stack([cos, -sin, sin], 1).astype(np.float32)
    return np.ascontiguousarray(table.reshape(TB, P, 3, HD // 2).transpose(1, 0, 2, 3))


def kernel(**inputs):
    import numpy as _np
    import concourse.bacc as _bacc
    from concourse import mybir as _mybir
    from concourse.bass_utils import run_bass_kernel_spmd as _run

    nc = _bacc.Bacc("TRN2", target_bir_lowering=False, num_devices=1)
    wq, wk, wv, wo = (_np.asarray(inputs[f"L0_attn_w{k}"]) for k in "qkvo")
    proj = [w.reshape(CB, P, G, GW).transpose(2, 0, 1, 3) for w in (wq, wk, wv)]
    w_all = _np.ascontiguousarray(_np.concatenate(proj + [wo.reshape(G, HG, P, D)], axis=1))
    feeds = {
        "x": inputs["x"], "ctx_in": inputs["ctx_2048"], "w_all": w_all,
        "gamma": _np.asarray(inputs["L0_xattn_gamma"]).reshape(1), "router_w": inputs["L0_ffn_router_w"],
        "router_b": inputs["L0_ffn_router_b"], "expert_w": inputs["L0_ffn_expert_w"],
        "expert_b": inputs["L0_ffn_expert_b"], "rope": rope_table(),
    }
    arrays, args = {}, {}
    for name, a in feeds.items():
        a = _np.ascontiguousarray(a)
        arrays[f"in_{name}_dram"] = a
        args[name] = nc.dram_tensor(f"in_{name}_dram", a.shape, _mybir.dt.from_np(a.dtype), kind="ExternalInput").ap()
    out = nc.dram_tensor("out_0_dram", (B, L, D), _mybir.dt.float32, kind="ExternalOutput").ap()
    decoder_layer(nc, out=out, **args)
    r = _run(nc, [arrays], core_ids=[0])
    return r.results[0]["out_0_dram"]
```

```python
import concourse.bass as bass
from concourse import mybir
from contextlib import ExitStack
import numpy as np

F32 = mybir.dt.float32
F32R = mybir.dt.float32r
BF16 = mybir.dt.bfloat16
I32 = mybir.dt.int32
ALU = mybir.AluOpType
ACT = mybir.ActivationFunctionType
AX = mybir.AxisListType

P = 128
B, L, D = 16, 256, 512
TILES = B * L // P
TB = L // P
CB = D // P
H, HD = 16, 128
HG = 4
G = H // HG
GW = HG * HD
NCH = 3 * CB + HG
KBLK = 3
XH, XD = 8, 32
XPT = P // XD
E = 16
TOPK = B * L // E
EPS = 1e-5
MASKED = -3.0e38
SCALE = HD ** -0.5
XSCALE = XD ** -0.5
CH_Q, CH_K, CH_V, CH_O = 0, CB, 2 * CB, 3 * CB


def turns(eng, count, body):
    body(0)
    with eng.Fori(1, count) as i:
        body(i)


def rstd_of_all(nc, act, dve, rstd, tmp, s_in, s_sqrt, s_step, turn=0, scale=1.0):
    if act is not None:
        act.wait_ge(s_in, turn + 1)
        nc.scalar.activation(tmp[:, 1, :], tmp[:, 0, :], ACT.Sqrt).then_inc(s_sqrt, 1)
    if dve is not None:
        steps = [5 * turn]

        def step(ins):
            steps[0] += 1
            ins.then_inc(s_step, 1)
            dve.wait_ge(s_step, steps[0])

        dve.wait_ge(s_sqrt, turn + 1)
        step(nc.vector.reciprocal(rstd, tmp[:, 1, :]))
        step(nc.vector.tensor_tensor(tmp[:, 1, :], rstd, rstd, ALU.mult))
        step(nc.vector.tensor_tensor(tmp[:, 1, :], tmp[:, 1, :], tmp[:, 0, :], ALU.mult))
        step(nc.vector.tensor_scalar(tmp[:, 1, :], tmp[:, 1, :], -0.5 * scale, 1.5 * scale, ALU.mult, ALU.add))
        step(nc.vector.tensor_tensor(rstd, rstd, tmp[:, 1, :], ALU.mult))


def layer_norm_1(nc, x, w_all, xt, cst, wts):
    ident = cst["ident"]
    whi, wlo, raw = wts["hi"], wts["lo"], wts["raw"]
    s_raw, s_whi, s_wlo = wts["s_raw"], wts["s_hi"], wts["s_lo"]
    ctx = ExitStack()
    with ctx:
        def sb(name, shape, dt):
            return ctx.enter_context(nc.sbuf_tensor(name, shape, dt))

        def sem(name):
            return ctx.enter_context(nc.semaphore(name))

        QUARTERS = 4
        per = TILES // QUARTERS
        pairs = B // 2
        x_all = sb("x_all", [P, TILES, D], F32)
        bn = sb("bn1", [P, TILES, 6], F32)
        mv = sb("mv1", [P, TILES, 2], F32)
        tmp = sb("rs_tmp1", [P, 2, TILES], F32)
        rstd = sb("rstd1", [P, TILES], F32)
        xn = sb("xn1", [P, 2, D], F32)
        parts = [sb(f"parts{i}", [P, 2, CB, L], F32R) for i in range(2)]
        ps = [ctx.enter_context(nc.psum_tensor(f"n1ps{i}", [P, CB, P], F32)) for i in range(2)]

        s_x = [sem(f"n1_x{i}") for i in range(QUARTERS)]
        s_const = sem("n1_const")
        s_bn, s_mv, s_var = sem("n1_bn"), sem("n1_mv"), sem("n1_var")
        s_sqrt, s_step = sem("n1_sqrt"), sem("n1_step")
        s_xn, s_tr, s_hi, s_lo = sem("n1_xn"), sem("n1_tr"), sem("n1_hi"), sem("n1_lo")
        s_out = [sem(f"n1_out{i}") for i in range(2)]
        xv = x.rearrange("b (t p) d -> p (b t) d", p=P)
        block = ctx.enter_context(nc.Block())

        def tok(t):
            return slice(t * P, (t + 1) * P)

        @block.sync
        def _(sp):
            def load_x(i):
                sp.dma_start(x_all[:, i * per:(i + 1) * per, :], xv[:, i * per:(i + 1) * per, :]).then_inc(s_x[i], 16)

            def load_w(b, m):
                src = w_all[0, b] if isinstance(b, int) else w_all[0, bass.ds(b, 1)].rearrange("o p d -> (o p) d")
                sp.dma_start(raw[:, m, :], src).then_inc(s_raw[m], 16)

            load_x(0)
            load_w(0, 0)
            load_w(1, 1)
            for i in range(1, QUARTERS):
                load_x(i)

            def pair(j, more):
                for m in range(2):
                    b = 2 * j + m
                    sp.wait_ge(s_lo, 2 * b + 2)
                    dst = xt[b] if isinstance(b, int) else xt[bass.ds(b, 1)].rearrange("o p h c n -> (o p) h c n")
                    sp.dma_start(dst, parts[m][:, :, :, :].bitcast(F32)).then_inc(s_out[m], 16)
                    if more:
                        sp.wait_ge(s_wlo, b + 1)
                        load_w(b + 2, m)

            pair(0, True)
            with sp.Fori(1, pairs - 1) as j:
                pair(j, True)
            pair(pairs - 1, False)
            for m in range(2):
                sp.wait_ge(s_out[m], 16 * pairs)

        @block.gpsimd
        def _(pool):
            nc.gpsimd.memset(ident[:, :], 0.0).then_inc(s_const, 1)
            nc.gpsimd.memset(cst["identb"][:, :], 0.0).then_inc(s_const, 1)
            nc.gpsimd.memset(cst["mask"][:, :], 0.0).then_inc(s_const, 1)
            nc.gpsimd.memset(cst["ones"][:, :], 1.0).then_inc(s_const, 1)
            nc.gpsimd.memset(cst["tri"][:, :], 1.0).then_inc(s_const, 1)
            pool.wait_ge(s_const, 5)
            for m in (ident, cst["identb"]):
                nc.gpsimd.affine_select(out=m[:, :], in_=m[:, :], compare_op=ALU.not_equal, fill=1.0, base=0,
                                        pattern=[[-1, P]], channel_multiplier=1).then_inc(s_const, 1)
            nc.gpsimd.affine_select(out=cst["mask"][:, :], in_=cst["mask"][:, :], compare_op=ALU.is_ge, fill=MASKED,
                                    base=0, pattern=[[-1, P]], channel_multiplier=1).then_inc(s_const, 1)
            nc.gpsimd.affine_select(out=cst["tri"][:, :], in_=cst["tri"][:, :], compare_op=ALU.is_ge, fill=0.0,
                                    base=0, pattern=[[1, P]], channel_multiplier=-1).then_inc(s_const, 1)
            for c in range(NCH):
                pool.wait_ge(s_whi, c + 1)
                nc.gpsimd.tensor_tensor(wlo[:, c, :], raw[:, c % 2, :], whi[:, c, :].bitcast(F32),
                                        ALU.subtract).then_inc(s_wlo, 1)

        @block.vector
        def _(dve):
            def stats(t):
                nc.vector.bn_stats(bn[:, t, :], x_all[:, t, :]).then_inc(s_bn, 1)

            def normed(n):
                if n >= 2:
                    dve.wait_ge(s_tr, n - 1)
                nc.vector.tensor_scalar(xn[:, n % 2, :], x_all[:, n, :], mv[:, n, 0:1], rstd[:, n:n + 1],
                                        ALU.subtract, ALU.mult).then_inc(s_xn, 1)

            def rest(n):
                dve.wait_ge(s_hi, n + 1)
                m = n // 2 % 2
                nc.vector.tensor_tensor(parts[m][:, 1, :, tok(n % 2)], ps[n % 2][:, :, :],
                                        parts[m][:, 0, :, tok(n % 2)].bitcast(F32), ALU.subtract).then_inc(s_lo, 1)

            dve.wait_ge(s_x[0], 16)
            for t in range(per):
                stats(t)
            for i in range(QUARTERS):
                q = slice(i * per, (i + 1) * per)
                dve.wait_ge(s_bn, (i + 1) * per)
                for t in range(i * per, (i + 1) * per):
                    nc.vector.bn_aggr(mv[:, t, :], bn[:, t, :]).then_inc(s_mv, 1)
                dve.wait_ge(s_mv, (i + 1) * per)
                nc.vector.tensor_scalar(tmp[:, 0, q], mv[:, q, 1], EPS, None, ALU.add).then_inc(s_var, 1)
                rstd_of_all(nc, None, dve, rstd[:, q], tmp[:, :, q], s_var, s_sqrt, s_step, i)
                normed(i * per)
                normed(i * per + 1)
                if i + 1 < QUARTERS:
                    dve.wait_ge(s_x[i + 1], 16)
                for n in range(i * per, (i + 1) * per):
                    if n + 2 < (i + 1) * per:
                        normed(n + 2)
                    if i + 1 < QUARTERS:
                        stats(n + per)
                    rest(n)

        @block.scalar
        def _(act):
            def quarter(i):
                q = slice(0, per) if isinstance(i, int) else bass.ds(i * per, per)
                rstd_of_all(nc, act, None, rstd, tmp[:, :, q], s_var, s_sqrt, s_step, i)
                for k in range(per // 2):
                    b, m = i * (per // 2) + k, k % 2
                    if not (isinstance(b, int) and b < 2):
                        act.wait_ge(s_out[m], 8 * (b - m))
                    for t in range(TB):
                        act.wait_ge(s_tr, 2 * b + t + 1)
                        nc.scalar.activation(parts[m][:, 0, :, tok(t)], ps[t][:, :, :], ACT.Copy).then_inc(s_hi, 1)
                    act.wait_ge(s_raw[m], 8 * (b - m) + 16)
                    dst = whi[:, b, :] if isinstance(b, int) else whi[:, bass.ds(b, 1), :].rearrange("p o d -> p (o d)")
                    nc.scalar.activation(dst, raw[:, m, :], ACT.Copy).then_inc(s_whi, 1)

            turns(act, QUARTERS, quarter)

        @block.tensor
        def _(pe):
            pe.wait_ge(s_const, 9)

            def turn(b):
                for t in range(TB):
                    pe.wait_ge(s_xn, 2 * b + t + 1)
                    if not (isinstance(b, int) and b == 0):
                        pe.wait_ge(s_lo, 2 * b + t - 1)
                    for c in range(CB):
                        last = nc.tensor.transpose(ps[t][:, c, :], xn[:, t, c * P:(c + 1) * P], ident[:, :])
                    last.then_inc(s_tr, 1)

            turns(pe, B, turn)


def self_attention(nc, x, w_all, rope, xt, x1, mv2, cst, wts):
    ident, identb, mask = cst["ident"], cst["identb"], cst["mask"]
    ctx = ExitStack()
    with ctx:
        def sb(name, shape, dt):
            return ctx.enter_context(nc.sbuf_tensor(name, shape, dt))

        def pb(name):
            return ctx.enter_context(nc.psum_tensor(name, [P, 512], F32))

        def sem(name):
            return ctx.enter_context(nc.semaphore(name))

        whi = [wts["hi"], sb("whi1", [P, NCH, 512], F32R)]
        wlo = [wts["lo"], sb("wlo1", [P, NCH, 512], F32R)]
        raw = wts["raw"]
        s_raw, s_whi, s_wlo = wts["s_raw"], wts["s_hi"], wts["s_lo"]
        xnt = [sb(f"xnt{i}", [P, 2, CB, L], F32R) for i in range(2)]
        rot = [sb(f"rot{i}", [P, TB, GW], F32) for i in range(2)]
        swp = sb("swp", [P, 2, GW], F32)
        v_sb = [sb(f"v{i}", [P, TB, GW], F32) for i in range(2)]
        qkt = [sb(f"qkt{i}", [P, HG, L], F32) for i in range(2)]
        pr = sb("pr", [P, HG, KBLK * P], F32)
        prt = sb("prt", [P, HG, KBLK * P], F32)
        ohi = sb("ohi", [P, HG, L], F32R)
        olo = sb("olo", [P, HG, L], F32R)
        xio = sb("xio", [P, 2, TB, D], F32)
        trig = sb("trig", [P, TB, 3, HD // 2], F32)
        mx = sb("mx", [P, HG, TB], F32)
        nmx = sb("nmx", [P, HG, TB], F32)
        rsum = sb("rsum", [P, HG, TB], F32)
        rinv = sb("rinv", [P, HG, TB], F32)
        bn = sb("bn2", [P, TB, 6], F32)
        agg = sb("agg2", [P, TB, 2], F32)
        hold = sb("hold2", [P, 1], F32)

        PJ = [pb("pj0"), pb("pj1")]
        TR = [pb("tr0"), pb("tr1")]
        SC = [pb("sc0"), pb("sc1")]
        OB = [pb("ob0"), pb("ob1")]

        s_trig = sem("a_trig")
        s_xn = [sem(f"a_xn{i}") for i in range(2)]
        s_xi = [sem(f"a_xi{i}") for i in range(2)]
        s_xo = [sem(f"a_xo{i}") for i in range(2)]
        s_proj = sem("a_proj")
        s_mul = sem("a_mul")
        s_swp = sem("a_swp")
        s_vev = sem("a_vev")
        s_qkt = sem("a_qkt")
        s_qke = sem("a_qke")
        s_sc = sem("a_sc")
        s_mx, s_nmx = sem("a_mx"), sem("a_nmx")
        s_exp = sem("a_exp")
        s_ri, s_pr = sem("a_ri"), sem("a_pr")
        s_pt = sem("a_pt")
        s_pte = sem("a_pte")
        s_pv = sem("a_pv")
        s_ohi, s_olo = sem("a_ohi"), sem("a_olo")
        s_wo = sem("a_wo")
        s_x1 = [sem(f"a_x1{i}") for i in range(TB)]
        s_bn, s_mv = sem("a_bn"), sem("a_mv")
        block = ctx.enter_context(nc.Block())

        xv = x.rearrange("b (t p) d -> b p t d", p=P)
        ITEMS = G * B

        def items(eng, item, ahead=True):
            for g in range(G):
                if g == 0:
                    item(0, 0, 0, 0, 0, True)
                    item(1, 0, 1, 1, 0, True)
                with eng.Fori(1 if g == 0 else 0, B // 2 - 1) as j:
                    for par in range(2):
                        item(2 * j + (g * B + par), g, 2 * j + par, par, g, True)
                item(g * B + B - 2, g, B - 2, 0, g, True)
                item(g * B + B - 1, g, B - 1, 1, g + 1, g + 1 < G)

        def one(ap, i):
            return ap[bass.ds(i, 1)].rearrange("o p a d -> (o p) a d") if not isinstance(i, int) else ap[i]

        @block.sync
        def _(sp):
            sp.dma_start(trig[:, :, :, :], rope).then_inc(s_trig, 16)
            for m in range(2):
                sp.dma_start(xnt[m][:, :, :, :].bitcast(F32), xt[m]).then_inc(s_xn[m], 16)

            def item(n, g, b, par, gn, more):
                half = (n - par) // 2 if isinstance(n, int) else None
                stored = 16 * half if half is not None else 8 * (n - par)
                sp.wait_ge(s_xo[par], stored)
                src = (xv if g == 0 else x1)
                src = src[b] if isinstance(b, int) else src[bass.ds(b, 1)].rearrange("o p t d -> (o p) t d")
                sp.dma_start(xio[:, par, :, :], src).then_inc(s_xi[par], 16)
                if g + 1 < G:
                    sp.wait_ge(s_wlo, n + (NCH - 1))
                    wsrc = w_all[g + 1, b] if isinstance(b, int) else w_all[g + 1, bass.ds(b, 1)].rearrange("o p d -> (o p) d")
                    sp.dma_start(raw[:, par, :], wsrc).then_inc(s_raw[par], 16)
                if isinstance(b, int):
                    b2, there = (b + 2) % B, g + (b + 2) // B < G
                else:
                    b2, there = b + 2, True
                if there:
                    sp.wait_ge(s_proj, 6 * n + 6)
                    xsrc = xt[b2] if isinstance(b2, int) else xt[bass.ds(b2, 1)].rearrange("o p h c n -> (o p) h c n")
                    sp.dma_start(xnt[par][:, :, :, :].bitcast(F32), xsrc).then_inc(s_xn[par], 16)
                for t in range(TB):
                    sp.wait_ge(s_x1[t], n + 1)
                dst = x1[b] if isinstance(b, int) else x1[bass.ds(b, 1)].rearrange("o p t d -> (o p) t d")
                sp.dma_start(dst, xio[:, par, :, :]).then_inc(s_xo[par], 16)

            items(sp, item)
            for par in range(2):
                sp.wait_ge(s_xo[par], 16 * ITEMS // 2)

        @block.gpsimd
        def _(pool):
            def rotate(m):
                for i in range(4):
                    pool.wait_ge(s_mul, 4 * m + i + 1)
                    r = rot[i // 2][:, i % 2, :]
                    nc.gpsimd.tensor_tensor(r, r, swp[:, i % 2, :], ALU.add).then_inc(s_swp, 1)

            rotate(0)
            items(pool, lambda n, g, b, par, gn, more: rotate(n + 1) if more else None)

        @block.tensor
        def _(pe):
            def project(bank, m, gn, par, kind, t):
                k = 0
                for c in range(CB):
                    tok = slice(t * P, (t + 1) * P)
                    for xpart, w in ((0, whi), (0, wlo), (1, whi)):
                        last = nc.tensor.matmul(bank[:, :], xnt[par][:, xpart, c, tok], w[gn % 2][:, kind + c, :],
                                                start=(k == 0), stop=(k == 3 * CB - 1))
                        k += 1
                last.then_inc(s_proj, 1)

            def xn_here(m, par):
                if isinstance(m, int):
                    pe.wait_ge(s_xn[par], 16 * (m // 2 + 1))
                else:
                    pe.wait_ge(s_xn[par], 8 * (m - par) + 16)

            pe.wait_ge(s_wlo, NCH)
            xn_here(0, 0)
            project(PJ[0], 0, 0, 0, CH_Q, 0)
            project(PJ[1], 0, 0, 0, CH_Q, 1)
            pe.wait_ge(s_mul, 1)
            project(PJ[0], 0, 0, 0, CH_K, 0)
            pe.wait_ge(s_mul, 2)
            project(PJ[1], 0, 0, 0, CH_K, 1)
            pe.wait_ge(s_mul, 3)
            project(PJ[0], 0, 0, 0, CH_V, 0)
            pe.wait_ge(s_mul, 4)
            project(PJ[1], 0, 0, 0, CH_V, 1)

            def item(n, g, b, par, gn, more):
                m, mp = n + 1, 1 - par

                def transposes(i):
                    src, h0 = rot[i % 2], 2 * (i // 2)
                    for h in range(2):
                        for t in range(TB):
                            last = nc.tensor.transpose(TR[i % 2][:, (h * TB + t) * P:(h * TB + t + 1) * P],
                                                       src[:, t, (h0 + h) * HD:(h0 + h + 1) * HD], ident[:, :])
                    last.then_inc(s_qkt, 1)

                def scores(h):
                    bank = SC[h % 2]
                    qT, kT = qkt[0][:, h, :], qkt[1][:, h, :]
                    nc.tensor.matmul(bank[:, 0:P], qT[:, 0:P], kT[:, 0:P], start=True, stop=False)
                    nc.tensor.matmul(bank[:, 0:P], identb[:, :], mask[:, :], start=False, stop=True)
                    nc.tensor.matmul(bank[:, P:3 * P], qT[:, P:2 * P], kT[:, 0:2 * P], start=True, stop=False)
                    nc.tensor.matmul(bank[:, 2 * P:3 * P], identb[:, :], mask[:, :], start=False,
                                     stop=True).then_inc(s_sc, 1)

                def prob_transposes(h):
                    for k in range(KBLK):
                        last = nc.tensor.transpose(TR[h % 2][:, k * P:(k + 1) * P], pr[:, h, k * P:(k + 1) * P],
                                                   ident[:, :])
                    last.then_inc(s_pt, 1)

                def weigh(h):
                    bank, o = OB[h // 2], (h % 2) * L
                    hd = slice(h * HD, (h + 1) * HD)
                    nc.tensor.matmul(bank[:, o:o + L], v_sb[par][:, 0, hd], prt[:, h, 0:2 * P], start=True, stop=False)
                    last = nc.tensor.matmul(bank[:, o + P:o + L], v_sb[par][:, 1, hd], prt[:, h, 2 * P:3 * P],
                                            start=False, stop=True)
                    if h % 2:
                        last.then_inc(s_pv, 1)

                pe.wait_ge(s_swp, 4 * n + 4)
                pe.wait_ge(s_pte, 4 * n)
                transposes(0)
                transposes(1)
                if more:
                    xn_here(m, mp)
                    pe.wait_ge(s_wlo, gn * NCH + 3 * CB)
                    pe.wait_ge(s_vev, 2 * n + 2)
                    pe.wait_ge(s_x1[0], n)
                    project(PJ[0], m, gn, mp, CH_Q, 0)
                pe.wait_ge(s_qke, 4 * n + 1)
                transposes(2)
                pe.wait_ge(s_qke, 4 * n + 2)
                transposes(3)
                pe.wait_ge(s_exp, 8 * n)
                scores(0)
                scores(1)
                if more:
                    pe.wait_ge(s_x1[1], n)
                    project(PJ[1], m, gn, mp, CH_Q, 1)
                    pe.wait_ge(s_mul, 4 * m + 1)
                    project(PJ[0], m, gn, mp, CH_K, 0)
                pe.wait_ge(s_qke, 4 * n + 4)
                pe.wait_ge(s_exp, 8 * n + 4)
                scores(2)
                scores(3)
                pe.wait_ge(s_pr, 8 * n + 4)
                prob_transposes(0)
                prob_transposes(1)
                if more:
                    pe.wait_ge(s_mul, 4 * m + 2)
                    project(PJ[1], m, gn, mp, CH_K, 1)
                    pe.wait_ge(s_mul, 4 * m + 3)
                    project(PJ[0], m, gn, mp, CH_V, 0)
                pe.wait_ge(s_pr, 8 * n + 8)
                pe.wait_ge(s_pte, 4 * n + 1)
                prob_transposes(2)
                pe.wait_ge(s_pte, 4 * n + 2)
                prob_transposes(3)
                pe.wait_ge(s_vev, 2 * n + 2)
                pe.wait_ge(s_olo, 2 * n)
                weigh(0)
                weigh(1)
                if more:
                    pe.wait_ge(s_mul, 4 * m + 4)
                    project(PJ[1], m, gn, mp, CH_V, 1)
                pe.wait_ge(s_pte, 4 * n + 4)
                weigh(2)
                weigh(3)
                pe.wait_ge(s_wlo, (g + 1) * NCH)
                for half in range(2):
                    pe.wait_ge(s_olo, 2 * n + half + 1)
                    for t in range(TB):
                        if half == 0 and more:
                            pe.wait_ge(s_vev, 2 * m + t + 1)
                        elif half == 0:
                            pe.wait_ge(s_vev, 2 * n + 2)
                        for h in (2 * half, 2 * half + 1):
                            tok = slice(t * P, (t + 1) * P)
                            for k, (o, w) in enumerate(((ohi, whi), (ohi, wlo), (olo, whi))):
                                last = nc.tensor.matmul(PJ[t][:, :], o[:, h, tok], w[g % 2][:, CH_O + h, :],
                                                        start=(h == 0 and k == 0), stop=(h == HG - 1 and k == 2))
                        if half:
                            last.then_inc(s_wo, 1)

            items(pe, item)

        @block.scalar
        def _(act):
            def w_chunk(c, total, dst, par):
                act.wait_ge(s_raw[par], 8 * (total - par + 1))
                out = whi[dst][:, c, :] if isinstance(c, int) else whi[dst][:, bass.ds(c, 1), :].rearrange("p o d -> p (o d)")
                nc.scalar.activation(out, raw[:, par, :], ACT.Copy).then_inc(s_whi, 1)

            def v_evac(m, mp, t):
                act.wait_ge(s_proj, 6 * m + 5 + t)
                nc.scalar.activation(v_sb[mp][:, t, :], PJ[t][:, :], ACT.Copy).then_inc(s_vev, 1)

            v_evac(0, 0, 0)
            v_evac(0, 0, 1)

            def item(n, g, b, par, gn, more):
                m, mp = n + 1, 1 - par

                def qk_evac(i):
                    act.wait_ge(s_qkt, 4 * n + i + 1)
                    h0 = 2 * (i // 2)
                    nc.scalar.activation(qkt[i % 2][:, h0:h0 + 2, :].rearrange("p h n -> p (h n)"), TR[i % 2][:, :],
                                         ACT.Copy).then_inc(s_qke, 1)

                def exps(pair):
                    act.wait_ge(s_nmx, 2 * n + pair + 1)
                    for h in (2 * pair, 2 * pair + 1):
                        for t in range(TB):
                            lo, hi = (0, P) if t == 0 else (P, 3 * P)
                            nc.scalar.activation(pr[:, h, lo:hi], SC[h % 2][:, lo:hi], ACT.Exp,
                                                 bias=nmx[:, h, t:t + 1], scale=SCALE,
                                                 accum_out=rsum[:, h, t:t + 1]).then_inc(s_exp, 1)

                def pt_evac(h):
                    act.wait_ge(s_pt, 4 * n + h + 1)
                    nc.scalar.activation(prt[:, h, :], TR[h % 2][:, 0:KBLK * P], ACT.Copy).then_inc(s_pte, 1)

                def o_round(pair):
                    act.wait_ge(s_pv, 2 * n + pair + 1)
                    nc.scalar.activation(ohi[:, 2 * pair:2 * pair + 2, :].rearrange("p h n -> p (h n)"), OB[pair][:, :],
                                         ACT.Copy).then_inc(s_ohi, 1)

                act.wait_ge(s_sc, 4 * n)
                qk_evac(0)
                qk_evac(1)
                qk_evac(2)
                qk_evac(3)
                if g + 1 < G:
                    act.wait_ge(s_wo, 2 * B * g)
                    w_chunk(b, n + (NCH + 1), (g + 1) % 2, par)
                act.wait_ge(s_pt, 4 * n)
                exps(0)
                exps(1)
                act.wait_ge(s_pv, 2 * n)
                pt_evac(0)
                pt_evac(1)
                if more:
                    act.wait_ge(s_pv, 2 * n)
                    v_evac(m, mp, 0)
                pt_evac(2)
                pt_evac(3)
                act.wait_ge(s_wo, 2 * n)
                o_round(0)
                if more:
                    v_evac(m, mp, 1)
                o_round(1)

            items(act, item)

        @block.vector
        def _(dve):
            def w_chunk(c, total, dst):
                dve.wait_ge(s_whi, total)
                par_c = (lambda a: a[:, c, :] if isinstance(c, int) else a[:, bass.ds(c, 1), :].rearrange("p o d -> p (o d)"))
                return par_c(whi[dst]), par_c(wlo[dst])

            def rope_mul(m, i):
                t = i % 2
                dve.wait_ge(s_proj, 6 * m + i + 1)
                half = HD // 2
                r = rot[i // 2][:, t, :].rearrange("p (h s d) -> p h s d", h=HG, s=2)
                s = swp[:, t, :].rearrange("p (h d) -> p h d", h=HG)
                bank = PJ[t][:, :].rearrange("p (h d) -> p h d", h=HG)
                nc.vector.tensor_tensor(r, bank.rearrange("p h (s d) -> p h s d", s=2),
                                        trig[:, t, 0, :].unsqueeze(1).unsqueeze(1).broadcast_to([P, HG, 2, half]),
                                        ALU.mult)
                for k, (lo, hi) in enumerate(((0, half), (half, HD))):
                    src = bank[:, :, half - lo:half - lo + half]
                    last = nc.vector.tensor_tensor(s[:, :, lo:hi], src,
                                                   trig[:, t, 1 + k, :].unsqueeze(1).broadcast_to([P, HG, half]),
                                                   ALU.mult)
                last.then_inc(s_mul, 1)

            dve.wait_ge(s_trig, 16)
            for i in range(4):
                if i >= 2:
                    dve.wait_ge(s_swp, i - 1)
                rope_mul(0, i)

            def item(n, g, b, par, gn, more):
                m = n + 1

                def maxima(pair):
                    for h in (2 * pair, 2 * pair + 1):
                        dve.wait_ge(s_sc, 4 * n + h + 1)
                        for t in range(TB):
                            lo, hi = (0, P) if t == 0 else (P, 3 * P)
                            nc.vector.reduce_max(mx[:, h, t:t + 1], SC[h % 2][:, lo:hi], AX.X).then_inc(s_mx, 1)
                    dve.wait_ge(s_mx, 8 * n + 4 * pair + 4)
                    pr2 = slice(2 * pair, 2 * pair + 2)
                    nc.vector.tensor_scalar(nmx[:, pr2, :].rearrange("p h t -> p (h t)"),
                                            mx[:, pr2, :].rearrange("p h t -> p (h t)"), -SCALE, None,
                                            ALU.mult).then_inc(s_nmx, 1)

                def normalise(pair):
                    pr2 = slice(2 * pair, 2 * pair + 2)
                    dve.wait_ge(s_exp, 8 * n + 4 * pair + 4)
                    nc.vector.reciprocal(rinv[:, pr2, :].rearrange("p h t -> p (h t)"),
                                         rsum[:, pr2, :].rearrange("p h t -> p (h t)")).then_inc(s_ri, 1)
                    dve.wait_ge(s_ri, 2 * n + pair + 1)
                    for h in (2 * pair, 2 * pair + 1):
                        for t in range(TB):
                            lo, hi = (0, P) if t == 0 else (P, 3 * P)
                            nc.vector.tensor_scalar(pr[:, h, lo:hi], pr[:, h, lo:hi], rinv[:, h, t:t + 1], None,
                                                    ALU.mult).then_inc(s_pr, 1)

                def rope(i):
                    if more:
                        dve.wait_ge(s_swp, 4 * m + i - 1)
                        dve.wait_ge(s_qkt, 4 * n + 4)
                        rope_mul(m, i)

                rope(0)
                if g + 1 < G:
                    dve.wait_ge(s_wo, 2 * B * g)
                    hi, lo = w_chunk(b, n + (NCH + 1), (g + 1) % 2)
                    nc.vector.tensor_tensor(lo, raw[:, par, :], hi.bitcast(F32), ALU.subtract).then_inc(s_wlo, 1)
                maxima(0)
                rope(1)
                normalise(0)
                rope(2)
                maxima(1)
                rope(3)
                normalise(1)
                dve.wait_ge(s_wo, 2 * n)
                for pair in range(2):
                    dve.wait_ge(s_ohi, 2 * n + pair + 1)
                    nc.vector.tensor_tensor(olo[:, 2 * pair:2 * pair + 2, :].rearrange("p h n -> p (h n)"), OB[pair][:, :],
                                            ohi[:, 2 * pair:2 * pair + 2, :].rearrange("p h n -> p (h n)").bitcast(F32),
                                            ALU.subtract).then_inc(s_olo, 1)
                if isinstance(n, int):
                    dve.wait_ge(s_xi[par], 16 * (n // 2 + 1))
                else:
                    dve.wait_ge(s_xi[par], 8 * (n - par) + 16)
                for t in range(TB):
                    dve.wait_ge(s_wo, 2 * n + t + 1)
                    nc.vector.tensor_tensor(xio[:, par, t, :], PJ[t][:, :], xio[:, par, t, :], ALU.add).then_inc(s_x1[t], 1)
                if g == G - 1:
                    k = n - g * B
                    for t in range(TB):
                        dve.wait_ge(s_x1[t], n + 1)
                        dve.wait_ge(s_mv, 2 * k)
                        nc.vector.bn_stats(bn[:, t, :], xio[:, par, t, :]).then_inc(s_bn, 1)
                        dve.wait_ge(s_bn, 4 * k + 2 * t + 1)
                        dst = mv2[:, 2 * b + t, :] if isinstance(b, int) else mv2[:, bass.ds(2 * b + t, 1), :].rearrange("p o d -> p (o d)")
                        nc.vector.memset(hold[:, :], 0.0)
                        nc.vector.bn_aggr(agg[:, t, :], bn[:, t, :]).then_inc(s_bn, 1)
                        dve.wait_ge(s_bn, 4 * k + 2 * t + 2)
                        nc.vector.tensor_copy(dst, agg[:, t, :]).then_inc(s_mv, 1)

            items(dve, item)
            dve.wait_ge(s_mv, 2 * B)


def cross_attention(nc, x1, ctx_in, gamma, sq, sk, mv2, mv3, x2, cst):
    ident = cst["ident"]
    ctx = ExitStack()
    with ctx:
        def sb(name, shape, dt):
            return ctx.enter_context(nc.sbuf_tensor(name, shape, dt))

        def pb(name):
            return ctx.enter_context(nc.psum_tensor(name, [P, 512], F32))

        def sem(name):
            return ctx.enter_context(nc.semaphore(name))

        PARTS = 3
        KS = PARTS * XD
        gam = sb("gam", [P, 1], F32)
        tmp = sb("rs_tmp2", [P, 2, TILES], F32)
        rstd = sb("rstd2", [P, TILES], F32)
        cin = sb("cin", [P, 2, D], F32)
        xn = sb("xn2", [P, D], F32)
        qp = sb("qp", [P, 2, D], F32R)
        kp = sb("kp", [P, 2, D], F32R)
        qst = [sb(f"qst{i}", [P, XPT, D], F32R) for i in range(2)]
        kst = [sb(f"kst{i}", [P, XPT, D], F32R) for i in range(2)]
        vt = sb("vt", [P, 2, CB, P], F32)
        prt = [sb(f"xprt{i}", [P, XPT, CB, D], F32) for i in range(2)]
        nmx = sb("xnmx", [P, 2, CB], F32)
        nmp = sb("xnmp", [P, 2, CB, XD], F32R)
        ones = sb("xones", [P, XD], F32)
        rq = sb("xrq", [P, CB * XPT], F32)
        rrep = sb("xrrep", [P, CB, P], F32)
        osb = sb("xosb", [P, D], F32)
        ssb = sb("xssb", [P, D], F32)
        onm = sb("xonm", [P, D], F32)
        bn = sb("bn3", [P, 6], F32)
        agg = sb("agg3", [P, 2], F32)
        hold = sb("hold3", [P, 1], F32)
        SC = [pb(f"xsc{i}") for i in range(2)]
        ST = [pb(f"xst{i}") for i in range(2)]
        MB = pb("xmb")
        OB = pb("xob")
        SU = pb("xsu")
        VB = pb("xvb")

        s_gam, s_var, s_sqrt, s_step = sem("x_gam"), sem("x_var"), sem("x_sqrt"), sem("x_step")
        s_xi = [sem(f"x_xi{i}") for i in range(2)]
        s_ci = [sem(f"x_ci{i}") for i in range(2)]
        s_qn, s_qhi, s_qlo = sem("x_qn"), sem("x_qhi"), sem("x_qlo")
        s_khi, s_klo = sem("x_khi"), sem("x_klo")
        s_qw, s_kw = sem("x_qw"), sem("x_kw")
        s_st = [[sem(f"x_st{i}{k}") for k in range(2)] for i in range(2)]
        s_ones = sem("x_ones")
        s_vt, s_vte = sem("x_vt"), sem("x_vte")
        s_sc = sem("x_sc")
        s_mx = sem("x_mx")
        s_nm = sem("x_nm")
        s_mr = sem("x_mr")
        s_row = sem("x_row")
        s_ts = sem("x_ts")
        s_exp = sem("x_exp")
        s_pv = sem("x_pv")
        s_oe = sem("x_oe")
        s_sq = sem("x_sq")
        s_ri = sem("x_ri")
        s_rr = sem("x_rr")
        s_rt = sem("x_rt")
        s_on = sem("x_on")
        s_x2 = sem("x_x2")
        s_bn, s_mv = sem("x_bn"), sem("x_mv")
        block = ctx.enter_context(nc.Block())

        cv = ctx_in.rearrange("b (t p) d -> (b t) p d", p=P)
        x1v = x1.rearrange("b p t d -> b t p d")

        def col(ap, n):
            return ap[:, n, :] if isinstance(n, int) else ap[:, bass.ds(n, 1), :].rearrange("p o d -> p (o d)")

        def all_tiles(eng, item, unroll=4):
            item(0, 0, True, True, True)
            item(1, 1, False, True, True)
            with eng.Fori(1, 1 + (TILES - 4) // unroll) as i:
                for k in range(unroll):
                    item(unroll * i + (2 - unroll + k), k % 2, False, True, True)
            item(TILES - 2, 0, False, True, False)
            item(TILES - 1, 1, False, False, False)

        def ahead(n, h, d, more):
            return (n, h + d, True) if h + d < XPT else (n + 1, h + d - XPT, more)

        def stacks(n, t):
            per = 32 * PARTS
            return per * (n // 2 + 1) if isinstance(n, int) else (per // 2) * (n - t) + per

        def loads(n, t):
            return 16 * (n // 2 + 1) if isinstance(n, int) else 8 * (n - t) + 16

        @block.sync
        def _(sp):
            sp.dma_start(gam[:, :], gamma.rearrange("(a b) -> a b", a=1).broadcast_to([P, 1])).then_inc(s_gam, 16)

            def load(n, t, b=None):
                dst = x2[:, n, :] if isinstance(n, int) else x2[:, bass.ds(n, 1), :].rearrange("p o d -> p (o d)")
                if isinstance(n, int):
                    src, csrc = x1v[n // 2, t], cv[n]
                else:
                    src = x1v[bass.ds(b, 1), t].rearrange("o p d -> (o p) d")
                    csrc = cv[bass.ds(n, 1)].rearrange("o p d -> (o p) d")
                sp.dma_start(dst, src).then_inc(s_xi[t], 16)
                sp.dma_start(cin[:, t, :], csrc).then_inc(s_ci[t], 16)

            def write_parts(count, t):
                sp.dma_start(sq[t].rearrange("h p d -> p h d"), qp[:, :, :].bitcast(F32)).then_inc(s_qw, 16)
                sp.wait_ge(s_klo, count)
                sp.dma_start(sk[t].rearrange("h p d -> p h d"), kp[:, :, :].bitcast(F32)).then_inc(s_kw, 16)

            def parts_written(n):
                sp.wait_ge(s_qw, 16 * n + 16)
                sp.wait_ge(s_kw, 16 * n + 16)

            def read_stacks(t, k):
                hs = slice(2 * k, 2 * k + 2)
                qv = sq[t].rearrange("h (j r) d -> h r j d", j=XPT)
                kv = sk[t].rearrange("h (j r) d -> h r j d", j=XPT)
                for c in range(PARTS):
                    rows = slice(XD * c, XD * (c + 1))
                    sp.dma_start(qst[t][rows, hs, :].bitcast(F32), qv[c // 2][:, hs]).then_inc(s_st[t][k], 16)
                    sp.dma_start(kst[t][rows, hs, :].bitcast(F32), kv[c % 2][:, hs]).then_inc(s_st[t][k], 16)

            for t in range(2):
                load(t, t)
            for t in range(2):
                sp.wait_ge(s_qlo, t + 1)
                write_parts(t + 1, t)
                parts_written(t)
                for k in range(2):
                    read_stacks(t, k)

            def item(n, t, first, more, more2):
                if more2:
                    b = None if isinstance(n, int) else sp.snap((n - t) // 2 + 1)
                    sp.wait_ge(s_vt, n + 1)
                    sp.wait_ge(s_klo, n + 1)
                    load(n + 2, t, b)
                    sp.wait_ge(s_qlo, n + 3)
                    for k in range(2):
                        sp.wait_ge(s_st[t][k], stacks(n, t))
                    write_parts(n + 3, t)
                    parts_written(n + 2)
                    for k in range(2):
                        sp.wait_ge(s_ts, 16 * n + 8 * k + 8)
                        read_stacks(t, k)

            all_tiles(sp, item, 2)

        @block.gpsimd
        def _(pool):
            def split(n, t):
                pool.wait_ge(s_ci[t], loads(n, t))
                pool.wait_ge(s_kw, 16 * n)
                pool.wait_ge(s_qhi, n + 1)
                pool.wait_ge(s_qw, 16 * n)
                nc.gpsimd.tensor_tensor(qp[:, 1, :], xn[:, :], qp[:, 0, :].bitcast(F32),
                                        ALU.subtract).then_inc(s_qlo, 1)
                nc.gpsimd.tensor_copy(kp[:, 0, :], cin[:, t, :]).then_inc(s_khi, 1)
                pool.wait_ge(s_khi, n + 1)
                nc.gpsimd.tensor_tensor(kp[:, 1, :], cin[:, t, :], kp[:, 0, :].bitcast(F32),
                                        ALU.subtract).then_inc(s_klo, 1)

            for k, (dst, value) in enumerate(((kst[0][KS:P, :, :].bitcast(F32), 1.0), (ones[:, :], 1.0),
                                              (kst[1][KS:P, :, :].bitcast(F32), 1.0),
                                              (nmp[:, :, :, :].bitcast(F32), 0.0))):
                nc.gpsimd.memset(dst, value).then_inc(s_ones, 1)
                pool.wait_ge(s_ones, k + 1)
            for t in range(2):
                split(t, t)

            def item(n, t, first, more, more2):
                if more2:
                    split(n + 2, t)

            all_tiles(pool, item)

        @block.tensor
        def _(pe):
            def early(n, h, k):
                return isinstance(n, int) and 16 * n + 4 * h + k < 2

            def scores(n, t, h, q):
                if not early(n, h, q):
                    pe.wait_ge(s_mx, 16 * n + 4 * h + q - 1)
                nc.tensor.matmul(SC[q % 2][:, :], qst[t][0:KS, h, q * P:(q + 1) * P], kst[t][0:KS, h, :],
                                 start=True, stop=True).then_inc(s_sc, 1)

            def max_rows(n, t, h):
                pe.wait_ge(s_nm, 8 * n + 2 * h + 2)
                if not (isinstance(n, int) and n == 0 and h == 0):
                    pe.wait_ge(s_row, 4 * n + h)
                for q in range(CB):
                    last = nc.tensor.matmul(MB[KS:P, q * P:(q + 1) * P], nmp[:, h % 2, q, :].bitcast(F32), ident[:, :],
                                            start=True, stop=True)
                last.then_inc(s_mr, 1)

            def transposed_scores(n, t, h, c):
                if c == 0:
                    pe.wait_ge(s_row, 4 * n + h + 1)
                if not early(n, h, c):
                    pe.wait_ge(s_exp, 16 * n + 4 * h + c - 1)
                nc.tensor.matmul(ST[c % 2][:, :], kst[t][:, h, c * P:(c + 1) * P], qst[t][:, h, :],
                                 start=True, stop=True).then_inc(s_ts, 1)

            def output(n, t, c, banks=(0, 1)):
                if c == 0 and 0 in banks:
                    pe.wait_ge(s_exp, 16 * n + 16)
                    pe.wait_ge(s_vte, n + 1)
                    pe.wait_ge(s_oe, 2 * n)
                for k in banks:
                    for h in range(XPT):
                        rows = slice(XD * h, XD * (h + 1))
                        last = nc.tensor.matmul((OB, SU)[k][rows, :], (vt[:, t, c, rows], ones[:, :])[k],
                                                prt[t][:, h, c, :], start=(c == 0), stop=(c == CB - 1))
                if c == CB - 1 and 1 in banks:
                    last.then_inc(s_pv, 1)

            def sums_by_query(n):
                pe.wait_ge(s_oe, 2 * n + 2)
                for q in range(CB):
                    last = nc.tensor.matmul(VB[:, q * XPT:(q + 1) * XPT], ssb[:, q * P:(q + 1) * P], ident[:, 0:P:XD],
                                            start=True, stop=True)
                last.then_inc(s_sq, 1)

            def inverses(n):
                pe.wait_ge(s_rr, n + 1)
                for q in range(CB):
                    last = nc.tensor.transpose(VB[:, q * P:(q + 1) * P], rrep[:, q, :], ident[:, :])
                last.then_inc(s_rt, 1)

            pe.wait_ge(s_ones, 4)
            pe.wait_ge(s_st[0][0], stacks(0, 0))
            for h in range(2):
                for q in range(CB):
                    scores(0, 0, h, q)
            max_rows(0, 0, 0)

            OUT_AT = {(0, 3): (0, 0), (1, 1): (0, 1), (1, 3): (1, 0), (2, 1): (1, 1), (2, 2): (2, 0), (2, 3): (2, 1),
                      (3, 1): (3, 0), (3, 3): (3, 1)}

            def item(n, t, first, more, more2):
                for h in range(XPT):
                    n2, h2, there2 = ahead(n, h, 2, more)
                    n1, h1, there1 = ahead(n, h, 1, more)
                    if h2 % 2 == 0 and there2:
                        t2 = t if n2 is n else 1 - t
                        pe.wait_ge(s_st[t2][h2 // 2], stacks(n2, t2))
                    for i in range(CB):
                        if there2:
                            scores(n2, t if n2 is n else 1 - t, h2, i)
                        transposed_scores(n, t, h, i)
                        if h == 0 and i == 0:
                            pe.wait_ge(s_ci[t], loads(n, t))
                            if not first:
                                pe.wait_ge(s_x2, n - 1)
                            for c in range(CB):
                                last = nc.tensor.transpose(VB[:, c * P:(c + 1) * P], cin[:, t, c * P:(c + 1) * P],
                                                           ident[:, :])
                            last.then_inc(s_vt, 1)
                        if i == 1 and there1:
                            max_rows(n1, t if n1 is n else 1 - t, h1)
                        if not first and (h, i) in OUT_AT:
                            c, k = OUT_AT[h, i]
                            output(n - 1, 1 - t, c, (k,))
                        if not first and not (isinstance(n, int) and n == 1):
                            if (h, i) == (1, 0):
                                pe.wait_ge(s_vte, n + 1)
                                sums_by_query(n - 2)
                            if (h, i) == (2, 0):
                                inverses(n - 2)

            all_tiles(pe, item)
            for c in range(CB):
                output(TILES - 1, 1, c)
            for n in (TILES - 2, TILES - 1):
                pe.wait_ge(s_vte, TILES)
                pe.wait_ge(s_x2, n + 1)
                sums_by_query(n)
                inverses(n)

        @block.scalar
        def _(act):
            rstd_of_all(nc, act, None, rstd, tmp, s_var, s_sqrt, s_step, scale=XSCALE)

            def max_row(n, t, h):
                act.wait_ge(s_mr, 4 * n + h + 1)
                nc.scalar.activation(qst[t][KS:P, h, :], MB[KS:P, :], ACT.Copy).then_inc(s_row, 1)

            def q_round(n):
                act.wait_ge(s_qn, n + 1)
                act.wait_ge(s_qw, 16 * n)
                nc.scalar.activation(qp[:, 0, :], xn[:, :], ACT.Copy).then_inc(s_qhi, 1)

            for t in range(2):
                q_round(t)
            max_row(0, 0, 0)

            def repeat(n):
                act.wait_ge(s_ri, n + 1)
                nc.scalar.activation(rrep[:, :, :].rearrange("p q (h r) -> p (q h) r", r=XD),
                                     rq[:, :].unsqueeze(2).broadcast_to([P, CB * XPT, XD]), ACT.Copy).then_inc(s_rr, 1)

            def output_evac(n):
                act.wait_ge(s_pv, n + 1)
                act.wait_ge(s_on, n)
                nc.scalar.activation(ssb[:, :], SU[:, :], ACT.Copy).then_inc(s_oe, 1)
                nc.scalar.activation(osb[:, :], OB[:, :], ACT.Copy).then_inc(s_oe, 1)

            def item(n, t, first, more, more2):
                if not first and not (isinstance(n, int) and n == 1):
                    act.wait_ge(s_pv, n - 1)
                for h in range(XPT):
                    for c in range(CB):
                        act.wait_ge(s_ts, 16 * n + 4 * h + c + 1)
                        nc.scalar.activation(prt[t][:, h, c, :], ST[c % 2][:, :], ACT.Exp).then_inc(s_exp, 1)
                        if (h, c) == (0, 1) and not first and not (isinstance(n, int) and n == 1):
                            output_evac(n - 2)
                        if (h, c) == (1, 3) and more2:
                            q_round(n + 2)
                        if (h, c) == (1, 2) and not first and not (isinstance(n, int) and n == 1):
                            repeat(n - 2)
                        if (h, c) == (0, 0):
                            act.wait_ge(s_vt, n + 1)
                            nc.scalar.activation(vt[:, t, :, :].rearrange("p c n -> p (c n)"), VB[:, :],
                                                 ACT.Copy).then_inc(s_vte, 1)
                        n1, h1, there1 = ahead(n, h, 1, more)
                        if c == 2 and there1:
                            max_row(n1, t if n1 is n else 1 - t, h1)

            all_tiles(act, item)
            for n in (TILES - 2, TILES - 1):
                output_evac(n)
                repeat(n)

        @block.vector
        def _(dve):
            nc.vector.tensor_scalar(tmp[:, 0, :], mv2[:, :, 1], EPS, None, ALU.add).then_inc(s_var, 1)
            dve.wait_ge(s_var, 1)
            rstd_of_all(nc, None, dve, rstd[:, :], tmp, s_var, s_sqrt, s_step, scale=XSCALE)
            dve.wait_ge(s_gam, 16)
            nc.vector.memset(hold[:, :], 0.0).then_inc(s_x2, 1)

            def normed(n, t):
                dve.wait_ge(s_xi[t], loads(n, t))
                dve.wait_ge(s_qlo, n)
                i = slice(n, n + 1) if isinstance(n, int) else bass.ds(n, 1)
                nc.vector.tensor_scalar(xn[:, :], col(x2, n), mv2[:, i, 0], rstd[:, i],
                                        ALU.subtract, ALU.mult).then_inc(s_qn, 1)

            def maxima(n, h, banks):
                for q in banks:
                    dve.wait_ge(s_sc, 16 * n + 4 * h + q + 1)
                    nc.vector.tensor_reduce(nmx[:, h % 2, q:q + 1], SC[q % 2][:, :], AX.X, ALU.max,
                                            negate=True).then_inc(s_mx, 1)

            def max_parts(n, h):
                dve.wait_ge(s_mx, 16 * n + 4 * h + 4)
                if not (isinstance(n, int) and n == 0 and h < 2):
                    dve.wait_ge(s_mr, 4 * n + h - 1)
                nc.vector.tensor_copy(nmp[:, h % 2, :, 0], nmx[:, h % 2, :]).then_inc(s_nm, 1)
                dve.wait_ge(s_nm, 8 * n + 2 * h + 1)
                nc.vector.tensor_tensor(nmp[:, h % 2, :, 1], nmx[:, h % 2, :], nmp[:, h % 2, :, 0].bitcast(F32),
                                        ALU.subtract).then_inc(s_nm, 1)

            def one_over_sums(n):
                dve.wait_ge(s_sq, n + 1)
                nc.vector.reciprocal(rq[:, :], VB[:, 0:CB * XPT]).then_inc(s_ri, 1)

            def output(n):
                dve.wait_ge(s_rt, n + 1)
                nc.vector.tensor_tensor(onm[:, :], osb[:, :], VB[:, :], ALU.mult).then_inc(s_on, 1)

            def residual(n):
                dve.wait_ge(s_on, n + 1)
                nc.vector.scalar_tensor_tensor(col(x2, n), onm[:, :], gam[:, 0:1], col(x2, n), ALU.mult,
                                               ALU.add).then_inc(s_x2, 1)

            def statistics(n):
                dve.wait_ge(s_x2, n + 2)
                dve.wait_ge(s_mv, n)
                nc.vector.memset(hold[:, :], 0.0)
                nc.vector.bn_stats(bn[:, :], col(x2, n)).then_inc(s_bn, 1)

            def mean_and_variance(n):
                dve.wait_ge(s_bn, 2 * n + 1)
                nc.vector.memset(hold[:, :], 0.0)
                nc.vector.bn_aggr(agg[:, :], bn[:, :]).then_inc(s_bn, 1)

            def keep_statistics(n):
                dve.wait_ge(s_bn, 2 * n + 2)
                nc.vector.tensor_copy(col(mv3, n), agg[:, :]).then_inc(s_mv, 1)

            def between(n, t, h, k, first, more2):
                work = {(1, 0): (one_over_sums,), (2, 0): (output,), (2, 1): (residual,), (3, 0): (statistics,),
                        (3, 1): (mean_and_variance, keep_statistics)}
                second = isinstance(n, int) and n == 1
                if not first and not second:
                    for do in work.get((h, k), ()):
                        do(n - 2)
                if more2 and (h, k) == (1, 1):
                    normed(n + 2, t)

            for t in range(2):
                normed(t, t)
            dve.wait_ge(s_ones, 4)
            for h in range(2):
                maxima(0, h, range(CB))
                max_parts(0, h)

            def item(n, t, first, more, more2):
                for h in range(XPT):
                    n2, h2, there2 = ahead(n, h, 2, more)
                    for k in range(2):
                        if there2:
                            maxima(n2, h2, (2 * k, 2 * k + 1))
                        if k == 1 and there2:
                            max_parts(n2, h2)
                        between(n, t, h, k, first, more2)

            all_tiles(dve, item)
            for n in (TILES - 2, TILES - 1):
                one_over_sums(n)
                for finish in (output, residual, statistics, mean_and_variance, keep_statistics):
                    finish(n)
            dve.wait_ge(s_mv, TILES)


def expert_mix(nc, router_w, router_b, expert_w, expert_b, mv3, x2, out, cst):
    ident, tri, ones = cst["ident"], cst["tri"], cst["ones"]
    ctx = ExitStack()
    with ctx:
        def sb(name, shape, dt):
            return ctx.enter_context(nc.sbuf_tensor(name, shape, dt))

        def pb(name):
            return ctx.enter_context(nc.psum_tensor(name, [P, 512], F32))

        def sem(name):
            return ctx.enter_context(nc.semaphore(name))

        TE = TILES * E
        BITS = 30
        PER = TE // 4
        z = sb("z", [P, TILES, D], F32)
        ew = sb("ew", [P, CB, D], F32)
        ewp = [sb(f"ewp{i}", [P, CB, D], F32R) for i in range(2)]
        rw = sb("rw", [P, CB, E], F32)
        rwp = [sb(f"rwp{i}", [P, CB, E], F32R) for i in range(2)]
        eb = sb("eb", [P, D], F32)
        rb = sb("rb", [P, E], F32)
        tmp = sb("rs_tmp3", [P, 2, TILES], F32)
        rstd = sb("rstd3", [P, TILES], F32)
        xn = sb("xn3", [P, 2, D], F32)
        xp = [sb(f"xp{i}", [P, 2, CB * P], F32R) for i in range(2)]
        prob = sb("prob", [P, TILES, E], F32)
        rmax = sb("rmax", [P, TILES], F32)
        rinv = sb("rinv3", [P, TILES], F32)
        bits = sb("bits", [P, 2, E], I32)
        thr = sb("thr", [P, E], I32)
        add = sb("add", [P, E], I32)
        cand = sb("cand", [P, E], I32)
        taken = sb("taken", [P, TILES, E], BF16)
        equal = sb("equal", [P, TILES, E], BF16)
        count = sb("count", [P, E], F32)
        total = sb("total", [P, TILES, E], F32)
        run = [sb(f"run{i}", [P, TILES, E], F32) for i in range(2)]
        coef = sb("coef", [P, TILES], F32)
        hold = sb("hold4", [P, 1], F32)
        held_out = sb("held_out", [P, 2], F32)
        TR = [pb(f"f_tr{i}") for i in range(2)]
        ZB = [pb(f"f_z{i}") for i in range(2)]
        LB = pb("f_l")
        CN = pb("f_cn")
        TB2 = pb("f_tb")

        s_w, s_b = sem("f_w"), sem("f_b")
        s_whi, s_wlo = sem("f_whi"), sem("f_wlo")
        s_var, s_sqrt, s_step = sem("f_var"), sem("f_sqrt"), sem("f_rstep")
        s_xn, s_tr, s_hi, s_lo = sem("f_xn"), sem("f_tr"), sem("f_hi"), sem("f_lo")
        s_keep = sem("f_keep")
        s_lg = sem("f_lg")
        s_zact = sem("f_zact")
        s_zlo = sem("f_zlo")
        s_z, s_zb = sem("f_z"), sem("f_zb")
        s_hold = sem("f_hold")
        s_soft, s_exp = sem("f_soft"), sem("f_exp")
        s_cand, s_cnt, s_srch = sem("f_cand"), sem("f_cnt"), sem("f_srch")
        s_pick, s_rank = sem("f_pick"), sem("f_rank")
        s_out, s_st = sem("f_out"), sem("f_st")
        block = ctx.enter_context(nc.Block())
        ov = out.rearrange("b (t p) d -> b p t d", p=P)

        def col(ap, n):
            return ap[:, bass.ds(n, 1), :].rearrange("p o d -> p (o d)")

        def flat(ap):
            return ap.rearrange("p a b -> p (a b)")

        @block.sync
        def _(sp):
            sp.dma_start(ew[:, :, :], expert_w.rearrange("(c p) n -> p c n", p=P)).then_inc(s_w, 16)
            sp.dma_start(rw[:, :, :], router_w.rearrange("(c p) n -> p c n", p=P)).then_inc(s_w, 16)
            sp.dma_start(eb[:, :], expert_b.rearrange("(a n) -> a n", a=1).broadcast_to([P, D])).then_inc(s_b, 16)
            sp.dma_start(rb[:, :], router_b.rearrange("(a n) -> a n", a=1).broadcast_to([P, E])).then_inc(s_b, 16)
            def turn(b):
                sp.wait_ge(s_out, 2 * b + 2)
                sp.dma_start(ov[bass.ds(b, 1)].rearrange("o p t d -> (o p) t d"),
                             z[:, bass.ds(2 * b, 2), :]).then_inc(s_st, 16)

            turns(sp, B, turn)
            sp.wait_ge(s_st, 16 * B)

        def lookahead(eng, first, step):
            for t in range(2):
                first(t)
            for t in range(2):
                step(t, t, True)
            with eng.Fori(1, TILES // 2 - 1) as i:
                for t in range(2):
                    step(2 * i + t, t, True)
            for t in range(2):
                step(TILES - 2 + t, t, False)

        def at(n):
            return slice(n, n + 1) if isinstance(n, int) else bass.ds(n, 1)

        @block.tensor
        def _(pe):
            pe.wait_ge(s_wlo, 2)

            def product(out_bank, t, w):
                k = 0
                for c in range(CB):
                    for a, b in ((0, 0), (0, 1), (1, 0)):
                        last = nc.tensor.matmul(out_bank, xp[t][:, a, c * P:(c + 1) * P], w[b][:, c, :],
                                                start=(k == 0), stop=(k == 3 * CB - 1))
                        k += 1
                return last

            def transposes(n, t):
                pe.wait_ge(s_xn, n + 1)
                if not (isinstance(n, int) and n < 2):
                    pe.wait_ge(s_lo, n - 1)
                    pe.wait_ge(s_keep, n - 1)
                for c in range(CB):
                    last = nc.tensor.transpose(TR[t][:, c * P:(c + 1) * P], xn[:, t, c * P:(c + 1) * P], ident[:, :])
                last.then_inc(s_tr, 1)

            def logits(n, t, more2):
                pe.wait_ge(s_lo, n + 1)
                product(LB[:, bass.ds(n * E, E)], t, rwp).then_inc(s_lg, 1)
                if more2:
                    transposes(n + 2, t)

            lookahead(pe, lambda t: transposes(t, t), logits)

            def count_taken():
                for i in range(4):
                    last = nc.tensor.matmul(CN[:, 0:PER], ones[:, :], flat(taken[:, i * (TILES // 4):(i + 1) * (TILES // 4), :]),
                                            start=(i == 0), stop=(i == 3))
                last.then_inc(s_cnt, 1)

            def expert(n, t):
                pe.wait_ge(s_zlo, 2 * n + 2)
                product(ZB[t][:, :], t, ewp).then_inc(s_z, 1)

            def rounds(i):
                for t in range(2):
                    expert(2 * i + t, t)
                    pe.wait_ge(s_cand, 2 * i + t + 1)
                    count_taken()

            turns(pe, BITS // 2, rounds)
            for n in range(BITS, TILES):
                expert(n, n % 2)
            pe.wait_ge(s_pick, 2)
            count_taken()
            nc.tensor.matmul(TR[0][:, :], tri[:, :], flat(equal[:, :, :]), start=True, stop=True)
            nc.tensor.matmul(TB2[:, :], ones[:, :], flat(equal[:, :, :]), start=True, stop=True).then_inc(s_rank, 1)

        @block.scalar
        def _(act):
            act.wait_ge(s_w, 32)
            nc.scalar.activation(flat(ewp[0][:, :, :]), flat(ew[:, :, :]), ACT.Copy).then_inc(s_whi, 1)
            nc.scalar.activation(flat(rwp[0][:, :, :]), flat(rw[:, :, :]), ACT.Copy).then_inc(s_whi, 1)
            rstd_of_all(nc, act, None, rstd, tmp, s_var, s_sqrt, s_step)

            def split(n, t, more2):
                act.wait_ge(s_tr, n + 1)
                if not (isinstance(n, int) and n < 2):
                    act.wait_ge(s_lg, n - 1)
                nc.scalar.activation(xp[t][:, 0, :], TR[t][:, :], ACT.Copy).then_inc(s_hi, 1)
                act.wait_ge(s_lo, n + 1)
                nc.scalar.activation(z[:, at(n), :].rearrange("p o d -> p (o d)"), TR[t][:, :],
                                     ACT.Copy).then_inc(s_keep, 1)

            lookahead(act, lambda t: None, split)
            act.wait_ge(s_soft, 3)
            nc.scalar.activation(flat(prob[:, :, :]), flat(prob[:, :, :]), ACT.Exp).then_inc(s_exp, 1)
            act.wait_ge(s_keep, TILES)

            def z_round(n, t):
                nc.scalar.activation(xp[t][:, 0, :], z[:, at(n), :].rearrange("p o d -> p (o d)"),
                                     ACT.Copy).then_inc(s_zact, 1)

            def z_keep(n, t, more2):
                act.wait_ge(s_z, n + 1)
                nc.scalar.activation(z[:, at(n), :].rearrange("p o d -> p (o d)"), ZB[t][:, :],
                                     ACT.Copy).then_inc(s_zact, 1)
                if more2:
                    z_round(n + 2, t)

            act.wait_ge(s_lg, TILES)
            lookahead(act, lambda t: z_round(t, t), z_keep)

        @block.gpsimd
        def _(pool):
            nc.gpsimd.memset(hold[:, :], 0.0).then_inc(s_hold, 1)
            pool.wait_ge(s_hold, 1)

            def z_rest(n, t, acts):
                pool.wait_ge(s_zact, acts)
                nc.gpsimd.tensor_tensor(held_out[:, t:t + 1], hold[:, :], hold[:, :], ALU.add).then_inc(s_zlo, 1)
                nc.gpsimd.tensor_tensor(xp[t][:, 1, :], z[:, at(n), :].rearrange("p o d -> p (o d)"),
                                        xp[t][:, 0, :].bitcast(F32), ALU.subtract).then_inc(s_zlo, 1)

            def z_bias(n, t, more2):
                if more2:
                    z_rest(n + 2, t, 2 * n + 4)
                else:
                    pool.wait_ge(s_zact, TILES + n + 1)
                zn = z[:, at(n), :].rearrange("p o d -> p (o d)")
                nc.gpsimd.tensor_tensor(zn, zn, eb[:, :], ALU.add).then_inc(s_zb, 1)

            pool.wait_ge(s_b, 32)
            lookahead(pool, lambda t: z_rest(t, t, t + 1), z_bias)

        @block.vector
        def _(dve):
            dve.wait_ge(s_whi, 2)
            nc.vector.tensor_tensor(flat(ewp[1][:, :, :]), flat(ew[:, :, :]), flat(ewp[0][:, :, :]).bitcast(F32),
                                    ALU.subtract).then_inc(s_wlo, 1)
            nc.vector.tensor_tensor(flat(rwp[1][:, :, :]), flat(rw[:, :, :]), flat(rwp[0][:, :, :]).bitcast(F32),
                                    ALU.subtract).then_inc(s_wlo, 1)
            nc.vector.tensor_scalar(tmp[:, 0, :], mv3[:, :, 1], EPS, None, ALU.add).then_inc(s_var, 1)
            dve.wait_ge(s_var, 1)
            rstd_of_all(nc, None, dve, rstd[:, :], tmp, s_var, s_sqrt, s_step)
            dve.wait_ge(s_b, 32)

            def normed(n, t):
                if not (isinstance(n, int) and n < 2):
                    dve.wait_ge(s_tr, n - 1)
                nc.vector.tensor_scalar(xn[:, t, :], x2[:, at(n), :].rearrange("p o d -> p (o d)"), mv3[:, at(n), 0],
                                        rstd[:, at(n)], ALU.subtract, ALU.mult).then_inc(s_xn, 1)

            def rest(n, t, more2):
                if more2:
                    normed(n + 2, t)
                dve.wait_ge(s_hi, n + 1)
                nc.vector.tensor_tensor(xp[t][:, 1, :], TR[t][:, :], xp[t][:, 0, :].bitcast(F32),
                                        ALU.subtract).then_inc(s_lo, 1)

            lookahead(dve, lambda t: normed(t, t), rest)

            def by_tile(ap):
                return ap.unsqueeze(2).broadcast_to([P, TILES, E])

            dve.wait_ge(s_lg, TILES)
            nc.vector.tensor_tensor(prob[:, :, :], LB[:, :].rearrange("p (t e) -> p t e", e=E),
                                    rb[:, :].unsqueeze(1).broadcast_to([P, TILES, E]), ALU.add).then_inc(s_soft, 1)
            dve.wait_ge(s_soft, 1)
            nc.vector.reduce_max(rmax[:, :], prob[:, :, :], AX.X).then_inc(s_soft, 1)
            dve.wait_ge(s_soft, 2)
            nc.vector.tensor_tensor(prob[:, :, :], prob[:, :, :], by_tile(rmax[:, :]), ALU.subtract).then_inc(s_soft, 1)
            nc.vector.memset(thr[:, :], 0).then_inc(s_soft, 1)
            nc.vector.memset(bits[:, 0, :], 1 << 29).then_inc(s_soft, 1)
            nc.vector.memset(cand[:, :], 1 << 29).then_inc(s_soft, 1)
            dve.wait_ge(s_exp, 1)
            nc.vector.reduce_sum(rmax[:, :], prob[:, :, :], AX.X).then_inc(s_soft, 1)
            dve.wait_ge(s_soft, 7)
            nc.vector.reciprocal(rinv[:, :], rmax[:, :]).then_inc(s_soft, 1)
            dve.wait_ge(s_soft, 8)
            nc.vector.tensor_tensor(prob[:, :, :], prob[:, :, :], by_tile(rinv[:, :]), ALU.mult).then_inc(s_soft, 1)
            dve.wait_ge(s_soft, 9)

            def by_expert(ap):
                return ap.unsqueeze(1).broadcast_to([P, TILES, E])

            STEPS = 5

            def counted(c):
                dve.wait_ge(s_cnt, c)
                return nc.vector.reduce_sum(count[:, :], CN[:, 0:PER].rearrange("p (t e) -> p e t", e=E), AX.X)

            with dve.Fori(0, BITS // 2) as i:
                for k in range(2):
                    r = 2 * i + k
                    nc.vector.tensor_tensor(taken[:, :, :], prob[:, :, :], by_expert(cand[:, :].bitcast(F32)),
                                            ALU.is_ge).then_inc(s_cand, 1)
                    nc.vector.tensor_scalar(bits[:, 1 - k, :], bits[:, k, :], 1, None,
                                            ALU.logical_shift_right).then_inc(s_srch, 1)
                    counted(r + 1).then_inc(s_srch, 1)
                    dve.wait_ge(s_srch, STEPS * r + 2)
                    nc.vector.scalar_tensor_tensor(add[:, :], count[:, :], float(TOPK), bits[:, k, :], ALU.is_ge,
                                                   ALU.mult).then_inc(s_srch, 1)
                    dve.wait_ge(s_srch, STEPS * r + 3)
                    nc.vector.tensor_tensor(thr[:, :], thr[:, :], add[:, :], ALU.bitwise_or).then_inc(s_srch, 1)
                    dve.wait_ge(s_srch, STEPS * r + 4)
                    nc.vector.tensor_tensor(cand[:, :], thr[:, :], bits[:, 1 - k, :], ALU.bitwise_or).then_inc(s_srch, 1)
                    dve.wait_ge(s_srch, STEPS * r + 5)

            t_f = by_expert(thr[:, :].bitcast(F32))
            nc.vector.tensor_tensor(taken[:, :, :], prob[:, :, :], t_f, ALU.is_gt).then_inc(s_pick, 1)
            nc.vector.tensor_tensor(equal[:, :, :], prob[:, :, :], t_f, ALU.is_equal).then_inc(s_pick, 1)
            steps = [2]

            def step(ins):
                steps[0] += 1
                ins.then_inc(s_pick, 1)
                dve.wait_ge(s_pick, steps[0])

            step(counted(BITS + 1))
            step(nc.vector.tensor_scalar(count[:, :], count[:, :], -1.0, float(TOPK), ALU.mult, ALU.add))
            dve.wait_ge(s_rank, 1)
            step(nc.vector.tensor_copy(flat(total[:, :, :]), TB2[:, :]))
            step(nc.vector.tensor_copy(flat(run[0][:, :, :]), TB2[:, :]))
            a, shift = 0, 1
            while shift < TILES:
                src, dst = run[a], run[1 - a]
                step(nc.vector.tensor_copy(dst[:, 0:shift, :], src[:, 0:shift, :]))
                step(nc.vector.tensor_tensor(dst[:, shift:TILES, :], src[:, shift:TILES, :],
                                             src[:, 0:TILES - shift, :], ALU.add))
                a, shift = 1 - a, 2 * shift
            rank = run[a]
            step(nc.vector.tensor_tensor(rank[:, :, :], rank[:, :, :], total[:, :, :], ALU.subtract))
            step(nc.vector.tensor_tensor(flat(rank[:, :, :]), TR[0][:, :], flat(rank[:, :, :]), ALU.add))
            step(nc.vector.tensor_tensor(rank[:, :, :], rank[:, :, :], by_expert(count[:, :]), ALU.is_le))
            step(nc.vector.tensor_tensor(rank[:, :, :], rank[:, :, :], equal[:, :, :], ALU.mult))
            step(nc.vector.tensor_tensor(rank[:, :, :], rank[:, :, :], taken[:, :, :], ALU.add))
            step(nc.vector.tensor_tensor(rank[:, :, :], rank[:, :, :], prob[:, :, :], ALU.mult))
            step(nc.vector.reduce_sum(coef[:, :], rank[:, :, :], AX.X))
            dve.wait_ge(s_zb, TILES)
            with dve.Fori(0, TILES) as n:
                nc.vector.scalar_tensor_tensor(col(z, n), col(z, n), coef[:, bass.ds(n, 1)], col(x2, n), ALU.mult,
                                               ALU.add).then_inc(s_out, 1)


def decoder_layer(nc, x, ctx_in, w_all, gamma, router_w, router_b, expert_w, expert_b, rope, out):
    xt = nc.dram_tensor("xt_scratch", [B, P, 2, CB, L], F32).ap()
    x1 = nc.dram_tensor("x1_scratch", [B, P, TB, D], F32).ap()
    sq = nc.dram_tensor("sq_scratch", [2, 2, P, D], F32).ap()
    sk = nc.dram_tensor("sk_scratch", [2, 2, P, D], F32).ap()
    ctx = ExitStack()
    with ctx:
        def sb(name, shape, dt):
            return ctx.enter_context(nc.sbuf_tensor(name, shape, dt))

        cst = dict(ident=sb("ident", [P, P], F32), identb=sb("identb", [P, P], BF16), mask=sb("mask", [P, P], BF16),
                   ones=sb("ones", [P, P], BF16), tri=sb("tri", [P, P], BF16))
        mv2 = sb("mv2", [P, TILES, 2], F32)
        mv3 = sb("mv3", [P, TILES, 2], F32)
        with ExitStack() as weights:
            def wb(name, shape, dt):
                return weights.enter_context(nc.sbuf_tensor(name, shape, dt))

            def sem(name):
                return weights.enter_context(nc.semaphore(name))

            wts = dict(hi=wb("whi0", [P, NCH, 512], F32R), lo=wb("wlo0", [P, NCH, 512], F32R),
                       raw=wb("wraw", [P, 2, 512], F32), s_raw=[sem(f"w_raw{i}") for i in range(2)],
                       s_hi=sem("w_hi"), s_lo=sem("w_lo"))
            layer_norm_1(nc, x, w_all, xt, cst, wts)
            self_attention(nc, x, w_all, rope, xt, x1, mv2, cst, wts)
        x2 = sb("x2", [P, TILES, D], F32)
        cross_attention(nc, x1, ctx_in, gamma, sq, sk, mv2, mv3, x2, cst)
        expert_mix(nc, router_w, router_b, expert_w, expert_b, mv3, x2, out, cst)


def rope_table():
    inv = (1.0 / np.power(np.float32(10000.0), np.arange(0, HD, 2, dtype=np.float32) / np.float32(HD))).astype(np.float32)
    ang = (np.arange(L, dtype=np.float32)[:, None] * inv[None, :]).astype(np.float64)
    cos, sin = np.cos(ang), np.sin(ang)
    table = np.stack([cos, -sin, sin], 1).astype(np.float32)
    return np.ascontiguousarray(table.reshape(TB, P, 3, HD // 2).transpose(1, 0, 2, 3))


def kernel(**inputs):
    import numpy as _np
    import concourse.bacc as _bacc
    from concourse import mybir as _mybir
    from concourse.bass_utils import run_bass_kernel_spmd as _run

    nc = _bacc.Bacc("TRN2", target_bir_lowering=False, num_devices=1)
    wq, wk, wv, wo = (_np.asarray(inputs[f"L0_attn_w{k}"]) for k in "qkvo")
    proj = [w.reshape(CB, P, G, GW).transpose(2, 0, 1, 3) for w in (wq, wk, wv)]
    w_all = _np.ascontiguousarray(_np.concatenate(proj + [wo.reshape(G, HG, P, D)], axis=1))
    feeds = {
        "x": inputs["x"], "ctx_in": inputs["ctx_2048"], "w_all": w_all,
        "gamma": _np.asarray(inputs["L0_xattn_gamma"]).reshape(1), "router_w": inputs["L0_ffn_router_w"],
        "router_b": inputs["L0_ffn_router_b"], "expert_w": inputs["L0_ffn_expert_w"],
        "expert_b": inputs["L0_ffn_expert_b"], "rope": rope_table(),
    }
    arrays, args = {}, {}
    for name, a in feeds.items():
        a = _np.ascontiguousarray(a)
        arrays[f"in_{name}_dram"] = a
        args[name] = nc.dram_tensor(f"in_{name}_dram", a.shape, _mybir.dt.from_np(a.dtype), kind="ExternalInput").ap()
    out = nc.dram_tensor("out_0_dram", (B, L, D), _mybir.dt.float32, kind="ExternalOutput").ap()
    decoder_layer(nc, out=out, **args)
    r = _run(nc, [arrays], core_ids=[0])
    return r.results[0]["out_0_dram"]
```
